# Optimizing a Trainium2 kernel written in Bass

```python
import numpy as np
import jax
import jax.numpy as jnp

def _softmax(x, axis=-1):
    return jax.nn.softmax(x, axis=axis)

def _gelu(x):
    return jax.nn.gelu(x, approximate=True)

def _silu(x):
    return jax.nn.silu(x)

def _sigmoid(x):
    return jax.nn.sigmoid(x)

def _layernorm(x, axis=-1, eps=1e-05):
    m = jnp.mean(x, axis=axis, keepdims=True)
    v = jnp.var(x, axis=axis, keepdims=True)
    return (x - m) / jnp.sqrt(v + eps)

def _scatter_add(tgt, idx, src, axis=0):
    return tgt.at[idx].add(src)

def _segment_sum(src, seg, n):
    return jax.ops.segment_sum(src, seg, n)
kernel_name = 'mk_seq_preln_d2_jaxref_r8_08bd29'

def setup_inputs(seed: int=0):
    np.random.seed(seed)
    _w = jnp.asarray

    def _L0_attn_setup():
        import jax, jax.numpy as jnp
        import numpy as np
        B, N, C, H = (8, 128, 128, 16)

        def _masked_softmax(dots, allow):
            neg = jnp.finfo(dots.dtype).min
            logits = jnp.where(allow, dots, neg)
            rowmax = jnp.max(logits, axis=-1, keepdims=True)
            unnorm = jnp.where(allow, jnp.exp(logits - rowmax), 0.0)
            denom = jnp.sum(unnorm, axis=-1, keepdims=True)
            return unnorm / jnp.where(denom == 0, 1.0, denom)
        key = jax.random.key(seed)
        k1, k2, k3 = jax.random.split(key, 3)
        x = jax.random.normal(k1, (B, N, C), dtype=jnp.float32)
        w_qkv = jax.random.normal(k2, (C, 3 * C), dtype=jnp.float32) * (1.0 / np.sqrt(C))
        scale = jnp.ones((H, 1, 1), dtype=jnp.float32)
        w_out = jax.random.normal(k3, (C, C), dtype=jnp.float32) * (1.0 / np.sqrt(C))
        b_out = jnp.zeros((C,), dtype=jnp.float32)
        return {'x': x, 'w_qkv': w_qkv, 'scale': scale, 'w_out': w_out, 'b_out': b_out}
    _L0_attn_in = _L0_attn_setup()

    def _L0_ffn_setup():
        import jax, jax.numpy as jnp
        import numpy as np
        E = 16
        K = 4
        B, S, H, I = (4, 128, 128, 256)
        key = jax.random.key(seed)
        k0, k1, k2, k3 = jax.random.split(key, 4)
        scale = 0.02
        return {'hidden_states': jax.random.normal(k0, (B, S, H), jnp.float32), 'router_w': jax.random.normal(k1, (H, E), jnp.float32) * scale, 'router_b': jnp.zeros((E,), jnp.float32), 'w1': jax.random.normal(k2, (E, H, I), jnp.float32) * scale, 'b1': jnp.zeros((E, I), jnp.float32), 'w2': jax.random.normal(k3, (E, I, H), jnp.float32) * scale, 'b2': jnp.zeros((E, H), jnp.float32)}
    _L0_ffn_in = _L0_ffn_setup()

    def _L1_attn_setup():
        import jax, jax.numpy as jnp
        import numpy as np
        import math
        N_HEAD = 16
        HEAD_DIM = 64
        N_EMBD = 128
        MIN_CTX = 32
        FULL_CTX = 128

        def _pruning_ratio(T):
            if T < MIN_CTX:
                return 1.0
            if T >= FULL_CTX:
                return 0.2
            progress = (T - MIN_CTX) / (FULL_CTX - MIN_CTX)
            return 0.5 - 0.3 * progress
        key = jax.random.key(seed)
        k1, k2, k3, k4, k5 = jax.random.split(key, 5)
        B, T = (1, 256)
        x = jax.random.normal(k1, (B, T, N_EMBD), dtype=jnp.float32)
        W_attn = jax.random.normal(k2, (3 * N_HEAD * HEAD_DIM, N_EMBD), dtype=jnp.float32) * 0.02
        b_attn = jnp.zeros((3 * N_HEAD * HEAD_DIM,), dtype=jnp.float32)
        W_proj = jax.random.normal(k3, (N_EMBD, N_HEAD * HEAD_DIM), dtype=jnp.float32) * 0.02
        b_proj = jnp.zeros((N_EMBD,), dtype=jnp.float32)
        return {'x': x, 'W_attn': W_attn, 'b_attn': b_attn, 'W_proj': W_proj, 'b_proj': b_proj}
    _L1_attn_in = _L1_attn_setup()

    def _L1_ffn_setup():
        import jax, jax.numpy as jnp
        import numpy as np
        B, S, H, F, E = (2, 256, 128, 512, 8)
        key = jax.random.key(seed)
        ks = jax.random.split(key, 4)
        x = jax.random.normal(ks[0], (B, S, H), dtype=jnp.float32)
        w_router = jax.random.normal(ks[1], (H, E), dtype=jnp.float32) * 0.02
        w1 = jax.random.normal(ks[2], (E, H, F), dtype=jnp.float32) * 0.02
        b1 = jnp.zeros((E, F), dtype=jnp.float32)
        w2 = jax.random.normal(ks[3], (E, F, H), dtype=jnp.float32) * 0.02
        b2 = jnp.zeros((E, H), dtype=jnp.float32)
        return {'x': x, 'w_router': w_router, 'w1': w1, 'b1': b1, 'w2': w2, 'b2': b2}
    _L1_ffn_in = _L1_ffn_setup()
    _d = {'L0_attn_x': _L0_attn_in['x'], 'L0_attn_w_qkv': _L0_attn_in['w_qkv'], 'L0_attn_scale': _L0_attn_in['scale'], 'L0_attn_w_out': _L0_attn_in['w_out'], 'L0_attn_b_out': _L0_attn_in['b_out'], 'L0_ffn_router_w': _L0_ffn_in['router_w'], 'L0_ffn_router_b': _L0_ffn_in['router_b'], 'L0_ffn_w1': _L0_ffn_in['w1'], 'L0_ffn_b1': _L0_ffn_in['b1'], 'L0_ffn_w2': _L0_ffn_in['w2'], 'L0_ffn_b2': _L0_ffn_in['b2'], 'L1_attn_W_attn': _L1_attn_in['W_attn'], 'L1_attn_b_attn': _L1_attn_in['b_attn'], 'L1_attn_W_proj': _L1_attn_in['W_proj'], 'L1_attn_b_proj': _L1_attn_in['b_proj'], 'L1_ffn_w_router': _L1_ffn_in['w_router'], 'L1_ffn_w1': _L1_ffn_in['w1'], 'L1_ffn_b1': _L1_ffn_in['b1'], 'L1_ffn_w2': _L1_ffn_in['w2'], 'L1_ffn_b2': _L1_ffn_in['b2']}
    _x0 = _d['L0_attn_x']
    _d['L0_attn_x'] = jax.random.normal(jax.random.fold_in(jax.random.key(seed), 1), (4, 512, 128), dtype=_x0.dtype)
    del _x0
    return _d

def reference(L0_attn_x, L0_attn_w_qkv, L0_attn_scale, L0_attn_w_out, L0_attn_b_out, L0_ffn_router_w, L0_ffn_router_b, L0_ffn_w1, L0_ffn_b1, L0_ffn_w2, L0_ffn_b2, L1_attn_W_attn, L1_attn_b_attn, L1_attn_W_proj, L1_attn_b_proj, L1_ffn_w_router, L1_ffn_w1, L1_ffn_b1, L1_ffn_w2, L1_ffn_b2):

    def _L0_attn_ref(x, w_qkv, scale, w_out, b_out):
        import jax, jax.numpy as jnp
        import numpy as np
        B, N, C, H = (8, 128, 128, 16)

        def _masked_softmax(dots, allow):
            neg = jnp.finfo(dots.dtype).min
            logits = jnp.where(allow, dots, neg)
            rowmax = jnp.max(logits, axis=-1, keepdims=True)
            unnorm = jnp.where(allow, jnp.exp(logits - rowmax), 0.0)
            denom = jnp.sum(unnorm, axis=-1, keepdims=True)
            return unnorm / jnp.where(denom == 0, 1.0, denom)
        b, n, c = x.shape
        h = scale.shape[0]
        d = c // h
        qkv = x @ w_qkv
        q, k, v = jnp.split(qkv, 3, axis=-1)

        def heads(t):
            return t.reshape(b, n, h, d).transpose(0, 2, 1, 3)
        q, k, v = (heads(q), heads(k), heads(v))
        dots = jnp.einsum('bhnd,bhmd->bhnm', q, k) * scale
        allow = jnp.tril(jnp.ones((n, n), dtype=bool), k=-1)
        attn = _masked_softmax(dots, allow)
        out = jnp.einsum('bhnm,bhmd->bhnd', attn, v)
        out = out.transpose(0, 2, 1, 3).reshape(b, n, c)
        return out @ w_out + b_out

    def _L0_ffn_ref(hidden_states, router_w, router_b, w1, b1, w2, b2):
        import jax, jax.numpy as jnp
        import numpy as np
        E = 16
        K = 4
        B, S, H, I = (4, 128, 128, 256)
        b, s, h = hidden_states.shape
        logits = hidden_states @ router_w + router_b
        probs = jax.nn.softmax(logits, axis=-1)
        topw, topi = jax.lax.top_k(probs, K)
        topw = topw / jnp.sum(topw, axis=-1, keepdims=True)
        combine = jnp.sum(jax.nn.one_hot(topi, E, dtype=hidden_states.dtype) * topw[..., None], axis=2)
        x = hidden_states.reshape(b * s, h)
        c = combine.reshape(b * s, E)

        def body(acc, expert):
            w1e, b1e, w2e, b2e, ce = expert
            hmid = jax.nn.gelu(x @ w1e + b1e, approximate=False)
            return (acc + (hmid @ w2e + b2e) * ce[:, None], None)
        out, _ = jax.lax.scan(body, jnp.zeros_like(x), (w1, b1, w2, b2, c.T))
        return out.reshape(b, s, h)

    def _L1_attn_ref(x, W_attn, b_attn, W_proj, b_proj):
        import jax, jax.numpy as jnp
        import numpy as np
        import math
        N_HEAD = 16
        HEAD_DIM = 64
        N_EMBD = 128
        MIN_CTX = 32
        FULL_CTX = 128

        def _pruning_ratio(T):
            if T < MIN_CTX:
                return 1.0
            if T >= FULL_CTX:
                return 0.2
            progress = (T - MIN_CTX) / (FULL_CTX - MIN_CTX)
            return 0.5 - 0.3 * progress
        B, T, C = x.shape
        H, hd = (N_HEAD, HEAD_DIM)
        qkv = x @ W_attn.T + b_attn
        q, k, v = jnp.split(qkv, 3, axis=-1)
        q = q.reshape(B, T, H, hd).transpose(0, 2, 1, 3)
        k = k.reshape(B, T, H, hd).transpose(0, 2, 1, 3)
        v = v.reshape(B, T, H, hd).transpose(0, 2, 1, 3)
        att = jnp.einsum('bhqd,bhkd->bhqk', q, k) * (1.0 / math.sqrt(hd))
        i = jnp.arange(T)
        causal = i[None, :] <= i[:, None]
        neg_inf = jnp.float32(-jnp.inf)
        att = jnp.where(causal[None, None], att, neg_inf)
        S = jnp.maximum(att[:, 0], 0.0)
        keepS = (i[None, :] != 0) & (i[:, None] != i[None, :])
        S = jnp.where(keepS[None], S, 0.0)
        S_shifted = jnp.roll(S, 1, axis=-2).at[:, 0, :].set(0.0)
        FF = jnp.cumsum(S_shifted, axis=-2)
        att = att - FF[:, None]
        ratio = _pruning_ratio(T)
        memory_budget = max(1, int(T * ratio))
        if ratio < 1.0:
            FF_mod = jnp.where(causal[None], FF, jnp.inf)
            sorted_idx = jnp.argsort(FF_mod, axis=-1)
            eff_k = jnp.minimum(memory_budget - 1, i + 1)
            sel = i[None, :] < eff_k[:, None]
            keep = jnp.zeros((B, T, T), dtype=bool)
            keep = keep.at[jnp.arange(B)[:, None, None], i[None, :, None], sorted_idx].set(jnp.broadcast_to(sel[None], (B, T, T)))
            keep = keep | jnp.eye(T, dtype=bool)[None]
            att = jnp.where(keep[:, None], att, neg_inf)
        y = jax.nn.softmax(att, axis=-1) @ v
        y = y.transpose(0, 2, 1, 3).reshape(B, T, H * hd)
        y = y @ W_proj.T + b_proj
        return y

    def _L1_ffn_ref(x, w_router, w1, b1, w2, b2):
        import jax, jax.numpy as jnp
        import numpy as np
        B, S, H, F, E = (2, 256, 128, 512, 8)
        'Top-1 MoE layer: route -> per-expert FFN -> weighted combine.\n\n            Faithful to ExpertParallelWrapper._process_moe_layer on a single group:\n            router picks one expert per token with a routing weight; tokens are\n            dispatched to experts (here expressed as a static mask over the fixed\n            expert set), processed by the expert FFN, and scatter-combined back\n            weighted by the routing probability.\n            '
        Bs, Ss, Hs = x.shape
        n_experts = w1.shape[0]
        logits = jnp.einsum('bsh,he->bse', x, w_router)
        probs = jax.nn.softmax(logits, axis=-1)
        sel = jnp.argmax(probs, axis=-1)
        wgt = jnp.take_along_axis(probs, sel[..., None], axis=-1)[..., 0]
        xt = x.reshape(-1, Hs)
        sel_t = sel.reshape(-1)
        wgt_t = wgt.reshape(-1)
        out = jnp.zeros_like(xt)
        for e in range(n_experts):
            h = jax.nn.relu(xt @ w1[e] + b1[e])
            y = h @ w2[e] + b2[e]
            m = (sel_t == e).astype(xt.dtype) * wgt_t
            out = out + m[:, None] * y
        return out.reshape(Bs, Ss, Hs)
    x = L0_attn_x
    x = x + _L0_attn_ref(_layernorm(x, axis=-1), L0_attn_w_qkv, L0_attn_scale, L0_attn_w_out, L0_attn_b_out)
    x = x + _L0_ffn_ref(_layernorm(x, axis=-1), L0_ffn_router_w, L0_ffn_router_b, L0_ffn_w1, L0_ffn_b1, L0_ffn_w2, L0_ffn_b2)
    x = x + _L1_attn_ref(_layernorm(x, axis=-1), L1_attn_W_attn, L1_attn_b_attn, L1_attn_W_proj, L1_attn_b_proj)
    x = x + _L1_ffn_ref(_layernorm(x, axis=-1), L1_ffn_w_router, L1_ffn_w1, L1_ffn_b1, L1_ffn_w2, L1_ffn_b2)
    return x

_drawn_inputs = setup_inputs


def setup_inputs(seed=0):
    import zlib

    import numpy as np

    out = dict(_drawn_inputs(seed))
    spreads = {'L0_attn_scale': (1.0, 0.2),
     'L0_attn_b_out': (0.0, 0.1),
     'L0_ffn_router_b': (0.0, 0.1),
     'L0_ffn_b1': (0.0, 0.8),
     'L0_ffn_b2': (0.0, 0.1),
     'L1_attn_b_attn': (0.0, 0.1),
     'L1_attn_b_proj': (0.0, 0.1),
     'L1_ffn_b1': (0.0, 0.8),
     'L1_ffn_b2': (0.0, 0.5)}
    factors = {'L0_ffn_w1': 3.32,
     'L0_ffn_w2': 2.99,
     'L1_ffn_w_router': 2.951,
     'L1_ffn_w1': 5.994,
     'L1_ffn_w2': 4.659}
    for name, (base, spread) in spreads.items():
        noise = np.random.default_rng([zlib.crc32(name.encode()), seed]).standard_normal(out[name].shape)
        drawn = base * np.exp(spread * noise) if base else spread * noise
        out[name] = jnp.asarray(drawn.astype(out[name].dtype))
    for name, factor in factors.items():
        out[name] = (out[name] * factor).astype(out[name].dtype)
    return out
```

```python
import math
from contextlib import ExitStack

import numpy as np

import concourse.bass as bass
from concourse import mybir

F32 = mybir.dt.float32
F32R = mybir.dt.float32r
ALU = mybir.AluOpType
ACT = mybir.ActivationFunctionType
AX = mybir.AxisListType

P = 128
EPS = 1e-5
MASKED = 1e37
FLOOR = 1e36
TAKEN = -3e38
SENTINEL = 1e37


NCONST = 15


def apart(eng, passed):
    eng.sem_inc(passed, 1)


def need(eng, sem, value):
    if isinstance(value, int) and value <= 0:
        return
    eng.wait_ge(sem, value)


class Steps:

    def __init__(self, eng, sem, it, per, before=0, per_trip=None):
        self.eng, self.sem, self.per, self.n = eng, sem, per, 0
        self.base = it * (per if per_trip is None else per_trip) + before

    def inc(self, ins):
        ins.then_inc(self.sem, 1)
        self.n += 1

    def wait(self, n=None):
        self.eng.wait_ge(self.sem, self.base + (self.n if n is None else n))

    def close(self):
        assert self.n == self.per, (self.n, self.per)


def build(nc, a, out):
    B, N, C = a["x"].shape
    NT = N // P
    T = B * NT
    H = 16
    D1 = a["wv1"].shape[1] // H
    TOT = P * NT * (NT + 1) // 2
    OFF = [P * i * (i + 1) // 2 for i in range(NT)]
    SLOTS = H * NT
    E0, _, I0 = a["w1_0"].shape
    E1, _, I1 = a["w1_1"].shape

    with ExitStack() as ctx:
        def sb(name, shape, dt=F32):
            return ctx.enter_context(nc.sbuf_tensor(name, shape, dt))

        def sem(name):
            return ctx.enter_context(nc.semaphore(name))

        x_tok = sb("x_tok", [P, T, C])
        ident = sb("ident", [P, P])
        strict = sb("strict", [P, P])
        ones = sb("ones", [P, P])
        notdiag = sb("notdiag", [P, P])
        pen0 = sb("pen0", [P, N])
        rneg = sb("rneg", [P, N])
        causal = sb("causal", [P, N])
        headrow = sb("headrow", [P, 4])
        scale0 = sb("scale0", [P, 4])
        scale_in = sb("scale_in", [P, 4])
        bo0 = sb("bo0", [P, C])
        bo1 = sb("bo1", [P, C])
        bv1 = sb("bv1", [P, H * D1])
        bqk_in = sb("bqk_in", [P, 2, H])
        bqs = sb("bqs", [P, H])
        rw0 = sb("rw0", [P, E0])
        rb0 = sb("rb0", [P, E0])
        rw1 = sb("rw1", [P, E1])
        b1t0 = sb("b1t0", [P, E0 * I0 // P])
        b1t1 = sb("b1t1", [P, E1 * I1 // P])
        b2s0 = sb("b2s0", [E0, C])
        b2s1 = sb("b2s1", [E1, C])
        banks = [ctx.enter_context(nc.psum_tensor(f"bank{i}", [P, 512], F32)) for i in range(8)]

        x_loaded = sem("x_loaded")
        const_loaded = sem("const_loaded")
        consts = sem("consts")
        passed = sem("passed")

        CONST_LOADS = [
            (scale_in, a["scale_rows"]), (bo0, a["b_out"].partition_broadcast(P)),
            (bo1, a["b_proj"].partition_broadcast(P)), (bv1, a["b_v"].partition_broadcast(P)),
            (bqk_in, a["b_qk"]), (rw0, a["router_w"]), (rb0, a["router_b"].partition_broadcast(P)),
            (rw1, a["w_router"]), (b1t0, a["b1_0"]), (b1t1, a["b1_1"]), (b2s0, a["b2_0"]),
            (b2s1, a["b2_1"]), (headrow, a["headrow"]),
        ]
        with nc.Block() as block:
            @block.sync
            def _(sp):
                xd = a["x"].rearrange("b (t p) c -> p (b t) c", p=P)
                for q in range(4):
                    sp.dma_start(x_tok[:, q * T // 4:(q + 1) * T // 4, :],
                                 xd[:, q * T // 4:(q + 1) * T // 4, :]).then_inc(x_loaded, 16)

            @block.scalar
            def _(act):
                for dst, src in CONST_LOADS:
                    act.dma_start(dst[:], src).then_inc(const_loaded, 16)

            @block.gpsimd
            def _(pool):
                c = Steps(pool, consts, 0, NCONST)
                for t, v in ((ident, 0.0), (strict, 1.0), (ones, 1.0), (notdiag, 1.0), (pen0, 0.0),
                             (rneg, -1.0), (causal, 0.0)):
                    c.inc(pool.memset(t[:], v))
                c.wait()
                last = slice(N - P, N)

                def select(t, cmp, fill, base, chan, step):
                    c.inc(pool.affine_select(out=t, in_=t, compare_op=cmp, fill=fill, base=base,
                                             pattern=[[step, P]], channel_multiplier=chan))
                select(ident[:], ALU.not_equal, 1.0, 0, 1, -1)
                select(strict[:], ALU.is_gt, 0.0, 0, -1, 1)
                select(notdiag[:], ALU.not_equal, 0.0, 0, 1, -1)
                select(pen0[:, last], ALU.is_gt, MASKED, 0, 1, -1)
                select(rneg[:, last], ALU.is_gt, 0.0, 0, 1, -1)
                select(causal[:, last], ALU.is_ge, -MASKED, 0, 1, -1)
                c.wait()
                pool.wait_ge(const_loaded, 16 * len(CONST_LOADS))
                c.inc(pool.tensor_scalar(scale0[:], scale_in[:], -1.0, None, ALU.mult))
                c.inc(pool.tensor_scalar(bqs[:], bqk_in[:, 0, :], -1.0 / math.sqrt(D1), None, ALU.mult))
                c.wait()
                c.close()

        def attention(layer):
            L1 = layer == 1
            with ExitStack() as at:
                def sbt(name, shape, dt=F32):
                    return at.enter_context(nc.sbuf_tensor(f"{name}{layer}", shape, dt))

                def s_(name):
                    return at.enter_context(nc.semaphore(f"{name}{layer}"))

                UNITS = H if L1 else 4
                PER = H // UNITS
                NCH = H * D1 // P if L1 else 1
                VW = D1 if L1 else 32
                AHEAD = 4
                NP = 8
                LOS = 2 if L1 else 4

                st = sbt("st", [P, NT, 6])
                mv = sbt("mv", [P, NT, 2])
                ve = sbt("ve", [P, NT])
                sd = sbt("sd", [P, NT])
                rs = sbt("rs", [P, NT])
                xn = sbt("xn", [P, NT, C])
                wq = sbt("wq", [P, UNITS, P])
                wk = sbt("wk", [P, UNITS, P])
                wv = sbt("wv", [P, H * D1 if L1 else C])
                wo = sbt("wo", [P, NCH, C])
                xb_next = sbt("xb_next", [P, N])
                xb = sbt("xb", [P, N])
                q_full = sbt("q_full", [P, N])
                k_full = sbt("k_full", [P, N])
                q_hi = sbt("q_hi", [P, 2, N], F32R)
                q_lo = sbt("q_lo", [P, 2, N], F32R) if L1 else None
                k_st = sbt("k_st", [P, 2, N], F32R)
                q_head = None if L1 else sbt("q_head", [P, 2, N], F32R)
                v_st = sbt("v_st", [P, NT, H * VW])
                probs = sbt("probs", [P, NP, N])
                rowmin = sbt("rowmin", [P, NP])
                rsum = sbt("rsum", [P, NP])
                rinv = sbt("rinv", [P, NP])
                pt = sbt("pt", [P, 2, N])
                yt = sbt("yt", [P, NCH, N])
                if L1:
                    adj = sbt("adj", [P, TOT])
                    rq_full = sbt("rq_full", [P, N])
                    rk_full = sbt("rk_full", [P, N])
                    rq_hi = sbt("rq_hi", [P, N], F32R)
                    rq_lo = sbt("rq_lo", [P, N], F32R)
                    rk_st = sbt("rk_st", [P, N], F32R)
                    rl = sbt("relu", [P, NT, N])
                    w0 = sbt("w0", [P, NT, N + 8])
                    w1 = sbt("w1", [P, NT, N + 8])
                    top = sbt("top", [P, NT, 8])
                    KEEP = max(1, int(N * 0.2)) - 1
                    PAD = -KEEP % 8
                    ROUNDS = (KEEP + PAD) // 8

                s_bank = banks[0:2]
                t_bank = banks[2:4]
                q_bank, k_bank = (banks[4], banks[4]) if L1 else (banks[4], banks[7])
                n_bank = banks[5]
                o_bank = [banks[6], banks[7] if L1 else banks[6]]
                v_bank = [banks[5], banks[4]]

                w_loaded = s_("w_loaded")
                preset = s_("preset")
                dve_step = s_("dve_step")
                var_ready = s_("var_ready")
                root_ready = s_("root_ready")
                xn_ready = s_("xn_ready")
                n_filled = s_("n_filled")
                n_read = s_("n_read")
                xb_ready = s_("xb_ready")
                v_proj = s_("v_proj")
                v_ready = s_("v_ready")
                q_proj = s_("q_proj")
                k_proj = s_("k_proj")
                q_copied = s_("q_copied")
                k_copied = s_("k_copied")
                q_rounded = s_("q_rounded")
                k_rounded = s_("k_rounded")
                lo_ready = s_("lo_ready")
                head_ready = s_("head_ready")
                scores = s_("scores")
                biased = s_("biased")
                exped = s_("exped")
                scaled = s_("scaled")
                transposed = s_("transposed")
                pt_ready = s_("pt_ready")
                pv_done = s_("pv_done")
                o_ready = s_("o_ready")
                out_proj = s_("out_proj")
                x_ready = s_("x_ready")
                rank_q = s_("rank_q")
                rank_k = s_("rank_k")
                rank_lo = s_("rank_lo")
                relu_ready = s_("relu_ready")

                START = {"transposed": 4, "pv_done": 2, "pt_ready": 2, "scores": 1, "o_ready": 2,
                         "out_proj": 1, "x_ready": 1}

                def need(eng, sem, value):
                    if isinstance(value, int) and value <= 0:
                        return
                    eng.wait_ge(sem, value + started.get(sem.name, 0))

                started = {sem.name: START[n] for n, sem in (
                    ("transposed", transposed), ("pv_done", pv_done), ("pt_ready", pt_ready),
                    ("scores", scores), ("o_ready", o_ready), ("out_proj", out_proj), ("x_ready", x_ready))}

                def start(eng, sems):
                    for sem in sems:
                        eng.sem_inc(sem, started[sem.name])

                NV = H * D1 // 512 * NT if L1 else 1
                OEV = NCH
                NB = 3 + 2 * NT if L1 else 1
                XB_SLOT = 53 if L1 else 40

                def unit_at(s):
                    h, i = divmod(s, NT)
                    if i or h % PER:
                        return None
                    return h // PER + (2 if L1 else 1)

                R_T, R_Q, R_K, R_S, R_D, R_TOP, R_PEN, R_ADJ = 2, 3, 4, 6, 10, 15, 55, 60

                def pe_unit(pe, b, u):
                    if not L1 or u % UNITS == 0:
                        need(pe, xb_ready, b + u // UNITS + 1)
                    need(pe, q_copied, b * UNITS + u)
                    if L1:
                        need(pe, k_copied, b * UNITS + u)
                    pe.matmul(q_bank[:], wq[:, u % UNITS, :], xb[:], start=True, stop=True).then_inc(q_proj, 1)
                    need(pe, *((q_copied, b * UNITS + u + 1) if L1 else (k_copied, b * UNITS + u)))
                    pe.matmul(k_bank[:], wk[:, u % UNITS, :], xb[:], start=True, stop=True).then_inc(k_proj, 1)

                def pe_values(pe, n):
                    need(pe, xb_ready, n + 1)
                    need(pe, n_read, (n + 1) * NB)
                    need(pe, k_copied, n * UNITS + (2 if L1 else 1))
                    for m in range(NV):
                        if m >= 2:
                            need(pe, v_ready, n * NV + m - 1)
                        bank = v_bank[m % 2]
                        if L1:
                            kb, half = divmod(m, NV // NT)
                            mm = pe.matmul(bank[:], xb[:, kb * P:(kb + 1) * P],
                                           wv[:, half * 512:(half + 1) * 512], start=True, stop=True)
                        else:
                            for kb in range(NT):
                                mm = pe.matmul(bank[:, kb * P:(kb + 1) * P], xb[:, kb * P:(kb + 1) * P],
                                               wv[:], start=True, stop=True)
                        mm.then_inc(v_proj, 1)

                def pe_next_x(pe, n):
                    need(pe, xn_ready, n + 1)
                    need(pe, v_ready, n * NV)
                    for i in range(NT):
                        mm = pe.transpose(n_bank[:, i * P:(i + 1) * P], xn[:, i, :], ident[:])
                    mm.then_inc(n_filled, 1)

                def pe_rank_unit(pe, n, k):
                    need(pe, n_read, n * NB + k)
                    w = wq if k == 1 else wk
                    pe.matmul(n_bank[:], w[:, 0, :], xb_next[:], start=True, stop=True).then_inc(n_filled, 1)

                def pe_rank_scores(pe, n, i):
                    need(pe, n_read, n * NB + 3 + i)
                    if i == 0:
                        need(pe, rank_lo, 2 * n + 2)
                    K, rows = P * (i + 1), slice(i * P, (i + 1) * P)
                    pe.matmul(n_bank[:, 0:K], rq_hi[:, rows], rk_st[:, 0:K], start=True, stop=False)
                    pe.matmul(n_bank[:, 0:K], rq_lo[:, rows], rk_st[:, 0:K], start=False, stop=True)\
                        .then_inc(n_filled, 1)

                def pe_decay(pe, n, i):
                    need(pe, n_read, n * NB + 3 + NT + i)
                    need(pe, relu_ready, n * NT + i + 1)
                    diag = slice(P * i, P * (i + 1))
                    mm = pe.matmul(n_bank[:, diag], strict[:], rl[:, i, diag], start=True, stop=True)
                    if i:
                        pe.matmul(n_bank[:, 0:P * i], strict[:], rl[:, i, 0:P * i], start=True, stop=False,
                                  skip_group_check=True)
                    for r in range(i):
                        mm = pe.matmul(n_bank[:, 0:P * (r + 1)], ones[:], rl[:, r, 0:P * (r + 1)],
                                       start=False, stop=(r == i - 1), skip_group_check=True)
                    mm.then_inc(n_filled, 1)

                def pe_score(pe, b, m):
                    h, i = divmod(m, NT)
                    u = h // PER
                    K = P * (i + 1)
                    dst = s_bank[m % 2][:, 0:K]
                    rows = slice(i * P, (i + 1) * P)
                    need(pe, biased, b * SLOTS + m - 1)
                    if i == 0:
                        need(pe, lo_ready, b * UNITS * LOS + LOS * (u + 1))
                    if L1:
                        pe.matmul(dst, q_hi[:, u % 2, rows], k_st[:, u % 2, 0:K], start=True, stop=False)
                        mm = pe.matmul(dst, q_lo[:, u % 2, rows], k_st[:, u % 2, 0:K], start=False, stop=True)
                    else:
                        if i == 0:
                            need(pe, head_ready, b * H + h + 1)
                        mm = pe.matmul(dst, q_head[:, h % 2, rows], k_st[:, u % 2, 0:K], start=True, stop=True)
                    mm.then_inc(scores, 1)

                def pe_transpose(pe, b, s):
                    need(pe, scaled, b * SLOTS + s + 1)
                    need(pe, pt_ready, b * SLOTS + s - 1)
                    for kb in range(s % NT + 1):
                        mm = pe.transpose(t_bank[s % 2][:, kb * P:(kb + 1) * P],
                                          probs[:, s % NP, kb * P:(kb + 1) * P], ident[:])
                    mm.then_inc(transposed, 1)

                def pe_pv(pe, b, s):
                    h, i = divmod(s, NT)
                    need(pe, pt_ready, b * SLOTS + s + 1)
                    if s == 0:
                        need(pe, v_ready, (b + 1) * NV)
                    if L1:
                        bank, row = o_bank[h // 2 % 2], (h % 2) * D1
                        if s % (2 * NT) == 0:
                            need(pe, o_ready, b * OEV + s // (2 * NT) - 1)
                    else:
                        bank, row = o_bank[0], 32 * (h // 4)
                        if s == 0:
                            need(pe, o_ready, b * OEV)
                    for kb in range(i + 1):
                        first = kb == 0 and (L1 or (i == 0 and h % 4 == 0))
                        last = kb == i and (L1 or h % 4 == 3)
                        mm = pe.matmul(bank[row:row + VW, i * P:(i + 1) * P],
                                       v_st[:, kb, h * VW:(h + 1) * VW],
                                       pt[:, s % 2, kb * P:(kb + 1) * P],
                                       start=first, stop=last, skip_group_check=True)
                    mm.then_inc(pv_done, 1)

                def pe_out(pe, b, last):
                    need(pe, o_ready, (b + 1) * OEV)
                    need(pe, v_ready, (b + (1 if last else 2)) * NV)
                    for i in range(NT):
                        for ch in range(NCH):
                            mm = pe.matmul(banks[4][:, i * P:(i + 1) * P], yt[:, ch, i * P:(i + 1) * P],
                                           wo[:, ch, :], start=(ch == 0), stop=(ch == NCH - 1))
                    mm.then_inc(out_proj, 1)

                def pe_body(pe, b, last):
                    for s in range(SLOTS):
                        if not last:
                            if s == R_T:
                                pe_next_x(pe, b + 1)
                            if L1 and s == R_Q:
                                pe_rank_unit(pe, b + 1, 1)
                            if L1 and s == R_K:
                                pe_rank_unit(pe, b + 1, 2)
                            if L1 and R_S <= s < R_S + NT:
                                pe_rank_scores(pe, b + 1, s - R_S)
                            if L1 and R_D <= s < R_D + NT:
                                pe_decay(pe, b + 1, s - R_D)
                        u = unit_at(s)
                        if u is not None and (u < UNITS or not last):
                            if u == (1 if not L1 else 2):
                                need(pe, x_ready, b)
                            pe_unit(pe, b, u)
                        if s + AHEAD < SLOTS or not last:
                            pe_score(pe, b, s + AHEAD)
                        pe_transpose(pe, b, s)
                        if s >= 1:
                            pe_pv(pe, b, s - 1)
                    pe_pv(pe, b, SLOTS - 1)
                    if not last:
                        pe_values(pe, b + 1)
                    pe_out(pe, b, last)

                def pe_program(pe):
                    start(pe, (transposed, pv_done, scores, out_proj))
                    pe.wait_ge(w_loaded, 64)
                    pe_next_x(pe, 0)
                    if L1:
                        pe_rank_unit(pe, 0, 1)
                        pe_rank_unit(pe, 0, 2)
                        for i in range(NT):
                            pe_rank_scores(pe, 0, i)
                        for i in range(NT):
                            pe_decay(pe, 0, i)
                    for u in range(2 if L1 else 1):
                        pe_unit(pe, 0, u)
                    pe_values(pe, 0)
                    for m in range(AHEAD):
                        pe_score(pe, 0, m)
                    with pe.Fori(0, B - 1) as b:
                        pe_body(pe, b, False)
                    pe_body(pe, B - 1, True)

                def dve_norm(dve, c, n):
                    for i in range(NT):
                        c.inc(dve.bn_stats(st[:, i, :], x_tok[:, bass.ds(n * NT + i, 1), :]
                                           .rearrange("p a c -> p (a c)")))
                    c.wait()
                    apart(dve, passed)
                    for i in range(NT):
                        c.inc(dve.bn_aggr(mv[:, i, :], st[:, i, :]))
                    c.wait()
                    dve.tensor_scalar(ve[:], mv[:, :, 1], EPS, None, ALU.add).then_inc(var_ready, 1)

                def dve_norm2(dve, c, n):
                    need(dve, root_ready, n + 1)
                    c.inc(dve.reciprocal(rs[:], sd[:]))
                    c.wait()
                    for i in range(NT):
                        ins = dve.tensor_scalar(xn[:, i, :], x_tok[:, bass.ds(n * NT + i, 1), :]
                                                .rearrange("p a c -> p (a c)"), mv[:, i, 0:1], rs[:, i:i + 1],
                                                ALU.subtract, ALU.mult)
                    ins.then_inc(xn_ready, 1)

                NORM_STEPS = 2 * NT + 1

                def dve_relu(dve, c, n, i):
                    K = P * (i + 1)
                    need(dve, n_filled, n * NB + 4 + i)
                    dve.scalar_tensor_tensor(out=rl[:, i, 0:K], in0=n_bank[:, 0:K], scalar=0.0,
                                             in1=rneg[:, N - K:N], op0=ALU.min, op1=ALU.mult).then_inc(n_read, 1)
                    need(dve, n_read, n * NB + 4 + i)
                    dve.memset(rl[:, i, 0:1], 0.0).then_inc(relu_ready, 1)

                def dve_decay(dve, c, n, i):
                    K = P * (i + 1)
                    need(dve, n_filled, n * NB + 4 + NT + i)
                    dve.scalar_tensor_tensor(out=w0[:, i, 0:K], in0=n_bank[:, 0:K], scalar=-1.0,
                                             in1=causal[:, N - K:N], op0=ALU.mult, op1=ALU.add).then_inc(n_read, 1)

                def dve_top(dve, c, r):
                    src = w0 if r == 0 else w1
                    c.wait()
                    apart(dve, passed)
                    for i in range(NT):
                        c.inc(dve.max(top[:, i, :], src[:, i, 0:P * (i + 1) + PAD]))
                    c.mark = c.n

                def dve_take(dve, c, r, tiles):
                    src = w0 if r == 0 else w1
                    c.wait(c.mark)
                    apart(dve, passed)
                    for i in tiles:
                        W = P * (i + 1) + PAD
                        c.inc(dve.match_replace(out=w1[:, i, 0:W], in_to_replace=top[:, i, :],
                                                in_values=src[:, i, 0:W], imm_value=TAKEN))

                def dve_penalty(dve, c):
                    c.wait()
                    for i in range(NT):
                        K = P * (i + 1)
                        c.inc(dve.tensor_scalar(w1[:, i, 0:K], w1[:, i, 0:K], TAKEN / 2, MASKED, ALU.is_gt, ALU.mult))
                    c.wait()
                    for i in range(NT):
                        blk = w1[:, i, P * i:P * (i + 1)]
                        c.inc(dve.tensor_tensor(blk, blk, notdiag[:], ALU.mult))

                def dve_adj(dve, c):
                    c.wait()
                    for i in range(NT):
                        K = P * (i + 1)
                        c.inc(dve.tensor_tensor(adj[:, OFF[i]:OFF[i] + K], w1[:, i, 0:K], w0[:, i, 0:K], ALU.subtract))
                    c.wait()

                RANK_STEPS = ROUNDS * 2 * NT + 3 * NT if L1 else 0

                def dve_values(dve, c, n):
                    need(dve, pv_done, n * SLOTS)
                    for m in range(NV):
                        need(dve, v_proj, n * NV + m + 1)
                        bank = v_bank[m % 2]
                        if L1:
                            kb, half = divmod(m, NV // NT)
                            cols = slice(half * 512, (half + 1) * 512)
                            dve.tensor_tensor(v_st[:, kb, cols], bank[:], bv1[:, cols], ALU.add).then_inc(v_ready, 1)
                        else:
                            for kb in range(NT):
                                for j in range(4):
                                    dst = v_st[:, kb, :].rearrange("p (g j c) -> p g j c", g=4, j=4)[:, :, j, 8 * j:8 * j + 8]
                                    src = bank[:, kb * P:(kb + 1) * P].rearrange("p (g j d) -> p g j d", g=4, j=4)[:, :, j, :]
                                    ins = dve.tensor_copy(dst, src)
                            ins.then_inc(v_ready, 1)

                def dve_round(dve, b, u):
                    need(dve, q_copied, b * UNITS + u + 1)
                    need(dve, scores, b * SLOTS + (u - 1) * PER * NT)
                    dve.tensor_copy(q_hi[:, u % 2, :], q_full[:]).then_inc(q_rounded, 1)

                def dve_bias(dve, b, m):
                    K = P * (m % NT + 1)
                    k = m % NP
                    need(dve, scores, b * SLOTS + m + 1)
                    need(dve, transposed, b * SLOTS + m - NP + 1)
                    apart(dve, passed)
                    bias = adj[:, OFF[m % NT]:OFF[m % NT] + K] if L1 else pen0[:, N - K:N]
                    dve.tensor_tensor_reduce(probs[:, k, 0:K], s_bank[m % 2][:, 0:K], bias, 1.0, FLOOR,
                                             ALU.add, ALU.min, rowmin[:, k:k + 1]).then_inc(biased, 1)

                def dve_scale(dve, c, b, m):
                    K = P * (m % NT + 1)
                    k = m % NP
                    need(dve, exped, b * SLOTS + m + 1)
                    if not L1 and m % NT == 0:
                        c.inc(dve.tensor_scalar(rsum[:, k:k + 1], rsum[:, k:k + 1], 0.5, None, ALU.max))
                        c.wait()
                    c.inc(dve.reciprocal(rinv[:, k:k + 1], rsum[:, k:k + 1]))
                    c.wait()
                    dve.tensor_scalar(probs[:, k, 0:K], probs[:, k, 0:K], rinv[:, k:k + 1], None,
                                      ALU.mult).then_inc(scaled, 1)

                def scale_steps(first, last):
                    return sum(1 if L1 or m % NT else 2 for m in range(first, last))

                def dve_body(dve, c, b, last):
                    for s in range(SLOTS):
                        if not last:
                            if s == 0:
                                dve_norm(dve, c, b + 1)
                            if s == 1:
                                dve_norm2(dve, c, b + 1)
                        u = unit_at(s)
                        if u is not None and (u < UNITS or not last):
                            dve_round(dve, b, u)
                        if not last and L1 and s == R_ADJ:
                            dve_adj(dve, c)
                        if s + AHEAD < SLOTS or not last:
                            dve_bias(dve, b, s + AHEAD)
                        if s + 2 < SLOTS or not last:
                            dve_scale(dve, c, b, s + 2)
                        if not last and L1:
                            if R_S <= s < R_S + NT:
                                dve_relu(dve, c, b + 1, s - R_S)
                            if R_D <= s < R_D + NT:
                                dve_decay(dve, c, b + 1, s - R_D)
                            r, part = divmod(s - R_TOP, 3)
                            if 0 <= r < ROUNDS:
                                if part == 0:
                                    if r == 0:
                                        need(dve, n_read, (b + 2) * NB)
                                    dve_top(dve, c, r)
                                elif part == 1:
                                    dve_take(dve, c, r, (3,))
                                else:
                                    dve_take(dve, c, r, (0, 1, 2))
                            if s == R_PEN:
                                dve_penalty(dve, c)
                    if not last:
                        dve_values(dve, c, b + 1)
                    need(dve, out_proj, b + 1)
                    xs = x_tok[:, bass.ds(b * NT, NT), :]
                    c.inc(dve.tensor_tensor(xs, xs, banks[4][:].rearrange("p (t c) -> p t c", c=C), ALU.add))
                    c.wait()
                    bo = bo1 if L1 else bo0
                    dve.tensor_tensor(xs, xs, bo[:].unsqueeze(1).to_broadcast([P, NT, C]), ALU.add).then_inc(x_ready, 1)
                    c.close()

                def dve_program(dve):
                    start(dve, (x_ready,))
                    if L1:
                        for i in range(NT):
                            K = P * (i + 1)
                            dve.memset(w0[:, i, K:K + PAD], SENTINEL).then_inc(preset, 1)
                        dve.wait_ge(preset, NT)
                    else:
                        dve.wait_ge(x_loaded, 64)
                        dve.memset(v_st[:], 0.0).then_inc(preset, 1)
                        dve.wait_ge(preset, 1)
                    head = NORM_STEPS + RANK_STEPS + scale_steps(0, 2)
                    c = Steps(dve, dve_step, 0, head)
                    dve_norm(dve, c, 0)
                    dve_norm2(dve, c, 0)
                    if L1:
                        for i in range(NT):
                            dve_relu(dve, c, 0, i)
                        for i in range(NT):
                            dve_decay(dve, c, 0, i)
                        need(dve, n_read, NB)
                        for r in range(ROUNDS):
                            dve_top(dve, c, r)
                            dve_take(dve, c, r, range(NT))
                        dve_penalty(dve, c)
                        dve_adj(dve, c)
                    for u in range(2 if L1 else 1):
                        dve_round(dve, 0, u)
                    dve_values(dve, c, 0)
                    for s in range(-AHEAD, 0):
                        dve_bias(dve, 0, s + AHEAD)
                        if s + 2 >= 0:
                            dve_scale(dve, c, 0, s + 2)
                    c.close()
                    per = NORM_STEPS + RANK_STEPS + scale_steps(2, SLOTS + 2) + 1
                    with dve.Fori(0, B - 1) as b:
                        dve_body(dve, Steps(dve, dve_step, b, per, head), b, False)
                    dve_body(dve, Steps(dve, dve_step, B - 1, scale_steps(2, SLOTS) + 1, head, per), B - 1, True)

                def act_root(act, n):
                    need(act, var_ready, n + 1)
                    act.activation(sd[:], ve[:], ACT.Sqrt).then_inc(root_ready, 1)

                def act_next_x(act, n):
                    need(act, n_filled, n * NB + 1)
                    act.activation(xb_next[:], n_bank[:], ACT.Copy).then_inc(n_read, 1)

                def act_rank_q(act, n):
                    need(act, n_filled, n * NB + 2)
                    act.activation(rq_full[:], n_bank[:], ACT.Identity, bias=bqs[:, 0:1],
                                   scale=-1.0 / math.sqrt(D1)).then_inc(n_read, 1)
                    need(act, n_read, n * NB + 2)
                    act.activation(rq_hi[:], rq_full[:], ACT.Copy).then_inc(rank_q, 1)

                def act_rank_k(act, n):
                    need(act, n_filled, n * NB + 3)
                    act.activation(rk_full[:], n_bank[:], ACT.Identity, bias=bqk_in[:, 1, 0:1]).then_inc(n_read, 1)
                    need(act, n_read, n * NB + 3)
                    act.activation(rk_st[:], rk_full[:], ACT.Copy).then_inc(rank_k, 1)

                def act_unit(act, b, u):
                    g = b * UNITS + u
                    need(act, q_proj, g + 1)
                    need(act, lo_ready, g * LOS)
                    if L1:
                        act.activation(q_full[:], q_bank[:], ACT.Identity, bias=bqs[:, u % UNITS:u % UNITS + 1],
                                       scale=-1.0 / math.sqrt(D1)).then_inc(q_copied, 1)
                        need(act, k_proj, g + 1)
                        act.activation(k_full[:], k_bank[:], ACT.Identity,
                                       bias=bqk_in[:, 1, u % UNITS:u % UNITS + 1]).then_inc(k_copied, 1)
                    else:
                        act.activation(q_full[:], q_bank[:], ACT.Copy,
                                       scale=scale0[:, u % UNITS:u % UNITS + 1]).then_inc(q_copied, 1)
                        need(act, k_proj, g + 1)
                        act.activation(k_full[:], k_bank[:], ACT.Copy).then_inc(k_copied, 1)
                    need(act, k_copied, g + 1)
                    need(act, scores, b * SLOTS + (u - 1) * PER * NT)
                    act.activation(k_st[:, u % 2, :], k_full[:], ACT.Copy).then_inc(k_rounded, 1)

                def act_exp(act, b, m):
                    K = P * (m % NT + 1)
                    k = m % NP
                    need(act, biased, b * SLOTS + m + 1)
                    act.activation(probs[:, k, 0:K], probs[:, k, 0:K], ACT.Exp, bias=rowmin[:, k:k + 1],
                                   scale=-1.0, accum_out=rsum[:, k:k + 1]).then_inc(exped, 1)

                def act_evacuate(act, b, s):
                    K = P * (s % NT + 1)
                    need(act, transposed, b * SLOTS + s + 1)
                    need(act, pv_done, b * SLOTS + s - 1)
                    act.activation(pt[:, s % 2, 0:K], t_bank[s % 2][:, 0:K], ACT.Copy).then_inc(pt_ready, 1)

                def act_outputs(act, b, n):
                    need(act, pv_done, b * SLOTS + (n + 1) * (SLOTS // OEV))
                    need(act, out_proj, b)
                    act.activation(yt[:, n, :], o_bank[n % 2][:], ACT.Copy).then_inc(o_ready, 1)

                def act_body(act, b, last):
                    for s in range(SLOTS):
                        if not last:
                            if s == 1:
                                act_root(act, b + 1)
                            if s == R_T:
                                act_next_x(act, b + 1)
                            if L1 and s == R_Q:
                                act_rank_q(act, b + 1)
                            if L1 and s == R_K:
                                act_rank_k(act, b + 1)
                        u = unit_at(s)
                        if u is not None and (u < UNITS or not last):
                            act_unit(act, b, u)
                        if s + 3 < SLOTS or not last:
                            act_exp(act, b, s + 3)
                        act_evacuate(act, b, s)
                        if s >= 2 and (s - 1) % (SLOTS // OEV) == 0:
                            act_outputs(act, b, (s - 1) // (SLOTS // OEV) - 1)
                    act_outputs(act, b, OEV - 1)

                def act_program(act):
                    start(act, (pt_ready, o_ready))
                    act_root(act, 0)
                    act_next_x(act, 0)
                    if L1:
                        act_rank_q(act, 0)
                        act_rank_k(act, 0)
                    for u in range(2 if L1 else 1):
                        act_unit(act, 0, u)
                    for m in range(3):
                        act_exp(act, 0, m)
                    with act.Fori(0, B - 1) as b:
                        act_body(act, b, False)
                    act_body(act, B - 1, True)

                def pool_xb(pool, n):
                    need(pool, n_read, n * NB + 1)
                    need(pool, k_proj, n * UNITS)
                    need(pool, v_proj, n * NV)
                    apart(pool, passed)
                    pool.tensor_copy(xb[:], xb_next[:]).then_inc(xb_ready, 1)
                    need(pool, xb_ready, n + 1)

                def pool_rank_lo(pool, n):
                    need(pool, rank_q, n + 1)
                    pool.tensor_tensor(rq_lo[:], rq_full[:], rq_hi[:].bitcast(F32), ALU.subtract).then_inc(rank_lo, 1)
                    need(pool, rank_lo, 2 * n + 1)
                    need(pool, rank_k, n + 1)
                    pool.tensor_tensor(rk_st[64:P, :], rk_full[64:P, :], rk_st[64:P, :].bitcast(F32),
                                       ALU.subtract).then_inc(rank_lo, 1)
                    need(pool, rank_lo, 2 * n + 2)

                def pool_unit(pool, b, u):
                    lo = (b * UNITS + u) * LOS
                    k = u % 2
                    need(pool, q_rounded, b * UNITS + u + 1)
                    if L1:
                        pool.tensor_tensor(q_lo[:, k, :], q_full[:], q_hi[:, k, :].bitcast(F32),
                                           ALU.subtract).then_inc(lo_ready, 1)
                    else:
                        pool.tensor_tensor(q_hi[64:P, k, :], q_full[64:P, :], q_hi[64:P, k, :].bitcast(F32),
                                           ALU.subtract).then_inc(lo_ready, 1)
                    need(pool, k_rounded, b * UNITS + u + 1)
                    for n, rows in enumerate([slice(64, P)] if L1 else [slice(32, 64), slice(96, P)]):
                        need(pool, lo_ready, lo + n + 1)
                        pool.tensor_tensor(k_st[rows, k, :], k_full[rows, :], k_st[rows, k, :].bitcast(F32),
                                           ALU.subtract).then_inc(lo_ready, 1 + n)
                    need(pool, lo_ready, lo + LOS)

                def pool_head(pool, b, h):
                    need(pool, scores, b * SLOTS + (h - 1) * NT)
                    apart(pool, passed)
                    pool.tensor_scalar(q_head[:, h % 2, :], q_hi[:, h // PER % 2, :].bitcast(F32),
                                       headrow[:, h % PER:h % PER + 1], None, ALU.mult).then_inc(head_ready, 1)
                    need(pool, head_ready, b * H + h + 1)

                def pool_body(pool, b, last):
                    for s in range(SLOTS):
                        if not last:
                            if L1 and s == R_K:
                                pool_rank_lo(pool, b + 1)
                            if s == XB_SLOT:
                                pool_xb(pool, b + 1)
                        u = unit_at(s)
                        if u is not None and (u < UNITS or not last):
                            pool_unit(pool, b, u)
                        if not L1 and s % NT == 1 and (s // NT + 2 < H or not last):
                            pool_head(pool, b, s // NT + 2)

                def pool_program(pool):
                    pool_xb(pool, 0)
                    if L1:
                        pool_rank_lo(pool, 0)
                    for u in range(2 if L1 else 1):
                        pool_unit(pool, 0, u)
                    if not L1:
                        pool_head(pool, 0, 0)
                        pool_head(pool, 0, 1)
                    with pool.Fori(0, B - 1) as b:
                        pool_body(pool, b, False)
                    pool_body(pool, B - 1, True)

                with nc.Block() as block:
                    @block.sync
                    def _(sp):
                        for dst, name in ((wq, "wq"), (wk, "wk"), (wv, "wv"), (wo, "wo")):
                            sp.dma_start(dst[:], a[f"{name}{layer}"]).then_inc(w_loaded, 16)
                        sp.wait_ge(w_loaded, 64)

                    @block.tensor
                    def _(pe):
                        pe_program(pe)

                    @block.vector
                    def _(dve):
                        dve_program(dve)

                    @block.scalar
                    def _(act):
                        act_program(act)

                    @block.gpsimd
                    def _(pool):
                        pool_program(pool)

        def experts(layer):
            E, I, TOPK = (E0, I0, 4) if layer == 0 else (E1, I1, 1)
            rw = rw0 if layer == 0 else rw1
            b1t = b1t0 if layer == 0 else b1t1
            b2s = b2s0 if layer == 0 else b2s1
            func = ACT.Gelu if layer == 0 else ACT.Relu
            NF = I // P
            PADW = 8 - TOPK
            RW = E + PADW
            CH = T * P // 512
            TC = T // CH
            w1d, w2d = a[f"w1_{layer}"], a[f"w2_{layer}"]
            with ExitStack() as at:
                def sbt(name, shape, dt=F32):
                    return at.enter_context(nc.sbuf_tensor(f"m{layer}_{name}", shape, dt))

                def s_(name):
                    return at.enter_context(nc.semaphore(f"m{layer}_{name}"))

                st = sbt("st", [P, T, 6])
                mv = sbt("mv", [P, T, 2])
                ve = sbt("ve", [P, T])
                sd = sbt("sd", [P, T])
                rs = sbt("rs", [P, T])
                xn = sbt("xn", [P, T, C])
                xt = sbt("xt", [P, T * P])
                xt_hi = sbt("xt_hi", [P, T * P], F32R)
                xt_lo = sbt("xt_lo", [P, T * P], F32R)
                lg = sbt("lg", [P, T, E])
                mx = sbt("mx", [P, T])
                pr = sbt("pr", [P, T, RW])
                pk = sbt("pk", [P, T, RW])
                top = sbt("top", [P, T, 8])
                sm = sbt("sm", [P, T])
                comb = sbt("comb", [P, T, E])
                combT = sbt("combT", [E, T * P])
                w1s = sbt("w1s", [P, 2, I])
                w2s = sbt("w2s", [P, 2, NF, C])
                w1_hi = sbt("w1_hi", [P, 2, I], F32R)
                w1_lo = sbt("w1_lo", [P, 2, I], F32R)
                w2_hi = sbt("w2_hi", [P, 2, NF, C], F32R)
                w2_lo = sbt("w2_lo", [P, 2, NF, C], F32R)
                hid = sbt("hid", [P, 2, NF, 512])
                hid_hi = sbt("hid_hi", [P, 2, NF, 512], F32R)
                hid_lo = sbt("hid_lo", [P, 2, NF, 512], F32R)

                norm_step = s_("norm_step")
                var_ready = s_("var_ready")
                root_ready = s_("root_ready")
                xn_ready = s_("xn_ready")
                xnt_ready = s_("xnt_ready")
                xt_ready = s_("xt_ready")
                xt_split = s_("xt_split")
                logits = s_("logits")
                shifted = s_("shifted")
                router_exp = s_("router_exp")
                router_step = s_("router_step")
                comb_ready = s_("comb_ready")
                comb_t = s_("comb_t")
                comb_t_read = s_("comb_t_read")
                bias_sum = s_("bias_sum")
                bias_read = s_("bias_read")
                weights = [s_("weights_even"), s_("weights_odd")]
                w_split = s_("w_split")
                hidden = s_("hidden")
                hid_full = s_("hid_full")
                hid_read = s_("hid_read")
                hid_round = s_("hid_round")
                lo_ready = s_("lo_ready")
                expert_out = s_("expert_out")
                acc = s_("acc")

                h_bank = banks[0:4]
                o_bank = banks[4:6]

                def act_rounds(f):
                    return f % 2 == 0
                ROUND_D = sum(not act_rounds(f) for f in range(NF))

                def pe_first(pe, e, u, k):
                    if k == 0:
                        need(pe, w_split, (e + 1) * 4)
                    if isinstance(e, int) and e == 0:
                        pe.wait_ge(xt_split, CH + k + 1)
                    cols = slice(k * 512, (k + 1) * 512)
                    for f in range(NF):
                        j = (e * CH + k) * NF + f
                        need(pe, hid_read, j - 3)
                        bank = h_bank[(k * NF + f) % 4]
                        rows = slice(f * P, (f + 1) * P)
                        pe.matmul(bank[:], w1_hi[:, u, rows], xt_hi[:, cols], start=True, stop=False)
                        pe.matmul(bank[:], w1_lo[:, u, rows], xt_hi[:, cols], start=False, stop=False)
                        pe.matmul(bank[:], w1_hi[:, u, rows], xt_lo[:, cols], start=False, stop=True).then_inc(hidden, 1)

                def pe_second(pe, e, u, k):
                    n = e * CH + k
                    need(pe, lo_ready, (n + 1) * NF)
                    need(pe, acc, n - 1)
                    for i in range(TC):
                        dst = o_bank[k % 2][:, i * P:(i + 1) * P]
                        rows = slice(i * P, (i + 1) * P)
                        for f in range(NF):
                            pe.matmul(dst, hid_hi[:, k % 2, f, rows], w2_hi[:, u, f, :], start=(f == 0), stop=False)
                            pe.matmul(dst, hid_hi[:, k % 2, f, rows], w2_lo[:, u, f, :], start=False, stop=False)
                            mm = pe.matmul(dst, hid_lo[:, k % 2, f, rows], w2_hi[:, u, f, :], start=False, stop=(f == NF - 1))
                    mm.then_inc(expert_out, 1)

                def pe_pair(pe, t, last):
                    for u in range(2):
                        e = t * 2 + u
                        for k in range(CH):
                            if k < CH - 1:
                                pe_first(pe, e, u, k + 1)
                            elif u == 0:
                                pe_first(pe, e + 1, 1, 0)
                            elif not last:
                                pe_first(pe, e + 1, 0, 0)
                            pe_second(pe, e, u, k)

                def pe_program(pe):
                    for q in range(CH):
                        pe.wait_ge(xn_ready, q + 1)
                        if q >= 2:
                            pe.wait_ge(xt_ready, q - 1)
                            pe.wait_ge(xt_split, q - 1)
                        for i in range(TC):
                            mm = pe.transpose(banks[6 + q % 2][:, i * P:(i + 1) * P], xn[:, q * TC + i, :], ident[:])
                        mm.then_inc(xnt_ready, 1)
                    for t in range(T):
                        if t % TC == 0:
                            pe.wait_ge(xt_ready, t // TC + 1)
                        mm = pe.matmul(banks[5][:, t * E:(t + 1) * E], xt[:, t * P:(t + 1) * P], rw[:],
                                       start=True, stop=True)
                    mm.then_inc(logits, 1)
                    pe_first(pe, 0, 0, 0)
                    pe.wait_ge(comb_ready, 1)
                    for q in range(CH):
                        if q >= 2:
                            pe.wait_ge(comb_t_read, q - 1)
                        for i in range(TC):
                            mm = pe.transpose(banks[6 + q % 2][0:E, i * P:(i + 1) * P], comb[:, TC * q + i, :], ident[:])
                        mm.then_inc(comb_t, 1)
                    pe_pair(pe, 0, False)
                    for q in range(CH):
                        pe.wait_ge(comb_t_read, CH)
                        if q >= 2:
                            pe.wait_ge(bias_read, q - 1)
                        for i in range(TC):
                            t = TC * q + i
                            mm = pe.matmul(banks[6 + q % 2][:, i * P:(i + 1) * P], combT[:, t * P:(t + 1) * P], b2s[:],
                                           start=True, stop=True)
                        mm.then_inc(bias_sum, 1)
                    with pe.Fori(1, E // 2 - 1) as t:
                        pe_pair(pe, t, False)
                    pe_pair(pe, E // 2 - 1, True)

                def dve_low(dve, e, u, k):
                    n = e * CH + k
                    for f in range(NF):
                        h = hid[:, k % 2, f, :]
                        hi = hid_hi[:, k % 2, f, :]
                        if act_rounds(f):
                            need(dve, hid_read, n * NF + f + 1)
                        else:
                            need(dve, hid_full, n * NF + f + 1)
                            need(dve, expert_out, n - 1)
                            dve.tensor_copy(hi, h).then_inc(hid_round, 1)
                    for f in range(NF):
                        h = hid[:, k % 2, f, :]
                        hi = hid_hi[:, k % 2, f, :]
                        if f == 0:
                            need(dve, expert_out, n - 1)
                            need(dve, hid_round, (n + 1) * ROUND_D)
                        dve.tensor_tensor(hid_lo[:, k % 2, f, :], h, hi.bitcast(F32), ALU.subtract).then_inc(lo_ready, 1)

                def dve_acc(dve, e, u, k):
                    n = e * CH + k
                    need(dve, expert_out, n + 1)
                    if not isinstance(n, int) or n >= CH:
                        need(dve, acc, n - CH + 1)
                    for i in range(TC):
                        tile = TC * k + i
                        ins = dve.scalar_tensor_tensor(
                            out=x_tok[:, tile, :], in0=o_bank[k % 2][:, i * P:(i + 1) * P],
                            scalar=comb[:, tile, bass.ds(e, 1)], in1=x_tok[:, tile, :],
                            op0=ALU.mult, op1=ALU.add)
                    ins.then_inc(acc, 1)

                def dve_pair(dve, t, last):
                    for u in range(2):
                        e = t * 2 + u
                        for k in range(CH):
                            if k < CH - 1:
                                dve_low(dve, e, u, k + 1)
                            elif u == 0:
                                dve_low(dve, e + 1, 1, 0)
                            elif not last:
                                dve_low(dve, e + 1, 0, 0)
                            dve_acc(dve, e, u, k)

                def dve_program(dve):
                    c = Steps(dve, norm_step, 0, 2 * T + 2)
                    for t in range(T):
                        c.inc(dve.bn_stats(st[:, t, :], x_tok[:, t, :]))
                    c.wait()
                    for t in range(T):
                        c.inc(dve.bn_aggr(mv[:, t, :], st[:, t, :]))
                    c.wait()
                    c.inc(dve.tensor_scalar(ve[:], mv[:, :, 1], EPS, None, ALU.add))
                    c.wait()
                    dve.sem_inc(var_ready, 1)
                    dve.wait_ge(root_ready, 1)
                    c.inc(dve.reciprocal(rs[:], sd[:]))
                    c.wait()
                    c.close()
                    for q in range(CH):
                        for i in range(TC):
                            t = q * TC + i
                            ins = dve.tensor_scalar(xn[:, t, :], x_tok[:, t, :], mv[:, t, 0:1], rs[:, t:t + 1],
                                                    ALU.subtract, ALU.mult)
                        ins.then_inc(xn_ready, 1)
                    for q in range(CH):
                        cols = slice(q * 512, (q + 1) * 512)
                        dve.wait_ge(xt_ready, q + 1)
                        dve.tensor_copy(xt_hi[:, cols], xt[:, cols]).then_inc(xt_split, 1)
                    dve.wait_ge(xt_split, CH)
                    for q in range(CH):
                        cols = slice(q * 512, (q + 1) * 512)
                        dve.tensor_tensor(xt_lo[:, cols], xt[:, cols], xt_hi[:, cols].bitcast(F32),
                                          ALU.subtract).then_inc(xt_split, 1)
                    step = Steps(dve, router_step, 0, (12 if layer == 0 else 10) - 1 + 2 * T)
                    dve.wait_ge(logits, 1)
                    lp = banks[5][:, 0:T * E].rearrange("p (t e) -> p t e", e=E)
                    if layer == 0:
                        step.inc(dve.tensor_tensor(lg[:], lp, rb0[:].unsqueeze(1).to_broadcast([P, T, E]), ALU.add))
                    else:
                        step.inc(dve.tensor_copy(lg[:], lp))
                    step.wait()
                    step.inc(dve.tensor_reduce(mx[:], lg[:], AX.X, ALU.max))
                    step.wait()
                    step.inc(dve.tensor_tensor(lg[:], lg[:], mx[:].unsqueeze(2).to_broadcast([P, T, E]), ALU.subtract))
                    step.inc(dve.memset(pr[:, :, E:RW], 2.0))
                    step.wait()
                    dve.sem_inc(shifted, 1)
                    dve.wait_ge(router_exp, 1)
                    step.inc(dve.tensor_reduce(sm[:], pr[:, :, 0:E], AX.X, ALU.add))
                    step.wait()
                    step.inc(dve.reciprocal(mx[:], sm[:]))
                    step.wait()
                    step.inc(dve.tensor_tensor(pr[:, :, 0:E], pr[:, :, 0:E], mx[:].unsqueeze(2).to_broadcast([P, T, E]), ALU.mult))
                    step.wait()
                    for t in range(T):
                        step.inc(dve.max(top[:, t, :], pr[:, t, :]))
                    step.wait()
                    for t in range(T):
                        step.inc(dve.match_replace(out=pk[:, t, :], in_to_replace=top[:, t, :], in_values=pr[:, t, :],
                                                   imm_value=-1.0))
                    step.wait()
                    step.inc(dve.tensor_scalar(pk[:, :, 0:E], pk[:, :, 0:E], 0.0, None, ALU.is_lt))
                    step.wait()
                    step.inc(dve.tensor_tensor(comb[:], pr[:, :, 0:E], pk[:, :, 0:E], ALU.mult))
                    step.wait()
                    if layer == 0:
                        step.inc(dve.tensor_reduce(sm[:], comb[:], AX.X, ALU.add))
                        step.wait()
                        step.inc(dve.reciprocal(mx[:], sm[:]))
                        step.wait()
                        step.inc(dve.tensor_tensor(comb[:], comb[:], mx[:].unsqueeze(2).to_broadcast([P, T, E]), ALU.mult))
                        step.wait()
                    dve.sem_inc(comb_ready, 1)
                    dve_low(dve, 0, 0, 0)
                    for q in range(CH):
                        dve.wait_ge(comb_t, q + 1)
                        dve.tensor_copy(combT[:, q * 512:(q + 1) * 512], banks[6 + q % 2][0:E, :]).then_inc(comb_t_read, 1)
                    dve_pair(dve, 0, False)
                    dve.wait_ge(acc, 2 * CH)
                    for q in range(CH):
                        dve.wait_ge(bias_sum, q + 1)
                        xs = x_tok[:, TC * q:TC * (q + 1), :]
                        dve.tensor_tensor(xs, xs, banks[6 + q % 2][:].rearrange("p (t c) -> p t c", c=C),
                                          ALU.add).then_inc(bias_read, 1)
                    dve.wait_ge(bias_read, CH)
                    with dve.Fori(1, E // 2 - 1) as t:
                        dve_pair(dve, t, False)
                    dve_pair(dve, E // 2 - 1, True)
                    dve.wait_ge(acc, E * CH)

                def act_hidden(act, e, u, k):
                    n = e * CH + k
                    for f in range(NF):
                        j = n * NF + f
                        bank = h_bank[(k * NF + f) % 4]
                        bias = b1t[:, bass.ds(e * NF + f, 1)]
                        need(act, hidden, j + 1)
                        need(act, lo_ready, (n - 1) * NF)
                        apart(act, passed)
                        ins = act.activation(hid[:, k % 2, f, :], bank[:], func, bias=bias)
                        ins.then_inc(hid_full, 1)
                        if act_rounds(f):
                            need(act, expert_out, n - 1)
                            apart(act, passed)
                            act.activation(hid_hi[:, k % 2, f, :], bank[:], func, bias=bias).then_inc(hid_read, 1)
                        else:
                            need(act, hid_full, j + 1)
                            act.sem_inc(hid_read, 1)

                def act_pair(act, t):
                    for u in range(2):
                        for k in range(CH):
                            act_hidden(act, t * 2 + u, u, k)

                def act_program(act):
                    act.wait_ge(var_ready, 1)
                    act.activation(sd[:], ve[:], ACT.Sqrt).then_inc(root_ready, 1)
                    for q in range(CH):
                        act.wait_ge(xnt_ready, q + 1)
                        act.activation(xt[:, q * 512:(q + 1) * 512], banks[6 + q % 2][:], ACT.Copy).then_inc(xt_ready, 1)
                    act.wait_ge(shifted, 1)
                    act.activation(pr[:, :, 0:E], lg[:], ACT.Exp).then_inc(router_exp, 1)
                    act_pair(act, 0)
                    with act.Fori(1, E // 2) as t:
                        act_pair(act, t)

                def pool_split(pool, e, u, t):
                    need(pool, weights[u], 32 * (t + 1))
                    need(pool, expert_out, (e - 1) * CH)
                    n = e * 4
                    for step, (hi, lo, raw) in enumerate(((w1_hi[:, u, :], w1_lo[:, u, :], w1s[:, u, :]),
                                                          (w2_hi[:, u], w2_lo[:, u], w2s[:, u]))):
                        apart(pool, passed)
                        pool.tensor_copy(hi, raw).then_inc(w_split, 1)
                        need(pool, w_split, n + 2 * step + 1)
                        pool.tensor_tensor(lo, raw, hi.bitcast(F32), ALU.subtract).then_inc(w_split, 1)
                        need(pool, w_split, n + 2 * step + 2)

                with nc.Block() as block:
                    @block.sync
                    def _(sp):
                        for u in range(2):
                            sp.dma_start(w1s[:, u, :], w1d[u]).then_inc(weights[u], 16)
                            sp.dma_start(w2s[:, u, :, :], w2d[u].rearrange("(f p) c -> p f c", p=P)).then_inc(weights[u], 16)
                        with sp.Fori(0, E // 2 - 1) as t:
                            for u in range(2):
                                sp.wait_ge(w_split, (t * 2 + u + 1) * 4)
                                e = bass.ds(t * 2 + 2 + u, 1)
                                sp.dma_start(w1s[:, u, :], w1d[e].rearrange("e p i -> p (e i)")).then_inc(weights[u], 16)
                                sp.dma_start(w2s[:, u, :, :], w2d[e].rearrange("e (f p) c -> p (e f) c", p=P)).then_inc(weights[u], 16)

                    @block.tensor
                    def _(pe):
                        pe_program(pe)

                    @block.vector
                    def _(dve):
                        dve_program(dve)

                    @block.scalar
                    def _(act):
                        act_program(act)

                    @block.gpsimd
                    def _(pool):
                        for u in range(2):
                            pool_split(pool, u, u, 0)
                        with pool.Fori(1, E // 2) as t:
                            for u in range(2):
                                pool_split(pool, t * 2 + u, u, t)

        attention(0)
        experts(0)
        attention(1)
        experts(1)
        stored = sem("stored")
        with nc.Block() as block:
            @block.sync
            def _(sp):
                sp.dma_start(out.rearrange("b (t p) c -> p (b t) c", p=P), x_tok[:]).then_inc(stored, 16)
                sp.wait_ge(stored, 16)


def kernel(**inputs):
    import concourse.bacc as bacc
    from concourse.bass_utils import run_bass_kernel_spmd

    i = {k: np.ascontiguousarray(v) for k, v in inputs.items()}
    x = i["L0_attn_x"]
    C = x.shape[-1]
    H = i["L0_attn_scale"].shape[0]
    d0 = C // H
    D1 = i["L1_attn_W_attn"].shape[0] // 3 // H

    def four(w):
        return np.repeat(w.reshape(C, 4, 1, 4 * d0), 4, axis=2).reshape(C, 4, 128)

    def two(w):
        return np.repeat(w.T.reshape(C, H, 1, D1), 2, axis=2).reshape(C, H, 2 * D1)

    wqkv = i["L0_attn_w_qkv"]
    wa, ba = i["L1_attn_W_attn"], i["L1_attn_b_attn"]
    M = H * D1
    scale = i["L0_attn_scale"].reshape(4, 4)
    headrow = np.zeros((4, 4, d0, 4), np.float32)
    for j in range(4):
        headrow[:, j, :, j] = 1.0
    arrays = {
        "x": x,
        "wq0": four(wqkv[:, 0:C]), "wk0": four(wqkv[:, C:2 * C]), "wv0": wqkv[:, 2 * C:],
        "wo0": i["L0_attn_w_out"].reshape(C, 1, C), "b_out": i["L0_attn_b_out"],
        "scale_rows": np.tile(np.repeat(scale.T, d0, axis=0), (4, 1)),
        "headrow": headrow.reshape(128, 4),
        "wq1": two(wa[0:M]), "wk1": two(wa[M:2 * M]), "wv1": wa[2 * M:].T,
        "wo1": i["L1_attn_W_proj"].T.reshape(M // 128, 128, C).transpose(1, 0, 2),
        "b_proj": i["L1_attn_b_proj"], "b_v": ba[2 * M:],
        "b_qk": np.repeat(ba[0:2 * M].reshape(1, 2, H, D1), 2, axis=0).transpose(0, 3, 1, 2).reshape(2 * D1, 2, H),
        "router_w": i["L0_ffn_router_w"], "router_b": i["L0_ffn_router_b"], "w_router": i["L1_ffn_w_router"],
    }
    for n in (0, 1):
        E, _, F = i[f"L{n}_ffn_w1"].shape
        arrays[f"w1_{n}"] = i[f"L{n}_ffn_w1"]
        arrays[f"w2_{n}"] = i[f"L{n}_ffn_w2"]
        arrays[f"b1_{n}"] = i[f"L{n}_ffn_b1"].reshape(E * F // 128, 128).T
        arrays[f"b2_{n}"] = i[f"L{n}_ffn_b2"]
    arrays = {f"in_{k}": np.ascontiguousarray(v) for k, v in arrays.items()}

    nc = bacc.Bacc("TRN2", target_bir_lowering=False, num_devices=1)
    aps = {k[3:]: nc.dram_tensor(k, v.shape, mybir.dt.from_np(v.dtype), kind="ExternalInput").ap()
           for k, v in arrays.items()}
    out = nc.dram_tensor("out_x", x.shape, mybir.dt.from_np(x.dtype), kind="ExternalOutput").ap()
    build(nc, aps, out)
    r = run_bass_kernel_spmd(nc, [arrays], core_ids=[0])
    return r.results[0]["out_x"]
```

```python
import math
from contextlib import ExitStack

import numpy as np

import concourse.bass as bass
from concourse import mybir

F32 = mybir.dt.float32
F32R = mybir.dt.float32r
ALU = mybir.AluOpType
ACT = mybir.ActivationFunctionType
AX = mybir.AxisListType

P = 128
EPS = 1e-5
MASKED = 1e37
FLOOR = 1e36
TAKEN = -3e38
SENTINEL = 1e37


NCONST = 15


def apart(eng, passed):
    eng.sem_inc(passed, 1)


def need(eng, sem, value):
    if isinstance(value, int) and value <= 0:
        return
    eng.wait_ge(sem, value)


class Steps:

    def __init__(self, eng, sem, it, per, before=0, per_trip=None):
        self.eng, self.sem, self.per, self.n = eng, sem, per, 0
        self.ranked = {}
        self.base = it * (per if per_trip is None else per_trip) + before

    def inc(self, ins):
        ins.then_inc(self.sem, 1)
        self.n += 1

    def wait(self, n=None):
        self.eng.wait_ge(self.sem, self.base + (self.n if n is None else n))

    def close(self):
        assert self.n == self.per, (self.n, self.per)


def build(nc, a, out):
    B, N, C = a["x"].shape
    NT = N // P
    T = B * NT
    H = 16
    D1 = a["wv1"].shape[1] // H
    TOT = P * NT * (NT + 1) // 2
    OFF = [P * i * (i + 1) // 2 for i in range(NT)]
    SLOTS = H * NT
    E0, _, I0 = a["w1_0"].shape
    E1, _, I1 = a["w1_1"].shape

    with ExitStack() as ctx:
        def sb(name, shape, dt=F32):
            return ctx.enter_context(nc.sbuf_tensor(name, shape, dt))

        def sem(name):
            return ctx.enter_context(nc.semaphore(name))

        x_tok = sb("x_tok", [P, T, C])
        ident = sb("ident", [P, P])
        strict = sb("strict", [P, P])
        ones = sb("ones", [P, P])
        notdiag = sb("notdiag", [P, P])
        pen0 = sb("pen0", [P, N])
        rneg = sb("rneg", [P, N])
        causal = sb("causal", [P, N])
        headrow = sb("headrow", [P, 4])
        scale0 = sb("scale0", [P, 4])
        scale_in = sb("scale_in", [P, 4])
        bo0 = sb("bo0", [P, C])
        bo1 = sb("bo1", [P, C])
        bv1 = sb("bv1", [P, H * D1])
        bqk_in = sb("bqk_in", [P, 2, H])
        bqs = sb("bqs", [P, H])
        rw0 = sb("rw0", [P, E0])
        rb0 = sb("rb0", [P, E0])
        rw1 = sb("rw1", [P, E1])
        b1t0 = sb("b1t0", [P, E0 * I0 // P])
        b1t1 = sb("b1t1", [P, E1 * I1 // P])
        b2s0 = sb("b2s0", [E0, C])
        b2s1 = sb("b2s1", [E1, C])
        banks = [ctx.enter_context(nc.psum_tensor(f"bank{i}", [P, 512], F32)) for i in range(8)]

        x_loaded = sem("x_loaded")
        const_loaded = sem("const_loaded")
        consts = sem("consts")
        passed = sem("passed")

        CONST_LOADS = [
            (scale_in, a["scale_rows"]), (bo0, a["b_out"].partition_broadcast(P)),
            (bo1, a["b_proj"].partition_broadcast(P)), (bv1, a["b_v"].partition_broadcast(P)),
            (bqk_in, a["b_qk"]), (rw0, a["router_w"]), (rb0, a["router_b"].partition_broadcast(P)),
            (rw1, a["w_router"]), (b1t0, a["b1_0"]), (b1t1, a["b1_1"]), (b2s0, a["b2_0"]),
            (b2s1, a["b2_1"]), (headrow, a["headrow"]),
        ]
        with nc.Block() as block:
            @block.sync
            def _(sp):
                xd = a["x"].rearrange("b (t p) c -> p (b t) c", p=P)
                for q in range(4):
                    sp.dma_start(x_tok[:, q * T // 4:(q + 1) * T // 4, :],
                                 xd[:, q * T // 4:(q + 1) * T // 4, :]).then_inc(x_loaded, 16)

            @block.scalar
            def _(act):
                for dst, src in CONST_LOADS:
                    act.dma_start(dst[:], src).then_inc(const_loaded, 16)

            @block.gpsimd
            def _(pool):
                c = Steps(pool, consts, 0, NCONST)
                for t, v in ((ident, 0.0), (strict, 1.0), (ones, 1.0), (notdiag, 1.0), (pen0, 0.0),
                             (rneg, -1.0), (causal, 0.0)):
                    c.inc(pool.memset(t[:], v))
                c.wait()
                last = slice(N - P, N)

                def select(t, cmp, fill, base, chan, step):
                    c.inc(pool.affine_select(out=t, in_=t, compare_op=cmp, fill=fill, base=base,
                                             pattern=[[step, P]], channel_multiplier=chan))
                select(ident[:], ALU.not_equal, 1.0, 0, 1, -1)
                select(strict[:], ALU.is_gt, 0.0, 0, -1, 1)
                select(notdiag[:], ALU.not_equal, 0.0, 0, 1, -1)
                select(pen0[:, last], ALU.is_gt, MASKED, 0, 1, -1)
                select(rneg[:, last], ALU.is_gt, 0.0, 0, 1, -1)
                select(causal[:, last], ALU.is_ge, -MASKED, 0, 1, -1)
                c.wait()
                pool.wait_ge(const_loaded, 16 * len(CONST_LOADS))
                c.inc(pool.tensor_scalar(scale0[:], scale_in[:], -1.0, None, ALU.mult))
                c.inc(pool.tensor_scalar(bqs[:], bqk_in[:, 0, :], -1.0 / math.sqrt(D1), None, ALU.mult))
                c.wait()
                c.close()

        def attention(layer):
            L1 = layer == 1
            with ExitStack() as at:
                def sbt(name, shape, dt=F32):
                    return at.enter_context(nc.sbuf_tensor(f"{name}{layer}", shape, dt))

                def s_(name):
                    return at.enter_context(nc.semaphore(f"{name}{layer}"))

                UNITS = H if L1 else 4
                PER = H // UNITS
                NCH = H * D1 // P if L1 else 1
                VW = D1 if L1 else 32
                AHEAD = 4
                NP = 8
                LOS = 2 if L1 else 4

                TURN = 8
                BIAS = 4
                EXP = 3
                LAG = 2
                PTB = 4
                OUTS = ((3, (0, 1)), (6, (2, 3))) if L1 else ((3, (0, 1, 2, 3)),)
                V_SLOTS = (18, 22, 26, 30, 42, 46, 50, 54) if L1 else (18, 42)
                XB_SLOT = 54 if L1 else 40
                NV = len(V_SLOTS)
                NO = len(OUTS)
                GROUP = 2 * NT if L1 else SLOTS
                OEV = SLOTS // GROUP
                SUMS = 2 * NT if L1 else PER * NT
                HG = GROUP // NT
                HR = P // HG
                R_T, R_Q, R_K, R_S, R_D, R_TOP, R_PEN = 9, 10, 11, 12, 16, 20, 59
                R_ADJ = SLOTS - BIAS
                NB = 3 + 2 * NT if L1 else 1

                st = sbt("st", [P, T, 6])
                mv = sbt("mv", [P, T, 2])
                ve = sbt("ve", [P, T])
                sd = sbt("sd", [P, T])
                rs = sbt("rs", [P, T])
                xn = sbt("xn", [P, NT, C])
                wq = sbt("wq", [P, UNITS, P])
                wk = sbt("wk", [P, UNITS, P])
                wv = sbt("wv", [P, H * D1 if L1 else C])
                wo = sbt("wo", [P, NCH, C])
                xb_next = sbt("xb_next", [P, N])
                xb = sbt("xb", [P, N])
                q_full = sbt("q_full", [P, N])
                k_full = sbt("k_full", [P, N])
                q_hi = sbt("q_hi", [P, 2, N], F32R)
                q_lo = sbt("q_lo", [P, 2, N], F32R) if L1 else None
                k_st = sbt("k_st", [P, 2, N], F32R)
                q_head = None if L1 else sbt("q_head", [P, 2, N], F32R)
                v_st = sbt("v_st", [P, NT, H * VW])
                probs = sbt("probs", [P, NP, N])
                rowmin = sbt("rowmin", [P, NP])
                rsum = sbt("rsum", [P, 2 * SUMS])
                rinv = sbt("rinv", [P, NT, HG])
                rinv_wide = sbt("rinv_wide", [P, NT, P])
                rb = sbt("spread_inv", [P, N])
                pt = sbt("pt", [P, PTB, N])
                yt = sbt("yt", [P, NCH, N])
                if L1:
                    adj = sbt("adj", [P, TOT])
                    rq_full = sbt("rq_full", [P, N])
                    rk_full = sbt("rk_full", [P, N])
                    rq_hi = sbt("rq_hi", [P, N], F32R)
                    rq_lo = sbt("rq_lo", [P, N], F32R)
                    rk_st = sbt("rk_st", [P, N], F32R)
                    rl = sbt("relu", [P, NT, N])
                    w0 = sbt("w0", [P, NT, N + 8])
                    w1 = sbt("w1", [P, NT, N + 8])
                    top = sbt("top", [P, NT, 8])
                    KEEP = max(1, int(N * 0.2)) - 1
                    PAD = -KEEP % 8
                    ROUNDS = (KEEP + PAD) // 8

                s_bank = banks[0:2]
                t_bank = banks[2:4]
                turn_bank = banks[4]
                n_bank = banks[5]
                o_bank = banks[6:8] if L1 else [banks[6]]

                w_loaded = s_("w_loaded")
                preset = s_("preset")
                dve_step = s_("dve_step")
                var_ready = s_("var_ready")
                root_ready = s_("root_ready")
                xn_ready = s_("xn_ready")
                n_filled = s_("n_filled")
                n_read = s_("n_read")
                xb_ready = s_("xb_ready")
                v_proj = s_("v_proj")
                v_ready = s_("v_ready")
                q_proj = s_("q_proj")
                k_proj = s_("k_proj")
                q_copied = s_("q_copied")
                k_copied = s_("k_copied")
                q_rounded = s_("q_rounded")
                k_rounded = s_("k_rounded")
                lo_ready = s_("lo_ready")
                head_ready = s_("head_ready")
                scores = s_("scores")
                biased = s_("biased")
                exped = s_("exped")
                transposed = s_("transposed")
                pt_act = s_("pt_act")
                pt_dve = s_("pt_dve")
                pv_done = s_("pv_done")
                inverted = s_("inverted")
                widened = s_("widened")
                spread = s_("spread")
                spread_copied = s_("spread_copied")
                o_ready = s_("o_ready")
                out_proj = s_("out_proj")
                x_ready = s_("x_ready")
                rank_q = s_("rank_q")
                rank_k = s_("rank_k")
                rank_lo = s_("rank_lo")
                relu_ready = s_("relu_ready")

                from_one = {s.name for s in (pv_done, spread, spread_copied, inverted, o_ready, out_proj, x_ready)}

                def need(eng, sem, value):
                    if isinstance(value, int) and value <= 0:
                        return
                    eng.wait_ge(sem, value + (sem.name in from_one))

                def start(eng, sems):
                    for sem in sems:
                        eng.sem_inc(sem, 1)

                def unit_at(s):
                    h, i = divmod(s, NT)
                    if i or h % PER:
                        return None
                    return h // PER + (2 if L1 else 1)

                def outs_before(b, s):
                    return (b + s // SLOTS - 1) * NO + sum(o < s % SLOTS for o, _ in OUTS)

                def values_before(b, s):
                    n = (b + s // SLOTS) * NV + NV // 2 + sum(v < s % SLOTS for v in V_SLOTS)
                    return min(n, B * NV) if isinstance(n, int) else n

                def copied_by_dve(m):
                    return m % NT in () if L1 else m % NT == 3

                def pt_wait(eng, b, m):
                    h, i = divmod(m, NT)
                    per = sum(copied_by_dve(j) for j in range(NT))
                    by_dve = sum(copied_by_dve(j) for j in range(i + 1))
                    if copied_by_dve(m):
                        need(eng, pt_dve, (b * H + h) * per + by_dve)
                    else:
                        need(eng, pt_act, (b * H + h) * (NT - per) + i + 1 - by_dve)

                def turn_free(pe, b, s):
                    need(pe, x_ready, outs_before(b, s))
                    need(pe, v_ready, values_before(b, s))

                def pe_q(pe, b, u):
                    if not L1 or u % UNITS == 0:
                        need(pe, xb_ready, b + u // UNITS + 1)
                    need(pe, k_copied, b * UNITS + u)
                    pe.matmul(turn_bank[:], wq[:, u % UNITS, :], xb[:], start=True, stop=True).then_inc(q_proj, 1)

                def pe_k(pe, b, u):
                    need(pe, q_copied, b * UNITS + u + 1)
                    pe.matmul(turn_bank[:], wk[:, u % UNITS, :], xb[:], start=True, stop=True).then_inc(k_proj, 1)

                def pe_value(pe, n, j, units):
                    need(pe, k_copied, units)
                    need(pe, v_ready, n * NV + j)
                    if j < NV // 2:
                        need(pe, n_read, n * NB + 1)
                        src = xb_next
                    else:
                        need(pe, xb_ready, n + 1)
                        src = xb
                    if L1:
                        half, kb = divmod(j, NT)
                        mm = pe.matmul(turn_bank[:], src[:, kb * P:(kb + 1) * P],
                                       wv[:, half * 512:(half + 1) * 512], start=True, stop=True)
                    else:
                        for kb in range(NT):
                            mm = pe.matmul(turn_bank[:, kb * P:(kb + 1) * P], src[:, kb * P:(kb + 1) * P],
                                           wv[:], start=True, stop=True)
                    mm.then_inc(v_proj, 1)

                def pe_out(pe, n, part):
                    _, tiles = OUTS[part]
                    need(pe, o_ready, (n + 1) * OEV)
                    need(pe, x_ready, n * NO + part)
                    if not (isinstance(n, int) and n == B - 1):
                        need(pe, k_copied, n * UNITS + unit_after(SLOTS + OUTS[part][0]))
                    for i in tiles:
                        for ch in range(NCH):
                            mm = pe.matmul(turn_bank[:, i * P:(i + 1) * P], yt[:, ch, i * P:(i + 1) * P],
                                           wo[:, ch, :], start=(ch == 0), stop=(ch == NCH - 1))
                    mm.then_inc(out_proj, 1)

                def pe_next_x(pe, n):
                    need(pe, xn_ready, n + 1)
                    need(pe, n_read, n * NB)
                    for i in range(NT):
                        mm = pe.transpose(n_bank[:, i * P:(i + 1) * P], xn[:, i, :], ident[:])
                    mm.then_inc(n_filled, 1)

                def pe_rank_unit(pe, n, k):
                    need(pe, n_read, n * NB + k)
                    w = wq if k == 1 else wk
                    pe.matmul(n_bank[:], w[:, 0, :], xb_next[:], start=True, stop=True).then_inc(n_filled, 1)

                def pe_rank_scores(pe, n, i):
                    need(pe, n_read, n * NB + 3 + i)
                    if i == 0:
                        need(pe, rank_lo, 2 * n + 2)
                    K, rows = P * (i + 1), slice(i * P, (i + 1) * P)
                    pe.matmul(n_bank[:, 0:K], rq_hi[:, rows], rk_st[:, 0:K], start=True, stop=False)
                    pe.matmul(n_bank[:, 0:K], rq_lo[:, rows], rk_st[:, 0:K], start=False, stop=True)\
                        .then_inc(n_filled, 1)

                def pe_decay(pe, n, i):
                    need(pe, n_read, n * NB + 3 + NT + i)
                    need(pe, relu_ready, n * NT + i + 1)
                    diag = slice(P * i, P * (i + 1))
                    mm = pe.matmul(n_bank[:, diag], strict[:], rl[:, i, diag], start=True, stop=True)
                    if i:
                        pe.matmul(n_bank[:, 0:P * i], strict[:], rl[:, i, 0:P * i], start=True, stop=False,
                                  skip_group_check=True)
                    for r in range(i):
                        mm = pe.matmul(n_bank[:, 0:P * (r + 1)], ones[:], rl[:, r, 0:P * (r + 1)],
                                       start=False, stop=(r == i - 1), skip_group_check=True)
                    mm.then_inc(n_filled, 1)

                def pe_score(pe, b, m):
                    h, i = divmod(m, NT)
                    u = h // PER
                    K = P * (i + 1)
                    dst = s_bank[m % 2][:, 0:K]
                    rows = slice(i * P, (i + 1) * P)
                    need(pe, biased, b * SLOTS + m - 1)
                    if i == 0:
                        need(pe, lo_ready, b * UNITS * LOS + LOS * (u + 1))
                    if L1:
                        pe.matmul(dst, q_hi[:, u % 2, rows], k_st[:, u % 2, 0:K], start=True, stop=False)
                        mm = pe.matmul(dst, q_lo[:, u % 2, rows], k_st[:, u % 2, 0:K], start=False, stop=True)
                    else:
                        if i == 0:
                            need(pe, head_ready, b * H + h + 1)
                        mm = pe.matmul(dst, q_head[:, h % 2, rows], k_st[:, u % 2, 0:K], start=True, stop=True)
                    mm.then_inc(scores, 1)

                def pe_transpose(pe, b, s):
                    need(pe, exped, b * SLOTS + s + 1)
                    pt_wait(pe, b, s - 2)
                    for kb in range(s % NT + 1):
                        mm = pe.transpose(t_bank[s % 2][:, kb * P:(kb + 1) * P],
                                          probs[:, s % NP, kb * P:(kb + 1) * P], ident[:])
                    mm.then_inc(transposed, 1)

                def pe_spread(pe, b, n):
                    need(pe, widened, b * OEV + n + 1)
                    need(pe, spread_copied, b * OEV + n)
                    need(pe, o_ready, b * OEV + n)
                    bank = o_bank[(n + 1) % 2] if L1 else banks[7]
                    for i in range(NT):
                        mm = pe.transpose(bank[:, i * P:(i + 1) * P], rinv_wide[:, i, :], ident[:])
                    mm.then_inc(spread, 1)

                def pe_pv(pe, b, s):
                    h, i = divmod(s % SLOTS, NT)
                    pt_wait(pe, b, s)
                    if s % SLOTS == 0:
                        need(pe, v_ready, (b + s // SLOTS) * NV + NV // 2)
                    if s % SLOTS == SLOTS // 2:
                        need(pe, v_ready, (b + 1) * NV)
                    if s % GROUP == 0:
                        need(pe, o_ready, b * OEV + s // GROUP - (1 if L1 else 0))
                        if L1:
                            need(pe, spread_copied, b * OEV + s // GROUP)
                    bank = o_bank[s // GROUP % 2] if L1 else o_bank[0]
                    row = (h % 2) * D1 if L1 else 32 * (h // 4)
                    for kb in range(i + 1):
                        first = kb == 0 and (L1 or (i == 0 and h % 4 == 0))
                        last = kb == i and (L1 or h % 4 == 3)
                        mm = pe.matmul(bank[row:row + VW, i * P:(i + 1) * P],
                                       v_st[:, kb, h * VW:(h + 1) * VW],
                                       pt[:, s % PTB, kb * P:(kb + 1) * P],
                                       start=first, stop=last, skip_group_check=True)
                    mm.then_inc(pv_done, 1)

                def pe_slots(pe, b, slots, last):
                    for s in slots:
                        if s < SLOTS and not last and s >= TURN:
                            if s == R_T:
                                pe_next_x(pe, b + 1)
                            if L1 and s == R_Q:
                                pe_rank_unit(pe, b + 1, 1)
                            if L1 and s == R_K:
                                pe_rank_unit(pe, b + 1, 2)
                            if L1 and R_S <= s < R_S + NT:
                                pe_rank_scores(pe, b + 1, s - R_S)
                            if L1 and R_D <= s < R_D + NT:
                                pe_decay(pe, b + 1, s - R_D)
                        if s + AHEAD < SLOTS or not last:
                            pe_score(pe, b, s + AHEAD)
                        if 0 <= s and (s < SLOTS or not last):
                            pe_transpose(pe, b, s)
                        if s >= LAG and (s - LAG < SLOTS or not last):
                            pe_pv(pe, b, s - LAG)
                        if s >= 0 and s % GROUP == GROUP - 1 and (s < SLOTS or not last):
                            pe_spread(pe, b, s // GROUP)
                        for k, product in ((0, pe_q), (1, pe_k)):
                            u = unit_at(s - k)
                            if s >= k and u is not None and (u < UNITS or not last):
                                if k == 0:
                                    turn_free(pe, b, s)
                                product(pe, b, u)
                        if s in V_SLOTS:
                            j = V_SLOTS.index(s)
                            if j < NV // 2:
                                pe_value(pe, b, j + NV // 2, b * UNITS + min(unit_after(s), UNITS if last else 99))
                            elif not last:
                                pe_value(pe, b + 1, j - NV // 2, b * UNITS + unit_after(s))
                        for part, (o, _) in enumerate(OUTS):
                            if s == SLOTS + o:
                                pe_out(pe, b, part)

                def unit_after(s):
                    h = s // NT
                    return h // PER + (2 if L1 else 1) + 1

                def pe_program(pe):
                    start(pe, (pv_done, spread, out_proj))
                    pe.wait_ge(w_loaded, 64)
                    pe_next_x(pe, 0)
                    if L1:
                        pe_rank_unit(pe, 0, 1)
                        pe_rank_unit(pe, 0, 2)
                        for i in range(NT):
                            pe_rank_scores(pe, 0, i)
                        for i in range(NT):
                            pe_decay(pe, 0, i)
                    for u in range(unit_at(0)):
                        pe_q(pe, 0, u)
                        pe_k(pe, 0, u)
                    for j in range(NV // 2):
                        pe_value(pe, 0, j, unit_at(0))
                    pe_slots(pe, 0, range(-AHEAD, TURN), False)
                    with pe.Fori(0, B - 1) as b:
                        pe_slots(pe, b, range(TURN, SLOTS + TURN), False)
                    pe_slots(pe, B - 1, range(TURN, SLOTS + TURN), True)

                def dve_stats(dve, c):
                    for t in range(T):
                        c.inc(dve.bn_stats(st[:, t, :], x_tok[:, t, :]))
                    c.wait()
                    for t in range(T):
                        c.inc(dve.bn_aggr(mv[:, t, :], st[:, t, :]))
                    c.wait()
                    dve.tensor_scalar(ve[:], mv[:, :, 1], EPS, None, ALU.add).then_inc(var_ready, 1)
                    dve.wait_ge(root_ready, 1)
                    c.inc(dve.reciprocal(rs[:], sd[:]))
                    c.wait()

                def dve_norm(dve, n):
                    need(dve, n_filled, (n - 1) * NB + 1)
                    for i in range(NT):
                        t = bass.ds(n * NT + i, 1)
                        ins = dve.tensor_scalar(xn[:, i, :], x_tok[:, t, :].rearrange("p a c -> p (a c)"),
                                                mv[:, t, 0:1].rearrange("p a c -> p (a c)"), rs[:, t],
                                                ALU.subtract, ALU.mult)
                    ins.then_inc(xn_ready, 1)

                def dve_relu(dve, c, n, i):
                    K = P * (i + 1)
                    need(dve, n_filled, n * NB + 4 + i)
                    dve.scalar_tensor_tensor(out=rl[:, i, 0:K], in0=n_bank[:, 0:K], scalar=0.0,
                                             in1=rneg[:, N - K:N], op0=ALU.min, op1=ALU.mult).then_inc(n_read, 1)
                    need(dve, n_read, n * NB + 4 + i)
                    dve.memset(rl[:, i, 0:1], 0.0).then_inc(relu_ready, 1)

                def dve_decay(dve, c, n, i):
                    K = P * (i + 1)
                    need(dve, n_filled, n * NB + 4 + NT + i)
                    dve.scalar_tensor_tensor(out=w0[:, i, 0:K], in0=n_bank[:, 0:K], scalar=-1.0,
                                             in1=causal[:, N - K:N], op0=ALU.mult, op1=ALU.add).then_inc(n_read, 1)

                RANKING = [(r, i, take) for r in range(ROUNDS) for take in (False, True)
                           for i in range(NT)] if L1 else []

                def dve_rank(dve, c, k):
                    r, i, take = RANKING[k]
                    src = w0 if r == 0 else w1
                    W = P * (i + 1) + PAD
                    if r or take:
                        c.wait(c.ranked[i])
                        apart(dve, passed)
                    if take:
                        c.inc(dve.match_replace(out=w1[:, i, 0:W], in_to_replace=top[:, i, :],
                                                in_values=src[:, i, 0:W], imm_value=TAKEN))
                    else:
                        c.inc(dve.max(top[:, i, :], src[:, i, 0:W]))
                    c.ranked[i] = c.n

                def dve_penalty(dve, c):
                    c.wait()
                    for i in range(NT):
                        K = P * (i + 1)
                        c.inc(dve.tensor_scalar(w1[:, i, 0:K], w1[:, i, 0:K], TAKEN / 2, MASKED, ALU.is_gt, ALU.mult))
                    c.wait()
                    for i in range(NT):
                        blk = w1[:, i, P * i:P * (i + 1)]
                        c.inc(dve.tensor_tensor(blk, blk, notdiag[:], ALU.mult))

                def dve_adj(dve, c, n):
                    need(dve, biased, n * SLOTS)
                    apart(dve, passed)
                    c.wait()
                    for i in range(NT):
                        K = P * (i + 1)
                        c.inc(dve.tensor_tensor(adj[:, OFF[i]:OFF[i] + K], w1[:, i, 0:K], w0[:, i, 0:K], ALU.subtract))
                    c.wait()

                RANK_STEPS = ROUNDS * 2 * NT + 3 * NT if L1 else 0

                def dve_value(dve, n, j):
                    half = j // (NV // 2)
                    need(dve, pv_done, n * SLOTS - (0 if half else SLOTS // 2))
                    need(dve, v_proj, n * NV + j + 1)
                    if L1:
                        kb = j % NT
                        cols = slice(half * 512, (half + 1) * 512)
                        dve.tensor_tensor(v_st[:, kb, cols], turn_bank[:], bv1[:, cols], ALU.add).then_inc(v_ready, 1)
                    else:
                        g = slice(2 * half, 2 * half + 2)
                        for i in range(4):
                            dst = v_st[:].rearrange("p k (g j c) -> p k g j c", g=4, j=4)[:, :, g, i, 8 * i:8 * i + 8]
                            src = turn_bank[:].rearrange("p (k g j d) -> p k g j d", k=NT, g=4, j=4)[:, :, g, i, :]
                            ins = dve.tensor_copy(dst, src)
                        ins.then_inc(v_ready, 1)

                def dve_round(dve, b, u):
                    need(dve, q_copied, b * UNITS + u + 1)
                    need(dve, scores, b * SLOTS + (u - 1) * PER * NT)
                    dve.tensor_copy(q_hi[:, u % 2, :], q_full[:]).then_inc(q_rounded, 1)

                def dve_head(dve, b, h):
                    need(dve, lo_ready, (b * UNITS + h // PER + 1) * LOS)
                    need(dve, scores, b * SLOTS + (h - 1) * NT)
                    dve.tensor_scalar(q_head[:, h % 2, :], q_hi[:, h // PER % 2, :].bitcast(F32),
                                      headrow[:, h % PER:h % PER + 1], None, ALU.mult).then_inc(head_ready, 1)

                def dve_bias(dve, b, m):
                    K = P * (m % NT + 1)
                    k = m % NP
                    need(dve, scores, b * SLOTS + m + 1)
                    need(dve, transposed, b * SLOTS + m - NP + 1)
                    apart(dve, passed)
                    bias = adj[:, OFF[m % NT]:OFF[m % NT] + K] if L1 else pen0[:, N - K:N]
                    dve.tensor_tensor_reduce(probs[:, k, 0:K], s_bank[m % 2][:, 0:K], bias, 1.0, FLOOR,
                                             ALU.add, ALU.min, rowmin[:, k:k + 1]).then_inc(biased, 1)

                def dve_copy(dve, b, s):
                    K = P * (s % NT + 1)
                    need(dve, transposed, b * SLOTS + s + 1)
                    need(dve, pv_done, b * SLOTS + s + 1 - PTB)
                    dve.tensor_copy(pt[:, s % PTB, 0:K], t_bank[s % 2][:, 0:K]).then_inc(pt_dve, 1)

                def dve_invert(dve, c, b, g):
                    need(dve, exped, b * SLOTS + (g + 1) * SUMS)
                    src = rsum[:, (g % 2) * SUMS:(g % 2 + 1) * SUMS]
                    if L1:
                        need(dve, spread, b * OEV + g)
                        dst = rinv[:]
                    else:
                        need(dve, spread, b * OEV)
                        c.inc(dve.tensor_scalar(src, src, 0.5, None, ALU.max))
                        c.wait()
                        dst = rinv[:, :, g * PER:(g + 1) * PER]
                    dve.reciprocal(dst, src.rearrange("p (h i) -> p i h", i=NT)).then_inc(inverted, 1)
                    if (g + 1) * SUMS % GROUP == 0:
                        need(dve, inverted, b * (SLOTS // SUMS) + g + 1)
                        dve.tensor_copy(rinv_wide[:].rearrange("p i (h r) -> p i h r", r=HR),
                                        rinv[:].unsqueeze(3).to_broadcast([P, NT, HG, HR])).then_inc(widened, 1)

                def dve_outputs(dve, b, n):
                    need(dve, pv_done, b * SLOTS + (n + 1) * GROUP)
                    need(dve, spread_copied, b * OEV + n + 1)
                    need(dve, out_proj, b * NO)
                    dve.tensor_tensor(yt[:, n, :], o_bank[n % len(o_bank)][:], rb[:], ALU.mult).then_inc(o_ready, 1)

                def dve_add(dve, c, n, part):
                    _, tiles = OUTS[part]
                    need(dve, out_proj, n * NO + part + 1)
                    k = len(tiles)
                    xs = x_tok[:, bass.ds(n * NT + tiles[0], k), :]
                    o = turn_bank[:, tiles[0] * P:(tiles[-1] + 1) * P].rearrange("p (t c) -> p t c", c=C)
                    c.inc(dve.tensor_tensor(xs, xs, o, ALU.add))
                    c.wait()
                    bo = bo1 if L1 else bo0
                    dve.tensor_tensor(xs, xs, bo[:].unsqueeze(1).to_broadcast([P, k, C]), ALU.add).then_inc(x_ready, 1)

                def dve_slots(dve, c, b, slots, last):
                    for s in slots:
                        for part, (o, _) in enumerate(OUTS):
                            if s == SLOTS + o + 1:
                                dve_add(dve, c, b, part)
                        if not last and L1 and s == R_ADJ:
                            dve_adj(dve, c, b + 1)
                        if s + BIAS >= 0 and (s + BIAS < SLOTS or not last):
                            dve_bias(dve, b, s + BIAS)
                        if s == TURN and not last:
                            dve_norm(dve, b + 1)
                        u = unit_at(s - 1)
                        if s >= 1 and u is not None and (u < UNITS or not last):
                            dve_round(dve, b, u)
                        if not L1 and s >= 0 and s % NT == 1 and (s // NT + 2 < H or not last):
                            dve_head(dve, b, s // NT + 2)
                        if s >= 0 and copied_by_dve(s) and (s < SLOTS or not last):
                            dve_copy(dve, b, s)
                        if s >= GROUP and s % GROUP == LAG:
                            dve_outputs(dve, b, s // GROUP - 1)
                        if s - 1 in V_SLOTS:
                            j = V_SLOTS.index(s - 1)
                            if j < NV // 2:
                                dve_value(dve, b, j + NV // 2)
                            elif not last:
                                dve_value(dve, b + 1, j - NV // 2)
                        if 0 <= s < SLOTS and s % SUMS == SUMS - 2:
                            dve_invert(dve, c, b, s // SUMS)
                        if s >= SLOTS and s % SUMS == SUMS - 2 and not last:
                            dve_invert(dve, c, b + 1, s % SLOTS // SUMS)
                        if not last and L1 and s >= TURN:
                            if R_S <= s < R_S + NT:
                                dve_relu(dve, c, b + 1, s - R_S)
                            if R_D <= s < R_D + NT:
                                dve_decay(dve, c, b + 1, s - R_D)
                            if s == R_TOP:
                                need(dve, n_read, (b + 2) * NB)
                                apart(dve, passed)
                            for k in range(len(RANKING)):
                                if s == R_TOP + k * (R_PEN - R_TOP) // len(RANKING):
                                    dve_rank(dve, c, k)
                            if s == R_PEN:
                                dve_penalty(dve, c)

                def dve_program(dve):
                    start(dve, (x_ready, o_ready, inverted))
                    if L1:
                        for i in range(NT):
                            K = P * (i + 1)
                            dve.memset(w0[:, i, K:K + PAD], SENTINEL).then_inc(preset, 1)
                        dve.wait_ge(preset, NT)
                    else:
                        dve.wait_ge(x_loaded, 64)
                        dve.memset(v_st[:], 0.0).then_inc(preset, 1)
                        dve.wait_ge(preset, 1)
                    head = 2 * T + 1 + RANK_STEPS
                    c = Steps(dve, dve_step, 0, head)
                    dve_stats(dve, c)
                    dve_norm(dve, 0)
                    if L1:
                        for i in range(NT):
                            dve_relu(dve, c, 0, i)
                        for i in range(NT):
                            dve_decay(dve, c, 0, i)
                    for u in range(unit_at(0)):
                        dve_round(dve, 0, u)
                    if not L1:
                        dve_head(dve, 0, 0)
                        dve_head(dve, 0, 1)
                    for j in range(NV // 2):
                        dve_value(dve, 0, j)
                    if L1:
                        need(dve, n_read, NB)
                        apart(dve, passed)
                        for k in range(len(RANKING)):
                            dve_rank(dve, c, k)
                        dve_penalty(dve, c)
                        dve_adj(dve, c, 0)
                    dve_slots(dve, c, 0, range(-AHEAD, TURN), False)
                    c.close()
                    tail = NO + (0 if L1 else SLOTS // SUMS)
                    per = RANK_STEPS + tail
                    slots = range(TURN, SLOTS + TURN)
                    with dve.Fori(0, B - 1) as b:
                        c = Steps(dve, dve_step, b, per, head)
                        dve_slots(dve, c, b, slots, False)
                        c.close()
                    c = Steps(dve, dve_step, B - 1, tail, head, per)
                    dve_slots(dve, c, B - 1, slots, True)
                    c.close()

                def act_next_x(act, n):
                    need(act, n_filled, n * NB + 1)
                    need(act, v_proj, n * NV - NV // 2)
                    need(act, xb_ready, n)
                    act.activation(xb_next[:], n_bank[:], ACT.Copy).then_inc(n_read, 1)

                def act_rank_q(act, n):
                    need(act, n_filled, n * NB + 2)
                    act.activation(rq_full[:], n_bank[:], ACT.Identity, bias=bqs[:, 0:1],
                                   scale=-1.0 / math.sqrt(D1)).then_inc(n_read, 1)
                    need(act, n_read, n * NB + 2)
                    act.activation(rq_hi[:], rq_full[:], ACT.Copy).then_inc(rank_q, 1)

                def act_rank_k(act, n):
                    need(act, n_filled, n * NB + 3)
                    act.activation(rk_full[:], n_bank[:], ACT.Identity, bias=bqk_in[:, 1, 0:1]).then_inc(n_read, 1)
                    need(act, n_read, n * NB + 3)
                    act.activation(rk_st[:], rk_full[:], ACT.Copy).then_inc(rank_k, 1)

                def act_q(act, b, u):
                    g = b * UNITS + u
                    need(act, q_proj, g + 1)
                    need(act, lo_ready, g * LOS)
                    if L1:
                        act.activation(q_full[:], turn_bank[:], ACT.Identity, bias=bqs[:, u % UNITS:u % UNITS + 1],
                                       scale=-1.0 / math.sqrt(D1)).then_inc(q_copied, 1)
                    else:
                        act.activation(q_full[:], turn_bank[:], ACT.Copy,
                                       scale=scale0[:, u % UNITS:u % UNITS + 1]).then_inc(q_copied, 1)

                def act_k(act, b, u):
                    g = b * UNITS + u
                    need(act, k_proj, g + 1)
                    if L1:
                        act.activation(k_full[:], turn_bank[:], ACT.Identity,
                                       bias=bqk_in[:, 1, u % UNITS:u % UNITS + 1]).then_inc(k_copied, 1)
                    else:
                        act.activation(k_full[:], turn_bank[:], ACT.Copy).then_inc(k_copied, 1)
                    need(act, k_copied, g + 1)
                    need(act, scores, b * SLOTS + (u - 1) * PER * NT)
                    act.activation(k_st[:, u % 2, :], k_full[:], ACT.Copy).then_inc(k_rounded, 1)

                def act_exp(act, b, m):
                    K = P * (m % NT + 1)
                    k, r = m % NP, m % (2 * SUMS)
                    need(act, biased, b * SLOTS + m + 1)
                    if m % SUMS == 0:
                        need(act, inverted, b * (SLOTS // SUMS) + m // SUMS - 1)
                    act.activation(probs[:, k, 0:K], probs[:, k, 0:K], ACT.Exp, bias=rowmin[:, k:k + 1],
                                   scale=-1.0, accum_out=rsum[:, r:r + 1]).then_inc(exped, 1)

                def act_copy(act, b, s):
                    K = P * (s % NT + 1)
                    need(act, transposed, b * SLOTS + s + 1)
                    need(act, pv_done, b * SLOTS + s + 1 - PTB)
                    act.activation(pt[:, s % PTB, 0:K], t_bank[s % 2][:, 0:K], ACT.Copy).then_inc(pt_act, 1)

                def act_spread(act, b, n):
                    need(act, spread, b * OEV + n + 1)
                    need(act, o_ready, b * OEV + n)
                    bank = o_bank[(n + 1) % 2] if L1 else banks[7]
                    act.activation(rb[:], bank[:], ACT.Copy).then_inc(spread_copied, 1)

                def act_slots(act, b, slots, last):
                    for s in slots:
                        if not last and s >= TURN:
                            if s == R_T:
                                act_next_x(act, b + 1)
                            if L1 and s == R_Q:
                                act_rank_q(act, b + 1)
                            if L1 and s == R_K:
                                act_rank_k(act, b + 1)
                        for k, step in ((1, act_q), (2, act_k)):
                            u = unit_at(s - k)
                            if s >= k and u is not None and (u < UNITS or not last):
                                step(act, b, u)
                        if s + EXP >= 0 and (s + EXP < SLOTS or not last):
                            act_exp(act, b, s + EXP)
                        if s >= 0 and not copied_by_dve(s) and (s < SLOTS or not last):
                            act_copy(act, b, s)
                        if s >= 0 and s % GROUP == GROUP - 1 and (s < SLOTS or not last):
                            act_spread(act, b, s // GROUP)

                def act_program(act):
                    start(act, (spread_copied,))
                    need(act, var_ready, 1)
                    act.activation(sd[:], ve[:], ACT.Sqrt).then_inc(root_ready, 1)
                    act_next_x(act, 0)
                    if L1:
                        act_rank_q(act, 0)
                        act_rank_k(act, 0)
                    for u in range(unit_at(0)):
                        act_q(act, 0, u)
                        act_k(act, 0, u)
                    act_slots(act, 0, range(-AHEAD, TURN), False)
                    with act.Fori(0, B - 1) as b:
                        act_slots(act, b, range(TURN, SLOTS + TURN), False)
                    act_slots(act, B - 1, range(TURN, SLOTS + TURN), True)

                def pool_xb(pool, n):
                    need(pool, n_read, n * NB + 1)
                    need(pool, k_proj, n * UNITS)
                    need(pool, v_proj, n * NV)
                    apart(pool, passed)
                    pool.tensor_copy(xb[:], xb_next[:]).then_inc(xb_ready, 1)
                    need(pool, xb_ready, n + 1)

                def pool_rank_lo(pool, n):
                    need(pool, rank_q, n + 1)
                    pool.tensor_tensor(rq_lo[:], rq_full[:], rq_hi[:].bitcast(F32), ALU.subtract).then_inc(rank_lo, 1)
                    need(pool, rank_lo, 2 * n + 1)
                    need(pool, rank_k, n + 1)
                    pool.tensor_tensor(rk_st[64:P, :], rk_full[64:P, :], rk_st[64:P, :].bitcast(F32),
                                       ALU.subtract).then_inc(rank_lo, 1)
                    need(pool, rank_lo, 2 * n + 2)

                def pool_unit(pool, b, u):
                    lo = (b * UNITS + u) * LOS
                    k = u % 2
                    need(pool, q_rounded, b * UNITS + u + 1)
                    if L1:
                        pool.tensor_tensor(q_lo[:, k, :], q_full[:], q_hi[:, k, :].bitcast(F32),
                                           ALU.subtract).then_inc(lo_ready, 1)
                    else:
                        pool.tensor_tensor(q_hi[64:P, k, :], q_full[64:P, :], q_hi[64:P, k, :].bitcast(F32),
                                           ALU.subtract).then_inc(lo_ready, 1)
                    need(pool, k_rounded, b * UNITS + u + 1)
                    for n, rows in enumerate([slice(64, P)] if L1 else [slice(32, 64), slice(96, P)]):
                        need(pool, lo_ready, lo + n + 1)
                        pool.tensor_tensor(k_st[rows, k, :], k_full[rows, :], k_st[rows, k, :].bitcast(F32),
                                           ALU.subtract).then_inc(lo_ready, 1 + n)
                    need(pool, lo_ready, lo + LOS)

                def pool_slots(pool, b, slots, last):
                    for s in slots:
                        if not last and s >= TURN:
                            if L1 and s == R_K:
                                pool_rank_lo(pool, b + 1)
                            if s == XB_SLOT:
                                pool_xb(pool, b + 1)
                        u = unit_at(s)
                        if s >= 0 and u is not None and (u < UNITS or not last):
                            pool_unit(pool, b, u)

                def pool_program(pool):
                    pool_xb(pool, 0)
                    if L1:
                        pool_rank_lo(pool, 0)
                    for u in range(unit_at(0)):
                        pool_unit(pool, 0, u)
                    pool_slots(pool, 0, range(0, TURN), False)
                    with pool.Fori(0, B - 1) as b:
                        pool_slots(pool, b, range(TURN, SLOTS + TURN), False)
                    pool_slots(pool, B - 1, range(TURN, SLOTS + TURN), True)

                with nc.Block() as block:
                    @block.sync
                    def _(sp):
                        for dst, name in ((wq, "wq"), (wk, "wk"), (wv, "wv"), (wo, "wo")):
                            sp.dma_start(dst[:], a[f"{name}{layer}"]).then_inc(w_loaded, 16)
                        sp.wait_ge(w_loaded, 64)

                    @block.tensor
                    def _(pe):
                        pe_program(pe)

                    @block.vector
                    def _(dve):
                        dve_program(dve)

                    @block.scalar
                    def _(act):
                        act_program(act)

                    @block.gpsimd
                    def _(pool):
                        pool_program(pool)

        def experts(layer):
            E, I, TOPK = (E0, I0, 4) if layer == 0 else (E1, I1, 1)
            rw = rw0 if layer == 0 else rw1
            b1t = b1t0 if layer == 0 else b1t1
            b2s = b2s0 if layer == 0 else b2s1
            func = ACT.Gelu if layer == 0 else ACT.Relu
            NF = I // P
            PADW = 8 - TOPK
            RW = E + PADW
            CH = T * P // 512
            TC = T // CH
            w1d, w2d = a[f"w1_{layer}"], a[f"w2_{layer}"]
            with ExitStack() as at:
                def sbt(name, shape, dt=F32):
                    return at.enter_context(nc.sbuf_tensor(f"m{layer}_{name}", shape, dt))

                def s_(name):
                    return at.enter_context(nc.semaphore(f"m{layer}_{name}"))

                st = sbt("st", [P, T, 6])
                mv = sbt("mv", [P, T, 2])
                ve = sbt("ve", [P, T])
                sd = sbt("sd", [P, T])
                rs = sbt("rs", [P, T])
                xn = sbt("xn", [P, T, C])
                xt = sbt("xt", [P, T * P])
                xt_hi = sbt("xt_hi", [P, T * P], F32R)
                xt_lo = sbt("xt_lo", [P, T * P], F32R)
                lg = sbt("lg", [P, T, E])
                mx = sbt("mx", [P, T])
                pr = sbt("pr", [P, T, RW])
                pk = sbt("pk", [P, T, RW])
                top = sbt("top", [P, T, 8])
                sm = sbt("sm", [P, T])
                comb = sbt("comb", [P, T, E])
                combT = sbt("combT", [E, T * P])
                w1s = sbt("w1s", [P, 2, I])
                w2s = sbt("w2s", [P, 2, NF, C])
                w1_hi = sbt("w1_hi", [P, 2, I], F32R)
                w1_lo = sbt("w1_lo", [P, 2, I], F32R)
                w2_hi = sbt("w2_hi", [P, 2, NF, C], F32R)
                w2_lo = sbt("w2_lo", [P, 2, NF, C], F32R)
                hid = sbt("hid", [P, 2, NF, 512])
                hid_hi = sbt("hid_hi", [P, 2, NF, 512], F32R)
                hid_lo = sbt("hid_lo", [P, 2, NF, 512], F32R)

                norm_step = s_("norm_step")
                var_ready = s_("var_ready")
                root_ready = s_("root_ready")
                xn_ready = s_("xn_ready")
                xnt_ready = s_("xnt_ready")
                xt_ready = s_("xt_ready")
                xt_split = s_("xt_split")
                logits = s_("logits")
                shifted = s_("shifted")
                router_exp = s_("router_exp")
                router_step = s_("router_step")
                comb_ready = s_("comb_ready")
                comb_t = s_("comb_t")
                comb_t_read = s_("comb_t_read")
                bias_sum = s_("bias_sum")
                bias_read = s_("bias_read")
                weights = [s_("weights_even"), s_("weights_odd")]
                w_split = s_("w_split")
                hidden = s_("hidden")
                hid_full = s_("hid_full")
                hid_read = s_("hid_read")
                hid_round = s_("hid_round")
                lo_ready = s_("lo_ready")
                expert_out = s_("expert_out")
                acc = s_("acc")

                h_bank = banks[0:4]
                o_bank = banks[4:6]

                def act_rounds(f):
                    return f % 2 == 0
                ROUND_D = sum(not act_rounds(f) for f in range(NF))

                def pe_first(pe, e, u, k):
                    if k == 0:
                        need(pe, w_split, (e + 1) * 4)
                    if isinstance(e, int) and e == 0:
                        pe.wait_ge(xt_split, CH + k + 1)
                    cols = slice(k * 512, (k + 1) * 512)
                    for f in range(NF):
                        j = (e * CH + k) * NF + f
                        need(pe, hid_read, j - 3)
                        bank = h_bank[(k * NF + f) % 4]
                        rows = slice(f * P, (f + 1) * P)
                        pe.matmul(bank[:], w1_hi[:, u, rows], xt_hi[:, cols], start=True, stop=False)
                        pe.matmul(bank[:], w1_lo[:, u, rows], xt_hi[:, cols], start=False, stop=False)
                        pe.matmul(bank[:], w1_hi[:, u, rows], xt_lo[:, cols], start=False, stop=True).then_inc(hidden, 1)

                def pe_second(pe, e, u, k):
                    n = e * CH + k
                    need(pe, lo_ready, (n + 1) * NF)
                    need(pe, acc, n - 1)
                    for i in range(TC):
                        dst = o_bank[k % 2][:, i * P:(i + 1) * P]
                        rows = slice(i * P, (i + 1) * P)
                        for f in range(NF):
                            pe.matmul(dst, hid_hi[:, k % 2, f, rows], w2_hi[:, u, f, :], start=(f == 0), stop=False)
                            pe.matmul(dst, hid_hi[:, k % 2, f, rows], w2_lo[:, u, f, :], start=False, stop=False)
                            mm = pe.matmul(dst, hid_lo[:, k % 2, f, rows], w2_hi[:, u, f, :], start=False, stop=(f == NF - 1))
                    mm.then_inc(expert_out, 1)

                def pe_pair(pe, t, last):
                    for u in range(2):
                        e = t * 2 + u
                        for k in range(CH):
                            if k < CH - 1:
                                pe_first(pe, e, u, k + 1)
                            elif u == 0:
                                pe_first(pe, e + 1, 1, 0)
                            elif not last:
                                pe_first(pe, e + 1, 0, 0)
                            pe_second(pe, e, u, k)

                def pe_program(pe):
                    for q in range(CH):
                        pe.wait_ge(xn_ready, q + 1)
                        if q >= 2:
                            pe.wait_ge(xt_ready, q - 1)
                            pe.wait_ge(xt_split, q - 1)
                        for i in range(TC):
                            mm = pe.transpose(banks[6 + q % 2][:, i * P:(i + 1) * P], xn[:, q * TC + i, :], ident[:])
                        mm.then_inc(xnt_ready, 1)
                    for t in range(T):
                        if t % TC == 0:
                            pe.wait_ge(xt_ready, t // TC + 1)
                        mm = pe.matmul(banks[5][:, t * E:(t + 1) * E], xt[:, t * P:(t + 1) * P], rw[:],
                                       start=True, stop=True)
                    mm.then_inc(logits, 1)
                    pe_first(pe, 0, 0, 0)
                    pe.wait_ge(comb_ready, 1)
                    for q in range(CH):
                        if q >= 2:
                            pe.wait_ge(comb_t_read, q - 1)
                        for i in range(TC):
                            mm = pe.transpose(banks[6 + q % 2][0:E, i * P:(i + 1) * P], comb[:, TC * q + i, :], ident[:])
                        mm.then_inc(comb_t, 1)
                    pe_pair(pe, 0, False)
                    for q in range(CH):
                        pe.wait_ge(comb_t_read, CH)
                        if q >= 2:
                            pe.wait_ge(bias_read, q - 1)
                        for i in range(TC):
                            t = TC * q + i
                            mm = pe.matmul(banks[6 + q % 2][:, i * P:(i + 1) * P], combT[:, t * P:(t + 1) * P], b2s[:],
                                           start=True, stop=True)
                        mm.then_inc(bias_sum, 1)
                    with pe.Fori(1, E // 2 - 1) as t:
                        pe_pair(pe, t, False)
                    pe_pair(pe, E // 2 - 1, True)

                def dve_low(dve, e, u, k):
                    n = e * CH + k
                    for f in range(NF):
                        h = hid[:, k % 2, f, :]
                        hi = hid_hi[:, k % 2, f, :]
                        if act_rounds(f):
                            need(dve, hid_read, n * NF + f + 1)
                        else:
                            need(dve, hid_full, n * NF + f + 1)
                            need(dve, expert_out, n - 1)
                            dve.tensor_copy(hi, h).then_inc(hid_round, 1)
                    for f in range(NF):
                        h = hid[:, k % 2, f, :]
                        hi = hid_hi[:, k % 2, f, :]
                        if f == 0:
                            need(dve, expert_out, n - 1)
                            need(dve, hid_round, (n + 1) * ROUND_D)
                        dve.tensor_tensor(hid_lo[:, k % 2, f, :], h, hi.bitcast(F32), ALU.subtract).then_inc(lo_ready, 1)

                def dve_acc(dve, e, u, k):
                    n = e * CH + k
                    need(dve, expert_out, n + 1)
                    if not isinstance(n, int) or n >= CH:
                        need(dve, acc, n - CH + 1)
                    for i in range(TC):
                        tile = TC * k + i
                        ins = dve.scalar_tensor_tensor(
                            out=x_tok[:, tile, :], in0=o_bank[k % 2][:, i * P:(i + 1) * P],
                            scalar=comb[:, tile, bass.ds(e, 1)], in1=x_tok[:, tile, :],
                            op0=ALU.mult, op1=ALU.add)
                    ins.then_inc(acc, 1)

                def dve_pair(dve, t, last):
                    for u in range(2):
                        e = t * 2 + u
                        for k in range(CH):
                            if k < CH - 1:
                                dve_low(dve, e, u, k + 1)
                            elif u == 0:
                                dve_low(dve, e + 1, 1, 0)
                            elif not last:
                                dve_low(dve, e + 1, 0, 0)
                            dve_acc(dve, e, u, k)

                def dve_program(dve):
                    c = Steps(dve, norm_step, 0, 2 * T + 2)
                    for t in range(T):
                        c.inc(dve.bn_stats(st[:, t, :], x_tok[:, t, :]))
                    c.wait()
                    for t in range(T):
                        c.inc(dve.bn_aggr(mv[:, t, :], st[:, t, :]))
                    c.wait()
                    c.inc(dve.tensor_scalar(ve[:], mv[:, :, 1], EPS, None, ALU.add))
                    c.wait()
                    dve.sem_inc(var_ready, 1)
                    dve.wait_ge(root_ready, 1)
                    c.inc(dve.reciprocal(rs[:], sd[:]))
                    c.wait()
                    c.close()
                    for q in range(CH):
                        for i in range(TC):
                            t = q * TC + i
                            ins = dve.tensor_scalar(xn[:, t, :], x_tok[:, t, :], mv[:, t, 0:1], rs[:, t:t + 1],
                                                    ALU.subtract, ALU.mult)
                        ins.then_inc(xn_ready, 1)
                    for q in range(CH):
                        cols = slice(q * 512, (q + 1) * 512)
                        dve.wait_ge(xt_ready, q + 1)
                        dve.tensor_copy(xt_hi[:, cols], xt[:, cols]).then_inc(xt_split, 1)
                    dve.wait_ge(xt_split, CH)
                    for q in range(CH):
                        cols = slice(q * 512, (q + 1) * 512)
                        dve.tensor_tensor(xt_lo[:, cols], xt[:, cols], xt_hi[:, cols].bitcast(F32),
                                          ALU.subtract).then_inc(xt_split, 1)
                    step = Steps(dve, router_step, 0, (12 if layer == 0 else 10) - 1 + 2 * T)
                    dve.wait_ge(logits, 1)
                    lp = banks[5][:, 0:T * E].rearrange("p (t e) -> p t e", e=E)
                    if layer == 0:
                        step.inc(dve.tensor_tensor(lg[:], lp, rb0[:].unsqueeze(1).to_broadcast([P, T, E]), ALU.add))
                    else:
                        step.inc(dve.tensor_copy(lg[:], lp))
                    step.wait()
                    step.inc(dve.tensor_reduce(mx[:], lg[:], AX.X, ALU.max))
                    step.wait()
                    step.inc(dve.tensor_tensor(lg[:], lg[:], mx[:].unsqueeze(2).to_broadcast([P, T, E]), ALU.subtract))
                    step.inc(dve.memset(pr[:, :, E:RW], 2.0))
                    step.wait()
                    dve.sem_inc(shifted, 1)
                    dve.wait_ge(router_exp, 1)
                    step.inc(dve.tensor_reduce(sm[:], pr[:, :, 0:E], AX.X, ALU.add))
                    step.wait()
                    step.inc(dve.reciprocal(mx[:], sm[:]))
                    step.wait()
                    step.inc(dve.tensor_tensor(pr[:, :, 0:E], pr[:, :, 0:E], mx[:].unsqueeze(2).to_broadcast([P, T, E]), ALU.mult))
                    step.wait()
                    for t in range(T):
                        step.inc(dve.max(top[:, t, :], pr[:, t, :]))
                    step.wait()
                    for t in range(T):
                        step.inc(dve.match_replace(out=pk[:, t, :], in_to_replace=top[:, t, :], in_values=pr[:, t, :],
                                                   imm_value=-1.0))
                    step.wait()
                    step.inc(dve.tensor_scalar(pk[:, :, 0:E], pk[:, :, 0:E], 0.0, None, ALU.is_lt))
                    step.wait()
                    step.inc(dve.tensor_tensor(comb[:], pr[:, :, 0:E], pk[:, :, 0:E], ALU.mult))
                    step.wait()
                    if layer == 0:
                        step.inc(dve.tensor_reduce(sm[:], comb[:], AX.X, ALU.add))
                        step.wait()
                        step.inc(dve.reciprocal(mx[:], sm[:]))
                        step.wait()
                        step.inc(dve.tensor_tensor(comb[:], comb[:], mx[:].unsqueeze(2).to_broadcast([P, T, E]), ALU.mult))
                        step.wait()
                    dve.sem_inc(comb_ready, 1)
                    dve_low(dve, 0, 0, 0)
                    for q in range(CH):
                        dve.wait_ge(comb_t, q + 1)
                        dve.tensor_copy(combT[:, q * 512:(q + 1) * 512], banks[6 + q % 2][0:E, :]).then_inc(comb_t_read, 1)
                    dve_pair(dve, 0, False)
                    dve.wait_ge(acc, 2 * CH)
                    for q in range(CH):
                        dve.wait_ge(bias_sum, q + 1)
                        xs = x_tok[:, TC * q:TC * (q + 1), :]
                        dve.tensor_tensor(xs, xs, banks[6 + q % 2][:].rearrange("p (t c) -> p t c", c=C),
                                          ALU.add).then_inc(bias_read, 1)
                    dve.wait_ge(bias_read, CH)
                    with dve.Fori(1, E // 2 - 1) as t:
                        dve_pair(dve, t, False)
                    dve_pair(dve, E // 2 - 1, True)
                    dve.wait_ge(acc, E * CH)

                def act_hidden(act, e, u, k):
                    n = e * CH + k
                    for f in range(NF):
                        j = n * NF + f
                        bank = h_bank[(k * NF + f) % 4]
                        bias = b1t[:, bass.ds(e * NF + f, 1)]
                        need(act, hidden, j + 1)
                        need(act, lo_ready, (n - 1) * NF)
                        apart(act, passed)
                        ins = act.activation(hid[:, k % 2, f, :], bank[:], func, bias=bias)
                        ins.then_inc(hid_full, 1)
                        if act_rounds(f):
                            need(act, expert_out, n - 1)
                            apart(act, passed)
                            act.activation(hid_hi[:, k % 2, f, :], bank[:], func, bias=bias).then_inc(hid_read, 1)
                        else:
                            need(act, hid_full, j + 1)
                            act.sem_inc(hid_read, 1)

                def act_pair(act, t):
                    for u in range(2):
                        for k in range(CH):
                            act_hidden(act, t * 2 + u, u, k)

                def act_program(act):
                    act.wait_ge(var_ready, 1)
                    act.activation(sd[:], ve[:], ACT.Sqrt).then_inc(root_ready, 1)
                    for q in range(CH):
                        act.wait_ge(xnt_ready, q + 1)
                        act.activation(xt[:, q * 512:(q + 1) * 512], banks[6 + q % 2][:], ACT.Copy).then_inc(xt_ready, 1)
                    act.wait_ge(shifted, 1)
                    act.activation(pr[:, :, 0:E], lg[:], ACT.Exp).then_inc(router_exp, 1)
                    act_pair(act, 0)
                    with act.Fori(1, E // 2) as t:
                        act_pair(act, t)

                def pool_split(pool, e, u, t):
                    need(pool, weights[u], 32 * (t + 1))
                    need(pool, expert_out, (e - 1) * CH)
                    n = e * 4
                    for step, (hi, lo, raw) in enumerate(((w1_hi[:, u, :], w1_lo[:, u, :], w1s[:, u, :]),
                                                          (w2_hi[:, u], w2_lo[:, u], w2s[:, u]))):
                        apart(pool, passed)
                        pool.tensor_copy(hi, raw).then_inc(w_split, 1)
                        need(pool, w_split, n + 2 * step + 1)
                        pool.tensor_tensor(lo, raw, hi.bitcast(F32), ALU.subtract).then_inc(w_split, 1)
                        need(pool, w_split, n + 2 * step + 2)

                with nc.Block() as block:
                    @block.sync
                    def _(sp):
                        for u in range(2):
                            sp.dma_start(w1s[:, u, :], w1d[u]).then_inc(weights[u], 16)
                            sp.dma_start(w2s[:, u, :, :], w2d[u].rearrange("(f p) c -> p f c", p=P)).then_inc(weights[u], 16)
                        with sp.Fori(0, E // 2 - 1) as t:
                            for u in range(2):
                                sp.wait_ge(w_split, (t * 2 + u + 1) * 4)
                                e = bass.ds(t * 2 + 2 + u, 1)
                                sp.dma_start(w1s[:, u, :], w1d[e].rearrange("e p i -> p (e i)")).then_inc(weights[u], 16)
                                sp.dma_start(w2s[:, u, :, :], w2d[e].rearrange("e (f p) c -> p (e f) c", p=P)).then_inc(weights[u], 16)

                    @block.tensor
                    def _(pe):
                        pe_program(pe)

                    @block.vector
                    def _(dve):
                        dve_program(dve)

                    @block.scalar
                    def _(act):
                        act_program(act)

                    @block.gpsimd
                    def _(pool):
                        for u in range(2):
                            pool_split(pool, u, u, 0)
                        with pool.Fori(1, E // 2) as t:
                            for u in range(2):
                                pool_split(pool, t * 2 + u, u, t)

        attention(0)
        experts(0)
        attention(1)
        experts(1)
        stored = sem("stored")
        with nc.Block() as block:
            @block.sync
            def _(sp):
                sp.dma_start(out.rearrange("b (t p) c -> p (b t) c", p=P), x_tok[:]).then_inc(stored, 16)
                sp.wait_ge(stored, 16)


def kernel(**inputs):
    import concourse.bacc as bacc
    from concourse.bass_utils import run_bass_kernel_spmd

    i = {k: np.ascontiguousarray(v) for k, v in inputs.items()}
    x = i["L0_attn_x"]
    C = x.shape[-1]
    H = i["L0_attn_scale"].shape[0]
    d0 = C // H
    D1 = i["L1_attn_W_attn"].shape[0] // 3 // H

    def four(w):
        return np.repeat(w.reshape(C, 4, 1, 4 * d0), 4, axis=2).reshape(C, 4, 128)

    def two(w):
        return np.repeat(w.T.reshape(C, H, 1, D1), 2, axis=2).reshape(C, H, 2 * D1)

    wqkv = i["L0_attn_w_qkv"]
    wa, ba = i["L1_attn_W_attn"], i["L1_attn_b_attn"]
    M = H * D1
    scale = i["L0_attn_scale"].reshape(4, 4)
    headrow = np.zeros((4, 4, d0, 4), np.float32)
    for j in range(4):
        headrow[:, j, :, j] = 1.0
    arrays = {
        "x": x,
        "wq0": four(wqkv[:, 0:C]), "wk0": four(wqkv[:, C:2 * C]), "wv0": wqkv[:, 2 * C:],
        "wo0": i["L0_attn_w_out"].reshape(C, 1, C), "b_out": i["L0_attn_b_out"],
        "scale_rows": np.tile(np.repeat(scale.T, d0, axis=0), (4, 1)),
        "headrow": headrow.reshape(128, 4),
        "wq1": two(wa[0:M]), "wk1": two(wa[M:2 * M]), "wv1": wa[2 * M:].T,
        "wo1": i["L1_attn_W_proj"].T.reshape(M // 128, 128, C).transpose(1, 0, 2),
        "b_proj": i["L1_attn_b_proj"], "b_v": ba[2 * M:],
        "b_qk": np.repeat(ba[0:2 * M].reshape(1, 2, H, D1), 2, axis=0).transpose(0, 3, 1, 2).reshape(2 * D1, 2, H),
        "router_w": i["L0_ffn_router_w"], "router_b": i["L0_ffn_router_b"], "w_router": i["L1_ffn_w_router"],
    }
    for n in (0, 1):
        E, _, F = i[f"L{n}_ffn_w1"].shape
        arrays[f"w1_{n}"] = i[f"L{n}_ffn_w1"]
        arrays[f"w2_{n}"] = i[f"L{n}_ffn_w2"]
        arrays[f"b1_{n}"] = i[f"L{n}_ffn_b1"].reshape(E * F // 128, 128).T
        arrays[f"b2_{n}"] = i[f"L{n}_ffn_b2"]
    arrays = {f"in_{k}": np.ascontiguousarray(v) for k, v in arrays.items()}

    nc = bacc.Bacc("TRN2", target_bir_lowering=False, num_devices=1)
    aps = {k[3:]: nc.dram_tensor(k, v.shape, mybir.dt.from_np(v.dtype), kind="ExternalInput").ap()
           for k, v in arrays.items()}
    out = nc.dram_tensor("out_x", x.shape, mybir.dt.from_np(x.dtype), kind="ExternalOutput").ap()
    build(nc, aps, out)
    r = run_bass_kernel_spmd(nc, [arrays], core_ids=[0])
    return r.results[0]["out_x"]
```

```python
import math
from contextlib import ExitStack

import numpy as np

import concourse.bass as bass
from concourse import mybir

F32 = mybir.dt.float32
F32R = mybir.dt.float32r
ALU = mybir.AluOpType
ACT = mybir.ActivationFunctionType
AX = mybir.AxisListType

P = 128
EPS = 1e-5
MASKED = 1e37
FLOOR = 1e36
TAKEN = -3e38
SENTINEL = 1e37


LEAD = 33
NCONST = 13


def apart(eng, passed):
    eng.sem_inc(passed, 1)


def lead(eng, sems):
    for sem in sems:
        eng.sem_inc(sem, LEAD)


class Steps:

    def __init__(self, it, per, before=0, per_trip=None):
        self.per, self.n = per, 0
        self.ranked, self.adj = {}, {}
        self.base = it * (per if per_trip is None else per_trip) + before

    def count(self, ins):
        self.n += 1

    def done(self, n=None):
        return self.base + (self.n if n is None else n)

    def close(self):
        assert self.n == self.per, (self.n, self.per)


def build(nc, a, out):
    B, N, C = a["x"].shape
    NT = N // P
    T = B * NT
    H = 16
    D1 = a["wv1"].shape[1] // H
    TOT = P * NT * (NT + 1) // 2
    OFF = [P * i * (i + 1) // 2 for i in range(NT)]
    SLOTS = H * NT
    E0, _, I0 = a["w1_0"].shape
    E1, _, I1 = a["w1_1"].shape

    with ExitStack() as ctx:
        def sb(name, shape, dt=F32):
            return ctx.enter_context(nc.sbuf_tensor(name, shape, dt))

        def sem(name):
            return ctx.enter_context(nc.semaphore(name))

        x_tok = sb("x_tok", [P, T, C])
        ident = sb("ident", [P, P])
        strict = sb("strict", [P, P])
        ones = sb("ones", [P, P])
        notdiag = sb("notdiag", [P, P])
        pen0 = sb("pen0", [P, N])
        rneg = sb("rneg", [P, N])
        causal = sb("causal", [P, N])
        headrow = sb("headrow", [P, 4])
        scale0 = sb("scale0", [P, 4])
        scale_in = sb("scale_in", [P, 4])
        bo0 = sb("bo0", [P, C])
        bo1 = sb("bo1", [P, C])
        bv1 = sb("bv1", [P, H * D1])
        bqk_in = sb("bqk_in", [P, 2, H])
        bqs = sb("bqs", [P, H])
        rw0 = sb("rw0", [P, E0])
        rb0 = sb("rb0", [P, E0])
        rw1 = sb("rw1", [P, E1])
        b1t0 = sb("b1t0", [P, E0 * I0 // P])
        b1t1 = sb("b1t1", [P, E1 * I1 // P])
        b2t0 = sb("b2t0", [P, E0])
        b2t1 = sb("b2t1", [P, E1])
        banks = [ctx.enter_context(nc.psum_tensor(f"bank{i}", [P, 512], F32)) for i in range(8)]

        attn_weights = [
            [sb("wq0", [P, 4, P]), sb("wk0", [P, 4, P]), sb("wv0", [P, C]), sb("wo0", [P, 1, C])],
            [sb("wq1", [P, H, P]), sb("wk1", [P, H, P]), sb("wv1", [P, H * D1]), sb("wo1", [P, H * D1 // P, C])],
        ]
        w_loaded = [sem("w_loaded0"), sem("w_loaded1")]

        def load_attention(sp, layer):
            for dst, name in zip(attn_weights[layer], ("wq", "wk", "wv", "wo")):
                sp.dma_start(dst[:], a[f"{name}{layer}"]).then_inc(w_loaded[layer], 16)

        x_loaded = sem("x_loaded")
        const_loaded = sem("const_loaded")
        scales_loaded = sem("scales_loaded")
        scales_ready = sem("scales_ready")
        consts = sem("consts")
        passed = sem("passed")
        stored = sem("stored")

        CONST_LOADS = [
            (bo0, a["b_out"].partition_broadcast(P)),
            (bo1, a["b_proj"].partition_broadcast(P)), (bv1, a["b_v"].partition_broadcast(P)),
            (rw0, a["router_w"]), (rb0, a["router_b"].partition_broadcast(P)),
            (rw1, a["w_router"]), (b1t0, a["b1_0"]), (b1t1, a["b1_1"]), (b2t0, a["b2_0"]),
            (b2t1, a["b2_1"]), (headrow, a["headrow"]),
        ]
        SCALE_LOADS = [(scale_in, a["scale_rows"]), (bqk_in, a["b_qk"])]
        with nc.Block() as block:
            @block.sync
            def _(sp):
                xd = a["x"].rearrange("b (t p) c -> p (b t) c", p=P)
                for q in range(4):
                    sp.dma_start(x_tok[:, q * T // 4:(q + 1) * T // 4, :],
                                 xd[:, q * T // 4:(q + 1) * T // 4, :]).then_inc(x_loaded, 16)

            @block.scalar
            def _(act):
                for dst, src in SCALE_LOADS:
                    act.dma_start(dst[:], src).then_inc(scales_loaded, 16)

            @block.gpsimd
            def _(pool):
                c = Steps(0, NCONST)
                for t, v in ((ident, 0.0), (strict, 1.0), (ones, 1.0), (notdiag, 1.0), (pen0, 0.0),
                             (rneg, -1.0), (causal, 0.0)):
                    c.count(pool.memset(t[:], v).then_inc(consts, 1))
                pool.wait_ge(consts, c.done())
                last = slice(N - P, N)

                def select(t, cmp, fill, base, chan, step):
                    c.count(pool.affine_select(out=t, in_=t, compare_op=cmp, fill=fill, base=base,
                                             pattern=[[step, P]], channel_multiplier=chan).then_inc(consts, 1))
                select(ident[:], ALU.not_equal, 1.0, 0, 1, -1)
                select(strict[:], ALU.is_gt, 0.0, 0, -1, 1)
                select(notdiag[:], ALU.not_equal, 0.0, 0, 1, -1)
                select(pen0[:, last], ALU.is_gt, MASKED, 0, 1, -1)
                select(rneg[:, last], ALU.is_gt, 0.0, 0, 1, -1)
                select(causal[:, last], ALU.is_ge, -MASKED, 0, 1, -1)
                pool.wait_ge(consts, c.done())
                c.close()

        def attention(layer):
            L1 = layer == 1
            with ExitStack() as at:
                def sbt(name, shape, dt=F32):
                    return at.enter_context(nc.sbuf_tensor(f"{name}{layer}", shape, dt))

                def s_(name):
                    return at.enter_context(nc.semaphore(f"{name}{layer}"))

                UNITS = H if L1 else 4
                PER = H // UNITS
                NCH = H * D1 // P if L1 else 1
                VW = D1 if L1 else 32
                AHEAD = 4
                NP = 8
                LOS = 2 if L1 else 4

                TURN = 8
                BIAS = 4
                EXP = 3
                AHEAD_U = 3 if L1 else 1
                QB = 4 if L1 else 2
                LAG = 2
                PTB = 4
                OUTS = ((3, (0, 1)), (6, (2, 3))) if L1 else ((3, (0, 1, 2, 3)),)
                V_SLOTS = (10, 14, 18, 22, 46, 50, 58, 62) if L1 else (18, 42)
                XB_SLOT = 50 if L1 else 40
                NV = len(V_SLOTS)
                NO = len(OUTS)
                GROUP = 2 * NT if L1 else SLOTS
                OEV = SLOTS // GROUP
                SUMS = 2 * NT if L1 else PER * NT
                HG = GROUP // NT
                HR = P // HG
                R_T, R_Q, R_K, R_S, R_D, R_TOP, R_PEN = 9, 10, 11, 12, 14, 16, 57

                def rank_tile(s, first, k):
                    i = 2 * (s - first) + k
                    return i if L1 and 0 <= s - first < NT // 2 else None
                NB = 3 + 2 * NT if L1 else 1

                st = sbt("st", [P, T, 6])
                mv = sbt("mv", [P, T, 2])
                ve = sbt("ve", [P, T])
                sd = sbt("sd", [P, T])
                rs = sbt("rs", [P, T])
                xn = sbt("xn", [P, NT, C])
                wq, wk, wv, wo = attn_weights[layer]
                xb_next = sbt("xb_next", [P, N])
                xb = sbt("xb", [P, N])
                q_full = sbt("q_full", [P, N])
                k_full = sbt("k_full", [P, N])
                q_hi = sbt("q_hi", [P, QB, N], F32R)
                q_lo = sbt("q_lo", [P, QB, N], F32R) if L1 else None
                k_st = sbt("k_st", [P, QB, N], F32R)
                q_head = None if L1 else sbt("q_head", [P, 2, N], F32R)
                v_st = sbt("v_st", [P, NT, H * VW])
                probs = sbt("probs", [P, NP, N])
                rowmin = sbt("rowmin", [P, NP])
                rsum = sbt("rsum", [P, 2 * SUMS])
                rinv = sbt("rinv", [P, NT, HG])
                rinv_wide = sbt("rinv_wide", [P, NT, P])
                spread_inv = sbt("spread_inv", [P, N])
                pt = sbt("pt", [P, PTB, N])
                yt = sbt("yt", [P, NCH, N])
                if L1:
                    adj = sbt("adj", [P, TOT])
                    rq_full = sbt("rq_full", [P, N])
                    rk_full = sbt("rk_full", [P, N])
                    rq_hi = sbt("rq_hi", [P, N], F32R)
                    rq_lo = sbt("rq_lo", [P, N], F32R)
                    rk_st = sbt("rk_st", [P, N], F32R)
                    rl = sbt("relu", [P, NT, N])
                    w0 = sbt("w0", [P, NT, N + 8])
                    w1 = sbt("w1", [P, NT, N + 8])
                    top = sbt("top", [P, NT, 8])
                    KEEP = max(1, int(N * 0.2)) - 1
                    PAD = -KEEP % 8
                    ROUNDS = (KEEP + PAD) // 8

                s_bank = banks[0:2]
                t_bank = banks[2:4]
                turn_bank = banks[4]
                n_bank = banks[5]
                o_bank = banks[6:8] if L1 else [banks[6]]

                preset = s_("preset")
                dve_step = s_("dve_step")
                var_ready = s_("var_ready")
                root_ready = s_("root_ready")
                xn_ready = s_("xn_ready")
                n_filled = s_("n_filled")
                n_read = s_("n_read")
                xb_ready = s_("xb_ready")
                v_proj = s_("v_proj")
                v_ready = s_("v_ready")
                q_proj = s_("q_proj")
                k_proj = s_("k_proj")
                q_copied = s_("q_copied")
                k_copied = s_("k_copied")
                q_rounded = s_("q_rounded")
                k_rounded = s_("k_rounded")
                lo_ready = s_("lo_ready")
                head_ready = s_("head_ready")
                scores = s_("scores")
                biased = s_("biased")
                exped = s_("exped")
                transposed = s_("transposed")
                pt_act = s_("pt_act")
                pt_dve = s_("pt_dve")
                pv_done = s_("pv_done")
                inverted = s_("inverted")
                widened = s_("widened")
                spread = s_("spread")
                spread_copied = s_("spread_copied")
                o_ready = s_("o_ready")
                out_proj = s_("out_proj")
                x_ready = s_("x_ready")
                rank_q = s_("rank_q")
                rank_k = s_("rank_k")
                rank_lo = s_("rank_lo")
                relu_ready = s_("relu_ready")

                def unit_at(s):
                    h, i = divmod(s, NT)
                    if i or h % PER:
                        return None
                    return h // PER + AHEAD_U

                def unit_after(s):
                    return s // NT // PER + AHEAD_U + 1

                def outs_before(b, s):
                    return (b + s // SLOTS - 1) * NO + sum(o < s % SLOTS for o, _ in OUTS)

                def values_before(b, s):
                    n = (b + s // SLOTS) * NV + NV // 2 + sum(v < s % SLOTS for v in V_SLOTS)
                    return min(n, B * NV) if isinstance(n, int) else n

                def copied_by_dve(m):
                    return not L1 and m % NT in (0, 3)

                def pt_wait(eng, b, m):
                    h, i = divmod(m, NT)
                    per = sum(copied_by_dve(j) for j in range(NT))
                    by_dve = sum(copied_by_dve(j) for j in range(i + 1))
                    if copied_by_dve(m):
                        eng.wait_ge(pt_dve, LEAD + (b * H + h) * per + by_dve)
                    else:
                        eng.wait_ge(pt_act, LEAD + (b * H + h) * (NT - per) + i + 1 - by_dve)

                def turn_free(pe, b, s):
                    pe.wait_ge(x_ready, LEAD + outs_before(b, s))
                    pe.wait_ge(v_ready, LEAD + values_before(b, s))

                def pe_q(pe, b, u):
                    if not L1 or u % UNITS == 0:
                        pe.wait_ge(xb_ready, LEAD + b + u // UNITS + 1)
                    pe.wait_ge(k_copied, LEAD + b * UNITS + u)
                    pe.matmul(turn_bank[:], wq[:, u % UNITS, :], xb[:], start=True, stop=True).then_inc(q_proj, 1)

                def pe_k(pe, b, u):
                    pe.wait_ge(q_copied, b * UNITS + u + 1)
                    pe.matmul(turn_bank[:], wk[:, u % UNITS, :], xb[:], start=True, stop=True).then_inc(k_proj, 1)

                def pe_value(pe, n, j, units):
                    pe.wait_ge(k_copied, LEAD + units)
                    pe.wait_ge(v_ready, LEAD + n * NV + j)
                    if j < NV // 2:
                        pe.wait_ge(n_read, LEAD + n * NB + 1)
                        src = xb_next
                    else:
                        pe.wait_ge(xb_ready, LEAD + n + 1)
                        src = xb
                    if L1:
                        half, kb = divmod(j, NT)
                        mm = pe.matmul(turn_bank[:], src[:, kb * P:(kb + 1) * P],
                                       wv[:, half * 512:(half + 1) * 512], start=True, stop=True)
                    else:
                        for kb in range(NT):
                            mm = pe.matmul(turn_bank[:, kb * P:(kb + 1) * P], src[:, kb * P:(kb + 1) * P],
                                           wv[:], start=True, stop=True)
                    mm.then_inc(v_proj, 1)

                def pe_out(pe, n, part):
                    _, tiles = OUTS[part]
                    pe.wait_ge(o_ready, LEAD + (n + 1) * OEV)
                    pe.wait_ge(x_ready, LEAD + n * NO + part)
                    if not (isinstance(n, int) and n == B - 1):
                        pe.wait_ge(k_copied, LEAD + n * UNITS + unit_after(SLOTS + OUTS[part][0]))
                    for i in tiles:
                        for ch in range(NCH):
                            mm = pe.matmul(turn_bank[:, i * P:(i + 1) * P], yt[:, ch, i * P:(i + 1) * P],
                                           wo[:, ch, :], start=(ch == 0), stop=(ch == NCH - 1))
                    mm.then_inc(out_proj, 1)

                def pe_next_x(pe, n):
                    pe.wait_ge(xn_ready, n + 1)
                    pe.wait_ge(n_read, LEAD + n * NB)
                    for i in range(NT):
                        mm = pe.transpose(n_bank[:, i * P:(i + 1) * P], xn[:, i, :], ident[:])
                    mm.then_inc(n_filled, 1)

                def pe_rank_unit(pe, n, k):
                    pe.wait_ge(n_read, LEAD + n * NB + k)
                    w = wq if k == 1 else wk
                    pe.matmul(n_bank[:], w[:, 0, :], xb_next[:], start=True, stop=True).then_inc(n_filled, 1)

                def pe_rank_scores(pe, n, i):
                    pe.wait_ge(n_read, LEAD + n * NB + 3 + i)
                    if i == 0:
                        pe.wait_ge(rank_lo, 2 * n + 2)
                    K, rows = P * (i + 1), slice(i * P, (i + 1) * P)
                    pe.matmul(n_bank[:, 0:K], rq_hi[:, rows], rk_st[:, 0:K], start=True, stop=False)
                    pe.matmul(n_bank[:, 0:K], rq_lo[:, rows], rk_st[:, 0:K], start=False, stop=True)\
                        .then_inc(n_filled, 1)

                def pe_decay(pe, n, i):
                    pe.wait_ge(n_read, LEAD + n * NB + 3 + NT + i)
                    pe.wait_ge(relu_ready, n * NT + i + 1)
                    diag = slice(P * i, P * (i + 1))
                    mm = pe.matmul(n_bank[:, diag], strict[:], rl[:, i, diag], start=True, stop=True)
                    if i:
                        pe.matmul(n_bank[:, 0:P * i], strict[:], rl[:, i, 0:P * i], start=True, stop=False,
                                  skip_group_check=True)
                    for r in range(i):
                        mm = pe.matmul(n_bank[:, 0:P * (r + 1)], ones[:], rl[:, r, 0:P * (r + 1)],
                                       start=False, stop=(r == i - 1), skip_group_check=True)
                    mm.then_inc(n_filled, 1)

                def pe_score(pe, b, m):
                    h, i = divmod(m, NT)
                    u = h // PER
                    K = P * (i + 1)
                    dst = s_bank[m % 2][:, 0:K]
                    rows = slice(i * P, (i + 1) * P)
                    pe.wait_ge(biased, LEAD + b * SLOTS + m - 1)
                    if i == 0:
                        pe.wait_ge(lo_ready, LEAD + b * UNITS * LOS + LOS * (u + 1))
                    if L1:
                        pe.matmul(dst, q_hi[:, u % QB, rows], k_st[:, u % QB, 0:K], start=True, stop=False)
                        mm = pe.matmul(dst, q_lo[:, u % QB, rows], k_st[:, u % QB, 0:K], start=False, stop=True)
                    else:
                        if i == 0:
                            pe.wait_ge(head_ready, b * H + h + 1)
                        mm = pe.matmul(dst, q_head[:, h % 2, rows], k_st[:, u % QB, 0:K], start=True, stop=True)
                    mm.then_inc(scores, 1)

                def pe_transpose(pe, b, s):
                    pe.wait_ge(exped, b * SLOTS + s + 1)
                    pt_wait(pe, b, s - 2)
                    for kb in range(s % NT + 1):
                        mm = pe.transpose(t_bank[s % 2][:, kb * P:(kb + 1) * P],
                                          probs[:, s % NP, kb * P:(kb + 1) * P], ident[:])
                    mm.then_inc(transposed, 1)

                def pe_spread(pe, b, n):
                    pe.wait_ge(widened, b * OEV + n + 1)
                    pe.wait_ge(spread_copied, LEAD + b * OEV + n)
                    pe.wait_ge(o_ready, LEAD + b * OEV + n)
                    bank = o_bank[(n + 1) % 2] if L1 else banks[7]
                    for i in range(NT):
                        mm = pe.transpose(bank[:, i * P:(i + 1) * P], rinv_wide[:, i, :], ident[:])
                    mm.then_inc(spread, 1)

                def pe_pv(pe, b, s):
                    h, i = divmod(s % SLOTS, NT)
                    pt_wait(pe, b, s)
                    if s % SLOTS == 0:
                        pe.wait_ge(v_ready, LEAD + (b + s // SLOTS) * NV + NV // 2)
                    if s % SLOTS == SLOTS // 2:
                        pe.wait_ge(v_ready, LEAD + (b + 1) * NV)
                    if s % GROUP == 0:
                        pe.wait_ge(o_ready, LEAD + (b * OEV + s // GROUP - (1 if L1 else 0)))
                        if L1:
                            pe.wait_ge(spread_copied, LEAD + b * OEV + s // GROUP)
                    bank = o_bank[s // GROUP % 2] if L1 else o_bank[0]
                    row = (h % 2) * D1 if L1 else 32 * (h // 4)
                    for kb in range(i + 1):
                        first = kb == 0 and (L1 or (i == 0 and h % 4 == 0))
                        last = kb == i and (L1 or h % 4 == 3)
                        mm = pe.matmul(bank[row:row + VW, i * P:(i + 1) * P],
                                       v_st[:, kb, h * VW:(h + 1) * VW],
                                       pt[:, s % PTB, kb * P:(kb + 1) * P],
                                       start=first, stop=last, skip_group_check=True)
                    mm.then_inc(pv_done, 1)

                def pe_slots(pe, b, slots, last):
                    for s in slots:
                        if s < SLOTS and not last and s >= TURN:
                            if s == R_T:
                                pe_next_x(pe, b + 1)
                            if L1 and s == R_Q:
                                pe_rank_unit(pe, b + 1, 1)
                            if L1 and s == R_K:
                                pe_rank_unit(pe, b + 1, 2)
                            if rank_tile(s, R_S, 0) is not None:
                                pe_rank_scores(pe, b + 1, rank_tile(s, R_S, 0))
                            if rank_tile(s, R_D, 0) is not None:
                                pe_decay(pe, b + 1, rank_tile(s, R_D, 0))
                        if s + AHEAD < SLOTS or not last:
                            pe_score(pe, b, s + AHEAD)
                        if 0 <= s and (s < SLOTS or not last):
                            pe_transpose(pe, b, s)
                        if s >= LAG and (s - LAG < SLOTS or not last):
                            pe_pv(pe, b, s - LAG)
                        if s >= 0 and s % GROUP == GROUP - 1 and (s < SLOTS or not last):
                            pe_spread(pe, b, s // GROUP)
                        for k, product in ((0, pe_q), (1, pe_k)):
                            u = unit_at(s - k)
                            if s >= k and u is not None and (u < UNITS or not last):
                                if k == 0:
                                    turn_free(pe, b, s)
                                product(pe, b, u)
                        if not last:
                            if rank_tile(s, R_S, 1) is not None:
                                pe_rank_scores(pe, b + 1, rank_tile(s, R_S, 1))
                            if rank_tile(s, R_D, 1) is not None:
                                pe_decay(pe, b + 1, rank_tile(s, R_D, 1))
                        if s in V_SLOTS:
                            j = V_SLOTS.index(s)
                            if j < NV // 2:
                                done = min(unit_after(s), UNITS) if last else unit_after(s)
                                pe_value(pe, b, j + NV // 2, b * UNITS + done)
                            elif not last:
                                pe_value(pe, b + 1, j - NV // 2, b * UNITS + unit_after(s))
                        for part, (o, _) in enumerate(OUTS):
                            if s == SLOTS + o:
                                pe_out(pe, b, part)

                def pe_program(pe):
                    lead(pe, (n_filled, scores, pv_done, v_proj, transposed, spread, out_proj, k_proj))
                    pe_next_x(pe, 0)
                    pe.wait_ge(w_loaded[layer], 64)
                    if L1:
                        pe_rank_unit(pe, 0, 1)
                        pe_rank_unit(pe, 0, 2)
                        for i in range(NT):
                            pe_rank_scores(pe, 0, i)
                        for i in range(NT):
                            pe_decay(pe, 0, i)
                    for u in range(unit_at(0)):
                        pe_q(pe, 0, u)
                        pe_k(pe, 0, u)
                    for j in range(NV // 2):
                        pe_value(pe, 0, j, unit_at(0))
                    pe_slots(pe, 0, range(-AHEAD, TURN), False)
                    with pe.Fori(0, B - 1) as b:
                        pe_slots(pe, b, range(TURN, SLOTS + TURN), False)
                    pe_slots(pe, B - 1, range(TURN, SLOTS + TURN), True)

                def dve_stats(dve, c, tiles):
                    t = slice(tiles[0], tiles[-1] + 1)
                    for i in tiles:
                        c.count(dve.bn_stats(st[:, i, :], x_tok[:, i, :]).then_inc(dve_step, 1))
                    dve.wait_ge(dve_step, c.done())
                    for i in tiles:
                        c.count(dve.bn_aggr(mv[:, i, :], st[:, i, :]).then_inc(dve_step, 1))
                    dve.wait_ge(dve_step, c.done())
                    dve.tensor_scalar(ve[:, t], mv[:, t, 1], EPS, None, ALU.add).then_inc(var_ready, 1)

                def dve_invert_root(dve, c, part, t):
                    dve.wait_ge(root_ready, part + 1)
                    c.count(dve.reciprocal(rs[:, t], sd[:, t]).then_inc(dve_step, 1))
                    dve.wait_ge(dve_step, c.done())

                def dve_norm(dve, n):
                    dve.wait_ge(n_filled, LEAD + (n - 1) * NB + 1)
                    for i in range(NT):
                        t = bass.ds(n * NT + i, 1)
                        ins = dve.tensor_scalar(xn[:, i, :], x_tok[:, t, :].rearrange("p a c -> p (a c)"),
                                                mv[:, t, 0:1].rearrange("p a c -> p (a c)"), rs[:, t],
                                                ALU.subtract, ALU.mult)
                    ins.then_inc(xn_ready, 1)

                def dve_relu(dve, c, n, i):
                    K = P * (i + 1)
                    dve.wait_ge(n_filled, LEAD + n * NB + 4 + i)
                    dve.scalar_tensor_tensor(out=rl[:, i, 0:K], in0=n_bank[:, 0:K], scalar=0.0,
                                             in1=rneg[:, N - K:N], op0=ALU.min, op1=ALU.mult).then_inc(n_read, 1)
                    dve.wait_ge(n_read, LEAD + n * NB + 4 + i)
                    dve.memset(rl[:, i, 0:1], 0.0).then_inc(relu_ready, 1)

                def dve_decay(dve, c, n, i):
                    K = P * (i + 1)
                    dve.wait_ge(n_filled, LEAD + n * NB + 4 + NT + i)
                    dve.scalar_tensor_tensor(out=w0[:, i, 0:K], in0=n_bank[:, 0:K], scalar=-1.0,
                                             in1=causal[:, N - K:N], op0=ALU.mult, op1=ALU.add).then_inc(n_read, 1)

                RANKING = [(r, i, take) for r in range(ROUNDS) for take in (False, True)
                           for i in range(NT)] if L1 else []

                def dve_rank(dve, c, n, r, i, take):
                    src = w0 if r == 0 else w1
                    W = P * (i + 1) + PAD
                    if r or take:
                        dve.wait_ge(dve_step, c.done(c.ranked[i]))
                    else:
                        dve.wait_ge(n_read, LEAD + n * NB + 4 + NT + i)
                    apart(dve, passed)
                    if take:
                        c.count(dve.match_replace(out=w1[:, i, 0:W], in_to_replace=top[:, i, :],
                                                  in_values=src[:, i, 0:W], imm_value=TAKEN).then_inc(dve_step, 1))
                    else:
                        c.count(dve.max(top[:, i, :], src[:, i, 0:W]).then_inc(dve_step, 1))
                    c.ranked[i] = c.n

                def dve_penalty(dve, c, i):
                    K = P * (i + 1)
                    dve.wait_ge(dve_step, c.done(c.ranked[i]))
                    c.count(dve.tensor_scalar(w1[:, i, 0:K], w1[:, i, 0:K], TAKEN / 2, MASKED,
                                              ALU.is_gt, ALU.mult).then_inc(dve_step, 1))
                    dve.wait_ge(dve_step, c.done())
                    blk = w1[:, i, P * i:P * (i + 1)]
                    c.count(dve.tensor_tensor(blk, blk, notdiag[:], ALU.mult).then_inc(dve_step, 1))
                    c.ranked[i] = c.n

                def dve_adj(dve, c, n, i):
                    K = P * (i + 1)
                    dve.wait_ge(biased, LEAD + n * SLOTS - NT + i + 1)
                    apart(dve, passed)
                    dve.wait_ge(dve_step, c.done(c.ranked[i]))
                    c.count(dve.tensor_tensor(adj[:, OFF[i]:OFF[i] + K], w1[:, i, 0:K], w0[:, i, 0:K],
                                              ALU.subtract).then_inc(dve_step, 1))
                    c.adj[i] = c.n

                RANK_STEPS = ROUNDS * 2 * NT + 3 * NT if L1 else 0

                def dve_value(dve, n, j):
                    half = j // (NV // 2)
                    dve.wait_ge(pv_done, LEAD + (n * SLOTS - (0 if half else SLOTS // 2)))
                    dve.wait_ge(v_proj, LEAD + n * NV + j + 1)
                    if L1:
                        kb = j % NT
                        cols = slice(half * 512, (half + 1) * 512)
                        dve.tensor_tensor(v_st[:, kb, cols], turn_bank[:], bv1[:, cols], ALU.add).then_inc(v_ready, 1)
                    else:
                        g = slice(2 * half, 2 * half + 2)
                        for i in range(4):
                            dst = v_st[:].rearrange("p k (g j c) -> p k g j c", g=4, j=4)[:, :, g, i, 8 * i:8 * i + 8]
                            src = turn_bank[:].rearrange("p (k g j d) -> p k g j d", k=NT, g=4, j=4)[:, :, g, i, :]
                            ins = dve.tensor_copy(dst, src)
                        ins.then_inc(v_ready, 1)

                def dve_round(dve, b, u):
                    dve.wait_ge(q_copied, b * UNITS + u + 1)
                    dve.wait_ge(scores, LEAD + b * SLOTS + (u + 1 - QB) * PER * NT)
                    dve.tensor_copy(q_hi[:, u % QB, :], q_full[:]).then_inc(q_rounded, 1)

                def dve_head(dve, b, h):
                    dve.wait_ge(lo_ready, LEAD + (b * UNITS + h // PER + 1) * LOS)
                    dve.wait_ge(scores, LEAD + b * SLOTS + (h - 1) * NT)
                    dve.tensor_scalar(q_head[:, h % 2, :], q_hi[:, h // PER % QB, :].bitcast(F32),
                                      headrow[:, h % PER:h % PER + 1], None, ALU.mult).then_inc(head_ready, 1)

                def dve_bias(dve, c, b, m):
                    K = P * (m % NT + 1)
                    k = m % NP
                    dve.wait_ge(scores, LEAD + b * SLOTS + m + 1)
                    dve.wait_ge(transposed, LEAD + b * SLOTS + m - NP + 1)
                    apart(dve, passed)
                    if L1 and m % NT in c.adj:
                        dve.wait_ge(dve_step, c.done(c.adj.pop(m % NT)))
                        apart(dve, passed)
                    bias = adj[:, OFF[m % NT]:OFF[m % NT] + K] if L1 else pen0[:, N - K:N]
                    dve.tensor_tensor_reduce(probs[:, k, 0:K], s_bank[m % 2][:, 0:K], bias, 1.0, FLOOR,
                                             ALU.add, ALU.min, rowmin[:, k:k + 1]).then_inc(biased, 1)

                def dve_copy(dve, b, s):
                    K = P * (s % NT + 1)
                    dve.wait_ge(transposed, LEAD + b * SLOTS + s + 1)
                    dve.wait_ge(pv_done, LEAD + b * SLOTS + s + 1 - PTB)
                    dve.tensor_copy(pt[:, s % PTB, 0:K], t_bank[s % 2][:, 0:K]).then_inc(pt_dve, 1)

                def dve_invert(dve, c, b, g):
                    dve.wait_ge(exped, b * SLOTS + (g + 1) * SUMS)
                    src = rsum[:, (g % 2) * SUMS:(g % 2 + 1) * SUMS]
                    if L1:
                        dve.wait_ge(spread, LEAD + b * OEV + g)
                        dst = rinv[:]
                    else:
                        dve.wait_ge(spread, LEAD + b * OEV)
                        c.count(dve.tensor_scalar(src, src, 0.5, None, ALU.max).then_inc(dve_step, 1))
                        dve.wait_ge(dve_step, c.done())
                        dst = rinv[:, :, g * PER:(g + 1) * PER]
                    dve.reciprocal(dst, src.rearrange("p (h i) -> p i h", i=NT)).then_inc(inverted, 1)
                    if (g + 1) * SUMS % GROUP == 0:
                        dve.wait_ge(inverted, LEAD + b * (SLOTS // SUMS) + g + 1)
                        dve.tensor_copy(rinv_wide[:].rearrange("p i (h r) -> p i h r", r=HR),
                                        rinv[:].unsqueeze(3).to_broadcast([P, NT, HG, HR])).then_inc(widened, 1)

                def dve_outputs(dve, b, n):
                    dve.wait_ge(pv_done, LEAD + b * SLOTS + (n + 1) * GROUP)
                    dve.wait_ge(spread_copied, LEAD + b * OEV + n + 1)
                    dve.wait_ge(out_proj, LEAD + b * NO)
                    dve.tensor_tensor(yt[:, n, :], o_bank[n % len(o_bank)][:], spread_inv[:], ALU.mult).then_inc(o_ready, 1)

                def dve_add(dve, c, n, part):
                    _, tiles = OUTS[part]
                    dve.wait_ge(out_proj, LEAD + n * NO + part + 1)
                    k = len(tiles)
                    xs = x_tok[:, bass.ds(n * NT + tiles[0], k), :]
                    o = turn_bank[:, tiles[0] * P:(tiles[-1] + 1) * P].rearrange("p (t c) -> p t c", c=C)
                    c.count(dve.tensor_tensor(xs, xs, o, ALU.add).then_inc(dve_step, 1))
                    dve.wait_ge(dve_step, c.done())
                    bo = bo1 if L1 else bo0
                    dve.tensor_tensor(xs, xs, bo[:].unsqueeze(1).to_broadcast([P, k, C]), ALU.add).then_inc(x_ready, 1)

                def dve_slots(dve, c, b, slots, last):
                    for s in slots:
                        for part, (o, _) in enumerate(OUTS):
                            if s == SLOTS + o + 1:
                                dve_add(dve, c, b, part)
                        if s + BIAS >= 0 and (s + BIAS < SLOTS or not last):
                            dve_bias(dve, c, b, s + BIAS)
                        if s == TURN and not last:
                            dve_norm(dve, b + 1)
                        u = unit_at(s - 1)
                        if not L1 and s >= 1 and u is not None and (u < UNITS or not last):
                            dve_round(dve, b, u)
                        if not L1 and s >= 0 and s % NT == 1 and (s // NT + 2 < H or not last):
                            dve_head(dve, b, s // NT + 2)
                        if s >= 0 and copied_by_dve(s) and (s < SLOTS or not last):
                            dve_copy(dve, b, s)
                        if s >= GROUP and s % GROUP == LAG:
                            dve_outputs(dve, b, s // GROUP - 1)
                        if s - 1 in V_SLOTS:
                            j = V_SLOTS.index(s - 1)
                            if j < NV // 2:
                                dve_value(dve, b, j + NV // 2)
                            elif not last:
                                dve_value(dve, b + 1, j - NV // 2)
                        if 0 <= s < SLOTS and s % SUMS == SUMS - 2:
                            dve_invert(dve, c, b, s // SUMS)
                        if s >= SLOTS and s % SUMS == SUMS - 2 and not last:
                            dve_invert(dve, c, b + 1, s % SLOTS // SUMS)
                        if not last and L1 and s >= TURN:
                            for k in range(2):
                                if rank_tile(s, R_S, k) is not None:
                                    dve_relu(dve, c, b + 1, rank_tile(s, R_S, k))
                                if rank_tile(s, R_D, k) is not None:
                                    dve_decay(dve, c, b + 1, rank_tile(s, R_D, k))
                            for k, op in enumerate(RANKING):
                                if s == R_TOP + k * (R_PEN - R_TOP) // len(RANKING):
                                    dve_rank(dve, c, b + 1, *op)
                            if 0 <= s - R_PEN < NT:
                                dve_penalty(dve, c, s - R_PEN)
                            if 0 <= s - R_PEN - 1 < NT:
                                dve_adj(dve, c, b + 1, s - R_PEN - 1)

                def dve_program(dve):
                    lead(dve, (v_ready, biased, x_ready, o_ready, inverted, pt_dve))
                    if L1:
                        for i in range(NT):
                            K = P * (i + 1)
                            dve.memset(w0[:, i, K:K + PAD], SENTINEL).then_inc(preset, 1)
                        dve.wait_ge(preset, NT)
                    else:
                        dve.memset(v_st[:], 0.0).then_inc(preset, 1)
                        dve.wait_ge(preset, 1)
                        dve.wait_ge(x_loaded, 64)
                    head = 2 * T + 2 + RANK_STEPS
                    c = Steps(0, head)
                    dve_stats(dve, c, range(NT))
                    dve_invert_root(dve, c, 0, slice(0, NT))
                    dve_norm(dve, 0)
                    dve_stats(dve, c, range(NT, T))
                    if L1:
                        for i in range(NT):
                            dve_relu(dve, c, 0, i)
                        left = {i: [op for op in RANKING if op[1] == i] for i in range(NT)}
                        last = None

                        def rank_some(count, tiles, last):
                            for _ in range(count):
                                others = [i for i in tiles if i != last and left[i]] or [i for i in tiles if left[i]]
                                last = max(others, key=lambda i: (len(left[i]), i))
                                dve_rank(dve, c, 0, *left[last].pop(0))
                            return last

                        for i, count in enumerate((4, 6, 8, 6)):
                            dve_decay(dve, c, 0, i)
                            last = rank_some(count, range(i + 1), last)
                        dve_invert_root(dve, c, 1, slice(NT, T))
                        last = rank_some(18, range(NT), last)
                        for j in range(NV // 2):
                            last = rank_some(6, range(NT), last)
                            dve_value(dve, 0, j)
                        last = rank_some(sum(len(v) for v in left.values()), range(NT), last)
                        for i in range(NT):
                            dve_penalty(dve, c, i)
                        for i in range(NT):
                            dve_adj(dve, c, 0, i)
                    else:
                        dve_invert_root(dve, c, 1, slice(NT, T))
                        for u in range(unit_at(0)):
                            dve_round(dve, 0, u)
                        dve.wait_ge(const_loaded, 16 * len(CONST_LOADS))
                        dve_head(dve, 0, 0)
                        dve_head(dve, 0, 1)
                        for j in range(NV // 2):
                            dve_value(dve, 0, j)
                    dve_slots(dve, c, 0, range(-AHEAD, TURN), False)
                    c.close()
                    tail = NO + (0 if L1 else SLOTS // SUMS)
                    per = RANK_STEPS + tail
                    slots = range(TURN, SLOTS + TURN)
                    with dve.Fori(0, B - 1) as b:
                        c = Steps(b, per, head)
                        dve_slots(dve, c, b, slots, False)
                        c.close()
                    c = Steps(B - 1, tail, head, per)
                    dve_slots(dve, c, B - 1, slots, True)
                    c.close()

                def act_root(act, part, t):
                    act.wait_ge(var_ready, part + 1)
                    act.activation(sd[:, t], ve[:, t], ACT.Sqrt).then_inc(root_ready, 1)

                def act_next_x(act, n):
                    act.wait_ge(n_filled, LEAD + n * NB + 1)
                    act.wait_ge(v_proj, LEAD + n * NV - NV // 2)
                    act.wait_ge(xb_ready, LEAD + n)
                    act.activation(xb_next[:], n_bank[:], ACT.Copy).then_inc(n_read, 1)

                def act_rank_q(act, n):
                    act.wait_ge(n_filled, LEAD + n * NB + 2)
                    act.activation(rq_full[:], n_bank[:], ACT.Identity, bias=bqs[:, 0:1],
                                   scale=-1.0 / math.sqrt(D1)).then_inc(n_read, 1)
                    act.wait_ge(n_read, LEAD + n * NB + 2)
                    act.activation(rq_hi[:], rq_full[:], ACT.Copy).then_inc(rank_q, 1)

                def act_rank_k(act, n):
                    act.wait_ge(n_filled, LEAD + n * NB + 3)
                    act.activation(rk_full[:], n_bank[:], ACT.Identity, bias=bqk_in[:, 1, 0:1]).then_inc(n_read, 1)
                    act.wait_ge(n_read, LEAD + n * NB + 3)
                    act.activation(rk_st[:], rk_full[:], ACT.Copy).then_inc(rank_k, 1)

                def act_q(act, b, u):
                    g = b * UNITS + u
                    act.wait_ge(q_proj, g + 1)
                    act.wait_ge(lo_ready, LEAD + g * LOS)
                    if L1:
                        act.activation(q_full[:], turn_bank[:], ACT.Identity, bias=bqs[:, u % UNITS:u % UNITS + 1],
                                       scale=-1.0 / math.sqrt(D1)).then_inc(q_copied, 1)
                    else:
                        act.activation(q_full[:], turn_bank[:], ACT.Copy,
                                       scale=scale0[:, u % UNITS:u % UNITS + 1]).then_inc(q_copied, 1)

                def act_k(act, b, u):
                    g = b * UNITS + u
                    act.wait_ge(k_proj, LEAD + g + 1)
                    if L1:
                        act.activation(k_full[:], turn_bank[:], ACT.Identity,
                                       bias=bqk_in[:, 1, u % UNITS:u % UNITS + 1]).then_inc(k_copied, 1)
                    else:
                        act.activation(k_full[:], turn_bank[:], ACT.Copy).then_inc(k_copied, 1)
                    act.wait_ge(k_copied, LEAD + g + 1)
                    act.wait_ge(scores, LEAD + b * SLOTS + (u + 1 - QB) * PER * NT)
                    act.activation(k_st[:, u % QB, :], k_full[:], ACT.Copy).then_inc(k_rounded, 1)

                def act_exp(act, b, m):
                    K = P * (m % NT + 1)
                    k, r = m % NP, m % (2 * SUMS)
                    act.wait_ge(biased, LEAD + b * SLOTS + m + 1)
                    if m % SUMS == 0:
                        act.wait_ge(inverted, LEAD + b * (SLOTS // SUMS) + m // SUMS - 1)
                    act.activation(probs[:, k, 0:K], probs[:, k, 0:K], ACT.Exp, bias=rowmin[:, k:k + 1],
                                   scale=-1.0, accum_out=rsum[:, r:r + 1]).then_inc(exped, 1)

                def act_copy(act, b, s):
                    K = P * (s % NT + 1)
                    act.wait_ge(transposed, LEAD + b * SLOTS + s + 1)
                    act.wait_ge(pv_done, LEAD + b * SLOTS + s + 1 - PTB)
                    act.activation(pt[:, s % PTB, 0:K], t_bank[s % 2][:, 0:K], ACT.Copy).then_inc(pt_act, 1)

                def act_spread(act, b, n):
                    act.wait_ge(spread, LEAD + b * OEV + n + 1)
                    act.wait_ge(o_ready, LEAD + b * OEV + n)
                    bank = o_bank[(n + 1) % 2] if L1 else banks[7]
                    act.activation(spread_inv[:], bank[:], ACT.Copy).then_inc(spread_copied, 1)

                def act_slots(act, b, slots, last):
                    for s in slots:
                        if not last and s >= TURN:
                            if s == R_T:
                                act_next_x(act, b + 1)
                            if L1 and s == R_Q:
                                act_rank_q(act, b + 1)
                            if L1 and s == R_K:
                                act_rank_k(act, b + 1)
                        for k, step in ((1, act_q), (2, act_k)):
                            u = unit_at(s - k)
                            if s >= k and u is not None and (u < UNITS or not last):
                                step(act, b, u)
                        if s + EXP >= 0 and (s + EXP < SLOTS or not last):
                            act_exp(act, b, s + EXP)
                        if s >= 0 and not copied_by_dve(s) and (s < SLOTS or not last):
                            act_copy(act, b, s)
                        if s >= 0 and s % GROUP == GROUP - 1 and (s < SLOTS or not last):
                            act_spread(act, b, s // GROUP)

                def act_program(act):
                    lead(act, (n_read, k_copied, pt_act, spread_copied))
                    act_root(act, 0, slice(0, NT))
                    act_next_x(act, 0)
                    if L1:
                        act_rank_q(act, 0)
                        act_rank_k(act, 0)
                    act_root(act, 1, slice(NT, T))
                    act.wait_ge(scales_ready, 2)
                    for u in range(unit_at(0)):
                        act_q(act, 0, u)
                        act_k(act, 0, u)
                    act_slots(act, 0, range(-AHEAD, TURN), False)
                    with act.Fori(0, B - 1) as b:
                        act_slots(act, b, range(TURN, SLOTS + TURN), False)
                    act_slots(act, B - 1, range(TURN, SLOTS + TURN), True)

                def pool_xb(pool, n):
                    pool.wait_ge(n_read, LEAD + n * NB + 1)
                    pool.wait_ge(k_proj, LEAD + n * UNITS)
                    pool.wait_ge(v_proj, LEAD + n * NV)
                    apart(pool, passed)
                    pool.tensor_copy(xb[:], xb_next[:]).then_inc(xb_ready, 1)
                    pool.wait_ge(xb_ready, LEAD + n + 1)

                def pool_rank_lo(pool, n):
                    pool.wait_ge(rank_q, n + 1)
                    pool.tensor_tensor(rq_lo[:], rq_full[:], rq_hi[:].bitcast(F32), ALU.subtract).then_inc(rank_lo, 1)
                    pool.wait_ge(rank_lo, 2 * n + 1)
                    pool.wait_ge(rank_k, n + 1)
                    pool.tensor_tensor(rk_st[64:P, :], rk_full[64:P, :], rk_st[64:P, :].bitcast(F32),
                                       ALU.subtract).then_inc(rank_lo, 1)
                    pool.wait_ge(rank_lo, 2 * n + 2)

                def pool_unit(pool, b, u):
                    lo = (b * UNITS + u) * LOS
                    k = u % QB
                    if L1:
                        pool.wait_ge(q_copied, b * UNITS + u + 1)
                        pool.wait_ge(scores, LEAD + b * SLOTS + (u + 1 - QB) * PER * NT)
                        apart(pool, passed)
                        pool.tensor_copy(q_hi[:, k, :], q_full[:]).then_inc(q_rounded, 1)
                    pool.wait_ge(q_rounded, b * UNITS + u + 1)
                    if L1:
                        pool.tensor_tensor(q_lo[:, k, :], q_full[:], q_hi[:, k, :].bitcast(F32),
                                           ALU.subtract).then_inc(lo_ready, 1)
                    else:
                        pool.tensor_tensor(q_hi[64:P, k, :], q_full[64:P, :], q_hi[64:P, k, :].bitcast(F32),
                                           ALU.subtract).then_inc(lo_ready, 1)
                    pool.wait_ge(k_rounded, b * UNITS + u + 1)
                    for n, rows in enumerate([slice(64, P)] if L1 else [slice(32, 64), slice(96, P)]):
                        pool.wait_ge(lo_ready, LEAD + lo + n + 1)
                        pool.tensor_tensor(k_st[rows, k, :], k_full[rows, :], k_st[rows, k, :].bitcast(F32),
                                           ALU.subtract).then_inc(lo_ready, 1 + n)
                    pool.wait_ge(lo_ready, LEAD + lo + LOS)

                def pool_slots(pool, b, slots, last):
                    for s in slots:
                        if not last and s >= TURN:
                            if L1 and s == R_K:
                                pool_rank_lo(pool, b + 1)
                            if s == XB_SLOT:
                                pool_xb(pool, b + 1)
                        u = unit_at(s)
                        if s >= 0 and u is not None and (u < UNITS or not last):
                            pool_unit(pool, b, u)

                def pool_program(pool):
                    lead(pool, (xb_ready, lo_ready))
                    if not L1:
                        pool.wait_ge(scales_loaded, 16 * len(SCALE_LOADS))
                        pool.tensor_scalar(scale0[:], scale_in[:], -1.0, None, ALU.mult).then_inc(scales_ready, 1)
                        pool.wait_ge(scales_ready, 1)
                        pool.tensor_scalar(bqs[:], bqk_in[:, 0, :], -1.0 / math.sqrt(D1), None,
                                           ALU.mult).then_inc(scales_ready, 1)
                        pool.wait_ge(scales_ready, 2)
                    pool_xb(pool, 0)
                    if L1:
                        pool_rank_lo(pool, 0)
                    for u in range(unit_at(0)):
                        pool_unit(pool, 0, u)
                    pool_slots(pool, 0, range(0, TURN), False)
                    with pool.Fori(0, B - 1) as b:
                        pool_slots(pool, b, range(TURN, SLOTS + TURN), False)
                    pool_slots(pool, B - 1, range(TURN, SLOTS + TURN), True)

                with nc.Block() as block:
                    @block.sync
                    def _(sp):
                        if not L1:
                            load_attention(sp, 0)
                            for dst, src in CONST_LOADS:
                                sp.dma_start(dst[:], src).then_inc(const_loaded, 16)

                    @block.tensor
                    def _(pe):
                        pe_program(pe)

                    @block.vector
                    def _(dve):
                        dve_program(dve)

                    @block.scalar
                    def _(act):
                        act_program(act)

                    @block.gpsimd
                    def _(pool):
                        pool_program(pool)

        def experts(layer):
            E, I, TOPK = (E0, I0, 4) if layer == 0 else (E1, I1, 1)
            rw = rw0 if layer == 0 else rw1
            b1t = b1t0 if layer == 0 else b1t1
            b2t = b2t0 if layer == 0 else b2t1
            func = ACT.Gelu if layer == 0 else ACT.Relu
            NF = I // P
            HB = 4 if layer == 0 else 2
            LOOK = HB // 2
            PADW = 8 - TOPK
            RW = E + PADW
            CH = T * P // 512
            TC = T // CH
            w1d, w2d = a[f"w1_{layer}"], a[f"w2_{layer}"]
            with ExitStack() as at:
                def sbt(name, shape, dt=F32):
                    return at.enter_context(nc.sbuf_tensor(f"m{layer}_{name}", shape, dt))

                def s_(name):
                    return at.enter_context(nc.semaphore(f"m{layer}_{name}"))

                st = sbt("st", [P, T, 6])
                mv = sbt("mv", [P, T, 2])
                ve = sbt("ve", [P, T])
                sd = sbt("sd", [P, T])
                rs = sbt("rs", [P, T])
                xn = sbt("xn", [P, T, C])
                xt = sbt("xt", [P, T * P])
                xt_hi = sbt("xt_hi", [P, T * P], F32R)
                xt_lo = sbt("xt_lo", [P, T * P], F32R)
                lg = sbt("lg", [P, T, E])
                mx = sbt("mx", [P, T])
                pr = sbt("pr", [P, T, RW])
                pk = sbt("pk", [P, T, RW])
                top = sbt("top", [P, T, 8])
                sm = sbt("sm", [P, T])
                comb = sbt("comb", [P, T, E])
                y = sbt("y", [P, 2, 512])
                w1s = sbt("w1s", [P, 2, I])
                w2s = sbt("w2s", [P, 2, NF, C])
                w1_hi = sbt("w1_hi", [P, 2, I], F32R)
                w1_lo = sbt("w1_lo", [P, 2, I], F32R)
                w2_hi = sbt("w2_hi", [P, 2, NF, C], F32R)
                w2_lo = sbt("w2_lo", [P, 2, NF, C], F32R)
                hid = sbt("hid", [P, HB, NF, 512])
                hid_hi = sbt("hid_hi", [P, HB, NF, 512], F32R)
                hid_lo = sbt("hid_lo", [P, HB, NF, 512], F32R)

                norm_step = s_("norm_step")
                var_ready = s_("var_ready")
                root_ready = s_("root_ready")
                xn_ready = s_("xn_ready")
                xnt_ready = s_("xnt_ready")
                xt_ready = s_("xt_ready")
                xt_split = s_("xt_split")
                logits = s_("logits")
                shifted = s_("shifted")
                router_exp = s_("router_exp")
                router_step = s_("router_step")
                weights = [s_("weights_even"), s_("weights_odd")]
                w_split = s_("w_split")
                hidden = s_("hidden")
                hid_full = s_("hid_full")
                hid_read = s_("hid_read")
                hid_round = s_("hid_round")
                lo_ready = s_("lo_ready")
                expert_out = s_("expert_out")
                y_ready = s_("y_ready")
                y_back = s_("y_back")
                acc = s_("acc")

                h_bank = banks[0:4]
                o_bank = banks[4:6]
                back_bank = banks[6:8]

                def act_rounds(f):
                    return f % 2 == 0
                ROUND_D = sum(not act_rounds(f) for f in range(NF))

                def pe_first(pe, e, u, k):
                    if k == 0:
                        pe.wait_ge(w_split, (e + 1) * 4)
                    if isinstance(e, int) and e == 0:
                        pe.wait_ge(xt_split, 2 * k + 2)
                    cols = slice(k * 512, (k + 1) * 512)
                    for f in range(NF):
                        j = (e * CH + k) * NF + f
                        pe.wait_ge(hid_read, LEAD + j - 3)
                        bank = h_bank[(k * NF + f) % 4]
                        rows = slice(f * P, (f + 1) * P)
                        pe.matmul(bank[:], w1_hi[:, u, rows], xt_hi[:, cols], start=True, stop=False)
                        pe.matmul(bank[:], w1_lo[:, u, rows], xt_hi[:, cols], start=False, stop=False)
                        pe.matmul(bank[:], w1_hi[:, u, rows], xt_lo[:, cols], start=False, stop=True).then_inc(hidden, 1)

                def pe_second(pe, e, u, k):
                    n = e * CH + k
                    pe.wait_ge(lo_ready, LEAD + (n + 1) * NF)
                    pe.wait_ge(y_ready, LEAD + n - 1)
                    dst = o_bank[k % 2][:]
                    for f in range(NF):
                        pe.matmul(dst, w2_hi[:, u, f, :], hid_hi[:, k % HB, f, :], start=(f == 0), stop=False)
                        pe.matmul(dst, w2_lo[:, u, f, :], hid_hi[:, k % HB, f, :], start=False, stop=False)
                        mm = pe.matmul(dst, w2_hi[:, u, f, :], hid_lo[:, k % HB, f, :], start=False, stop=(f == NF - 1))
                    mm.then_inc(expert_out, 1)

                def pe_back(pe, e, k):
                    n = e * CH + k
                    pe.wait_ge(y_ready, LEAD + n + 1)
                    pe.wait_ge(acc, LEAD + n - 1)
                    for i in range(TC):
                        cols = slice(i * P, (i + 1) * P)
                        mm = pe.transpose(back_bank[k % 2][:, cols], y[:, k % 2, cols], ident[:])
                    mm.then_inc(y_back, 1)

                def later(e, u, k):
                    return (e, u, k + LOOK) if k + LOOK < CH else (e + 1, 1 - u, k + LOOK - CH)

                def before(e, k):
                    return (e, k - 1) if k else (e - 1, CH - 1)

                def pe_pair(pe, t, last):
                    for u in range(2):
                        e = t * 2 + u
                        for k in range(CH):
                            if k + LOOK < CH or u == 0 or not last:
                                pe_first(pe, *later(e, u, k))
                            pe_second(pe, e, u, k)
                            if k or u or not isinstance(t, int) or t:
                                pe_back(pe, *before(e, k))
                    if last:
                        pe_back(pe, e, CH - 1)

                def pe_program(pe):
                    lead(pe, (expert_out, y_back))
                    for q in range(CH + 1):
                        if q < CH:
                            pe.wait_ge(xn_ready, q + 1)
                            if q >= 2:
                                pe.wait_ge(xt_ready, q - 1)
                            for i in range(TC):
                                mm = pe.transpose(banks[6 + q % 2][:, i * P:(i + 1) * P], xn[:, q * TC + i, :], ident[:])
                            mm.then_inc(xnt_ready, 1)
                        if q >= 1:
                            pe.wait_ge(xt_ready, q)
                            for t in range((q - 1) * TC, q * TC):
                                mm = pe.matmul(banks[5][:, t * E:(t + 1) * E], xt[:, t * P:(t + 1) * P], rw[:],
                                               start=True, stop=True)
                    mm.then_inc(logits, 1)
                    for k in range(LOOK):
                        pe_first(pe, 0, 0, k)
                    pe_pair(pe, 0, False)
                    with pe.Fori(1, E // 2 - 1) as t:
                        pe_pair(pe, t, False)
                    pe_pair(pe, E // 2 - 1, True)

                def dve_low(dve, e, u, k):
                    n = e * CH + k
                    for f in range(NF):
                        h = hid[:, k % HB, f, :]
                        hi = hid_hi[:, k % HB, f, :]
                        if act_rounds(f):
                            dve.wait_ge(hid_read, LEAD + n * NF + f + 1)
                        else:
                            dve.wait_ge(hid_full, n * NF + f + 1)
                            dve.wait_ge(expert_out, LEAD + n + 1 - HB)
                            dve.tensor_copy(hi, h).then_inc(hid_round, 1)
                    for f in range(NF):
                        h = hid[:, k % HB, f, :]
                        hi = hid_hi[:, k % HB, f, :]
                        if f == 0:
                            dve.wait_ge(expert_out, LEAD + n + 1 - HB)
                            dve.wait_ge(hid_round, (n + 1) * ROUND_D)
                        dve.tensor_tensor(hid_lo[:, k % HB, f, :], h, hi.bitcast(F32), ALU.subtract).then_inc(lo_ready, 1)

                def dve_acc(dve, e, k):
                    n = e * CH + k
                    dve.wait_ge(y_back, LEAD + n + 1)
                    if not isinstance(n, int) or n >= CH:
                        dve.wait_ge(acc, LEAD + n - CH + 1)
                    for i in range(TC):
                        tile = TC * k + i
                        ins = dve.scalar_tensor_tensor(
                            out=x_tok[:, tile, :], in0=back_bank[k % 2][:, i * P:(i + 1) * P],
                            scalar=comb[:, tile, bass.ds(e, 1)], in1=x_tok[:, tile, :],
                            op0=ALU.mult, op1=ALU.add)
                    ins.then_inc(acc, 1)

                def dve_pair(dve, t, last):
                    for u in range(2):
                        e = t * 2 + u
                        for k in range(CH):
                            if k + LOOK < CH or u == 0 or not last:
                                dve_low(dve, *later(e, u, k))
                            if k or u or not isinstance(t, int) or t:
                                dve_acc(dve, *before(e, k))
                    if last:
                        dve_acc(dve, e, CH - 1)

                def dve_stats(dve, c, q):
                    tiles = range(q * TC, (q + 1) * TC)
                    for t in tiles:
                        c.count(dve.bn_stats(st[:, t, :], x_tok[:, t, :]).then_inc(norm_step, 1))
                    dve.wait_ge(norm_step, c.done())
                    for t in tiles:
                        c.count(dve.bn_aggr(mv[:, t, :], st[:, t, :]).then_inc(norm_step, 1))
                    dve.wait_ge(norm_step, c.done())
                    ts = slice(tiles[0], tiles[-1] + 1)
                    dve.tensor_scalar(ve[:, ts], mv[:, ts, 1], EPS, None, ALU.add).then_inc(var_ready, 1)

                def dve_norm(dve, c, q):
                    tiles = range(q * TC, (q + 1) * TC)
                    ts = slice(tiles[0], tiles[-1] + 1)
                    dve.wait_ge(root_ready, q + 1)
                    c.count(dve.reciprocal(rs[:, ts], sd[:, ts]).then_inc(norm_step, 1))
                    dve.wait_ge(norm_step, c.done())
                    for t in tiles:
                        ins = dve.tensor_scalar(xn[:, t, :], x_tok[:, t, :], mv[:, t, 0:1], rs[:, t:t + 1],
                                                ALU.subtract, ALU.mult)
                    ins.then_inc(xn_ready, 1)

                def dve_split(dve, q):
                    cols = slice(q * 512, (q + 1) * 512)
                    dve.wait_ge(xt_ready, q + 1)
                    dve.tensor_copy(xt_hi[:, cols], xt[:, cols]).then_inc(xt_split, 1)
                    dve.wait_ge(xt_split, 2 * q + 1)
                    dve.tensor_tensor(xt_lo[:, cols], xt[:, cols], xt_hi[:, cols].bitcast(F32),
                                      ALU.subtract).then_inc(xt_split, 1)

                def dve_program(dve):
                    lead(dve, (lo_ready, acc))
                    c = Steps(0, 2 * T + CH)
                    for q in range(CH + 2):
                        if q < CH:
                            dve_stats(dve, c, q)
                        if 1 <= q <= CH:
                            dve_norm(dve, c, q - 1)
                        if q >= 2:
                            dve_split(dve, q - 2)
                    c.close()
                    step = Steps(0, (12 if layer == 0 else 10) - 1 + 2 * T)
                    dve.wait_ge(logits, 1)
                    lp = banks[5][:, 0:T * E].rearrange("p (t e) -> p t e", e=E)
                    if layer == 0:
                        step.count(dve.tensor_tensor(lg[:], lp, rb0[:].unsqueeze(1).to_broadcast([P, T, E]), ALU.add).then_inc(router_step, 1))
                    else:
                        step.count(dve.tensor_copy(lg[:], lp).then_inc(router_step, 1))
                    dve.wait_ge(router_step, step.done())
                    step.count(dve.tensor_reduce(mx[:], lg[:], AX.X, ALU.max).then_inc(router_step, 1))
                    dve.wait_ge(router_step, step.done())
                    step.count(dve.tensor_tensor(lg[:], lg[:], mx[:].unsqueeze(2).to_broadcast([P, T, E]), ALU.subtract).then_inc(router_step, 1))
                    step.count(dve.memset(pr[:, :, E:RW], 2.0).then_inc(router_step, 1))
                    dve.wait_ge(router_step, step.done())
                    dve.sem_inc(shifted, 1)
                    dve.wait_ge(router_exp, 1)
                    step.count(dve.tensor_reduce(sm[:], pr[:, :, 0:E], AX.X, ALU.add).then_inc(router_step, 1))
                    dve.wait_ge(router_step, step.done())
                    step.count(dve.reciprocal(mx[:], sm[:]).then_inc(router_step, 1))
                    dve.wait_ge(router_step, step.done())
                    step.count(dve.tensor_tensor(pr[:, :, 0:E], pr[:, :, 0:E], mx[:].unsqueeze(2).to_broadcast([P, T, E]), ALU.mult).then_inc(router_step, 1))
                    dve.wait_ge(router_step, step.done())
                    for t in range(T):
                        step.count(dve.max(top[:, t, :], pr[:, t, :]).then_inc(router_step, 1))
                    dve.wait_ge(router_step, step.done())
                    for t in range(T):
                        step.count(dve.match_replace(out=pk[:, t, :], in_to_replace=top[:, t, :], in_values=pr[:, t, :],
                                                   imm_value=-1.0).then_inc(router_step, 1))
                    dve.wait_ge(router_step, step.done())
                    for k in range(LOOK):
                        dve_low(dve, 0, 0, k)
                    step.count(dve.tensor_scalar(pk[:, :, 0:E], pk[:, :, 0:E], 0.0, None, ALU.is_lt).then_inc(router_step, 1))
                    dve.wait_ge(router_step, step.done())
                    step.count(dve.tensor_tensor(comb[:], pr[:, :, 0:E], pk[:, :, 0:E], ALU.mult).then_inc(router_step, 1))
                    dve.wait_ge(router_step, step.done())
                    if layer == 0:
                        step.count(dve.tensor_reduce(sm[:], comb[:], AX.X, ALU.add).then_inc(router_step, 1))
                        dve.wait_ge(router_step, step.done())
                        step.count(dve.reciprocal(mx[:], sm[:]).then_inc(router_step, 1))
                        dve.wait_ge(router_step, step.done())
                        step.count(dve.tensor_tensor(comb[:], comb[:], mx[:].unsqueeze(2).to_broadcast([P, T, E]), ALU.mult).then_inc(router_step, 1))
                        dve.wait_ge(router_step, step.done())
                    dve_pair(dve, 0, False)
                    with dve.Fori(1, E // 2 - 1) as t:
                        dve_pair(dve, t, False)
                    dve_pair(dve, E // 2 - 1, True)
                    dve.wait_ge(acc, LEAD + E * CH)

                def act_hidden(act, e, u, k):
                    n = e * CH + k
                    for f in range(NF):
                        j = n * NF + f
                        bank = h_bank[(k * NF + f) % 4]
                        bias = b1t[:, bass.ds(e * NF + f, 1)]
                        act.wait_ge(hidden, j + 1)
                        act.wait_ge(lo_ready, LEAD + (n + 1 - HB) * NF)
                        apart(act, passed)
                        ins = act.activation(hid[:, k % HB, f, :], bank[:], func, bias=bias)
                        ins.then_inc(hid_full, 1)
                        if act_rounds(f):
                            act.wait_ge(expert_out, LEAD + n + 1 - HB)
                            apart(act, passed)
                            act.activation(hid_hi[:, k % HB, f, :], bank[:], func, bias=bias).then_inc(hid_read, 1)
                        else:
                            act.wait_ge(hid_full, j + 1)
                            act.sem_inc(hid_read, 1)

                def act_out(act, e, k):
                    n = e * CH + k
                    act.wait_ge(expert_out, LEAD + n + 1)
                    act.wait_ge(y_back, LEAD + n - 1)
                    apart(act, passed)
                    act.activation(y[:, k % 2, :], o_bank[k % 2][:], ACT.Identity,
                                   bias=b2t[:, bass.ds(e, 1)]).then_inc(y_ready, 1)

                def act_pair(act, t, last):
                    for u in range(2):
                        e = t * 2 + u
                        for k in range(CH):
                            if k + LOOK < CH or u == 0 or not last:
                                act_hidden(act, *later(e, u, k))
                            act_out(act, e, k)

                def act_program(act):
                    lead(act, (hid_read, y_ready))
                    for q in range(CH + 2):
                        if q < CH:
                            ts = slice(q * TC, (q + 1) * TC)
                            act.wait_ge(var_ready, q + 1)
                            act.activation(sd[:, ts], ve[:, ts], ACT.Sqrt).then_inc(root_ready, 1)
                        if q >= 2:
                            p = q - 2
                            act.wait_ge(xnt_ready, p + 1)
                            act.activation(xt[:, p * 512:(p + 1) * 512], banks[6 + p % 2][:],
                                           ACT.Copy).then_inc(xt_ready, 1)
                    act.wait_ge(shifted, 1)
                    act.activation(pr[:, :, 0:E], lg[:], ACT.Exp).then_inc(router_exp, 1)
                    for k in range(LOOK):
                        act_hidden(act, 0, 0, k)
                    act_pair(act, 0, False)
                    with act.Fori(1, E // 2 - 1) as t:
                        act_pair(act, t, False)
                    act_pair(act, E // 2 - 1, True)

                def pool_split(pool, e, u, t):
                    pool.wait_ge(weights[u], 32 * (t + 1))
                    pool.wait_ge(expert_out, LEAD + (e - 1) * CH)
                    n = e * 4
                    for step, (hi, lo, raw) in enumerate(((w1_hi[:, u, :], w1_lo[:, u, :], w1s[:, u, :]),
                                                          (w2_hi[:, u], w2_lo[:, u], w2s[:, u]))):
                        apart(pool, passed)
                        pool.tensor_copy(hi, raw).then_inc(w_split, 1)
                        pool.wait_ge(w_split, n + 2 * step + 1)
                        pool.tensor_tensor(lo, raw, hi.bitcast(F32), ALU.subtract).then_inc(w_split, 1)
                        pool.wait_ge(w_split, n + 2 * step + 2)

                with nc.Block() as block:
                    @block.sync
                    def _(sp):
                        for u in range(2):
                            sp.dma_start(w1s[:, u, :], w1d[u]).then_inc(weights[u], 16)
                            sp.dma_start(w2s[:, u, :, :], w2d[u].rearrange("(f p) c -> p f c", p=P)).then_inc(weights[u], 16)
                        if layer == 0:
                            load_attention(sp, 1)
                        with sp.Fori(0, E // 2 - 1) as t:
                            for u in range(2):
                                sp.wait_ge(w_split, (t * 2 + u + 1) * 4)
                                e = bass.ds(t * 2 + 2 + u, 1)
                                sp.dma_start(w1s[:, u, :], w1d[e].rearrange("e p i -> p (e i)")).then_inc(weights[u], 16)
                                sp.dma_start(w2s[:, u, :, :], w2d[e].rearrange("e (f p) c -> p (e f) c", p=P)).then_inc(weights[u], 16)

                        if layer == 1:
                            od = out.rearrange("b (t p) c -> p (b t) c", p=P)
                            for k in range(CH):
                                sp.wait_ge(acc, LEAD + (E - 1) * CH + k + 1)
                                tiles = slice(k * TC, (k + 1) * TC)
                                sp.dma_start(od[:, tiles, :], x_tok[:, tiles, :]).then_inc(stored, 16)
                            sp.wait_ge(stored, 16 * CH)

                    @block.tensor
                    def _(pe):
                        pe_program(pe)

                    @block.vector
                    def _(dve):
                        dve_program(dve)

                    @block.scalar
                    def _(act):
                        act_program(act)

                    @block.gpsimd
                    def _(pool):
                        for u in range(2):
                            pool_split(pool, u, u, 0)
                        with pool.Fori(1, E // 2) as t:
                            for u in range(2):
                                pool_split(pool, t * 2 + u, u, t)

        attention(0)
        experts(0)
        attention(1)
        experts(1)


def kernel(**inputs):
    import concourse.bacc as bacc
    from concourse.bass_utils import run_bass_kernel_spmd

    i = {k: np.ascontiguousarray(v) for k, v in inputs.items()}
    x = i["L0_attn_x"]
    C = x.shape[-1]
    H = i["L0_attn_scale"].shape[0]
    d0 = C // H
    D1 = i["L1_attn_W_attn"].shape[0] // 3 // H

    def four(w):
        return np.repeat(w.reshape(C, 4, 1, 4 * d0), 4, axis=2).reshape(C, 4, 128)

    def two(w):
        return np.repeat(w.T.reshape(C, H, 1, D1), 2, axis=2).reshape(C, H, 2 * D1)

    wqkv = i["L0_attn_w_qkv"]
    wa, ba = i["L1_attn_W_attn"], i["L1_attn_b_attn"]
    M = H * D1
    scale = i["L0_attn_scale"].reshape(4, 4)
    headrow = np.zeros((4, 4, d0, 4), np.float32)
    for j in range(4):
        headrow[:, j, :, j] = 1.0
    arrays = {
        "x": x,
        "wq0": four(wqkv[:, 0:C]), "wk0": four(wqkv[:, C:2 * C]), "wv0": wqkv[:, 2 * C:],
        "wo0": i["L0_attn_w_out"].reshape(C, 1, C), "b_out": i["L0_attn_b_out"],
        "scale_rows": np.tile(np.repeat(scale.T, d0, axis=0), (4, 1)),
        "headrow": headrow.reshape(128, 4),
        "wq1": two(wa[0:M]), "wk1": two(wa[M:2 * M]), "wv1": wa[2 * M:].T,
        "wo1": i["L1_attn_W_proj"].T.reshape(M // 128, 128, C).transpose(1, 0, 2),
        "b_proj": i["L1_attn_b_proj"], "b_v": ba[2 * M:],
        "b_qk": np.repeat(ba[0:2 * M].reshape(1, 2, H, D1), 2, axis=0).transpose(0, 3, 1, 2).reshape(2 * D1, 2, H),
        "router_w": i["L0_ffn_router_w"], "router_b": i["L0_ffn_router_b"], "w_router": i["L1_ffn_w_router"],
    }
    for n in (0, 1):
        E, _, F = i[f"L{n}_ffn_w1"].shape
        arrays[f"w1_{n}"] = i[f"L{n}_ffn_w1"]
        arrays[f"w2_{n}"] = i[f"L{n}_ffn_w2"]
        arrays[f"b1_{n}"] = i[f"L{n}_ffn_b1"].reshape(E * F // 128, 128).T
        arrays[f"b2_{n}"] = i[f"L{n}_ffn_b2"].T
    arrays = {f"in_{k}": np.ascontiguousarray(v) for k, v in arrays.items()}

    nc = bacc.Bacc("TRN2", target_bir_lowering=False, num_devices=1)
    aps = {k[3:]: nc.dram_tensor(k, v.shape, mybir.dt.from_np(v.dtype), kind="ExternalInput").ap()
           for k, v in arrays.items()}
    out = nc.dram_tensor("out_x", x.shape, mybir.dt.from_np(x.dtype), kind="ExternalOutput").ap()
    build(nc, aps, out)
    r = run_bass_kernel_spmd(nc, [arrays], core_ids=[0])
    return r.results[0]["out_x"]
```
